# Optimizing a Trainium2 kernel written in Bass

```python
import numpy as np
import jax
import jax.numpy as jnp

def _softmax(x, axis=-1):
    return jax.nn.softmax(x, axis=axis)

def _gelu(x):
    return jax.nn.gelu(x, approximate=True)

def _silu(x):
    return jax.nn.silu(x)

def _sigmoid(x):
    return jax.nn.sigmoid(x)

def _layernorm(x, axis=-1, eps=1e-05):
    m = jnp.mean(x, axis=axis, keepdims=True)
    v = jnp.var(x, axis=axis, keepdims=True)
    return (x - m) / jnp.sqrt(v + eps)

def _scatter_add(tgt, idx, src, axis=0):
    return tgt.at[idx].add(src)

def _segment_sum(src, seg, n):
    return jax.ops.segment_sum(src, seg, n)
kernel_name = 'mk_seq_preln_d1_jaxref_r4_48a84e'

def setup_inputs(seed: int=0):
    np.random.seed(seed)
    _w = jnp.asarray

    def _L0_attn_setup():
        import jax, jax.numpy as jnp
        import numpy as np
        B, N, E = (2, 512, 256)
        H = 16
        BM = 32
        BN = 32
        BUDGET = 0.2

        def _forward(x, W_Q, W_K, W_V, W_O):
            Bx, Nx, Ex = x.shape
            D = Ex // H
            Tr, Tc = (Nx // BM, Nx // BN)
            k = max(1, int(BUDGET * Tc))

            def heads(t):
                return t.reshape(Bx, Nx, H, D).transpose(0, 2, 1, 3)
            Q = heads(x @ W_Q)
            K = heads(x @ W_K)
            V = heads(x @ W_V)
            Qp = Q.reshape(Bx, H, Tr, BM, D).mean(axis=3)
            Kp = K.reshape(Bx, H, Tc, BN, D).mean(axis=3)
            avg_sc = jnp.einsum('bhid,bhjd->bhij', Qp, Kp).mean(axis=(0, 1))
            _, idx = jax.lax.top_k(avg_sc, k)
            Kb = K.reshape(Bx, H, Tc, BN, D)
            Vb = V.reshape(Bx, H, Tc, BN, D)
            Ksel = Kb[:, :, idx]
            Vsel = Vb[:, :, idx]
            Qb = Q.reshape(Bx, H, Tr, BM, D)
            scale = 1.0 / jnp.sqrt(jnp.asarray(D, jnp.float32))
            logits = jnp.einsum('bhtqd,bhtknd->bhtqkn', Qb, Ksel).reshape(Bx, H, Tr, BM, k * BN) * scale
            P = jax.nn.softmax(logits, axis=-1)
            Ob = jnp.einsum('bhtqs,bhtsd->bhtqd', P, Vsel.reshape(Bx, H, Tr, k * BN, D))
            O = Ob.reshape(Bx, H, Nx, D).transpose(0, 2, 1, 3).reshape(Bx, Nx, Ex)
            return O @ W_O
        key = jax.random.key(seed)
        ks = jax.random.split(key, 5)
        w = lambda k: jax.random.normal(k, (E, E), jnp.float32) * 0.02
        return {'x': jax.random.normal(ks[0], (B, N, E), jnp.float32), 'W_Q': w(ks[1]), 'W_K': w(ks[2]), 'W_V': w(ks[3]), 'W_O': w(ks[4])}
    _L0_attn_in = _L0_attn_setup()

    def _L0_ffn_setup():
        import jax, jax.numpy as jnp
        import numpy as np
        B, S, D, E, F = (4, 512, 256, 8, 1024)
        key = jax.random.key(seed)
        k0, k1, k2, k3 = jax.random.split(key, 4)
        x = jax.random.normal(k0, (B, S, D), dtype=jnp.float32)
        wg = jax.random.normal(k1, (D, E), dtype=jnp.float32) * 0.02
        w_gate = jax.random.normal(k2, (E, D, F), dtype=jnp.float32) * 0.02
        w_down = jax.random.normal(k3, (E, F, D), dtype=jnp.float32) * 0.02
        return {'x': x, 'wg': wg, 'w_gate': w_gate, 'w_down': w_down}
    _L0_ffn_in = _L0_ffn_setup()
    _d = {'L0_attn_x': _L0_attn_in['x'], 'L0_attn_W_Q': _L0_attn_in['W_Q'], 'L0_attn_W_K': _L0_attn_in['W_K'], 'L0_attn_W_V': _L0_attn_in['W_V'], 'L0_attn_W_O': _L0_attn_in['W_O'], 'L0_ffn_wg': _L0_ffn_in['wg'], 'L0_ffn_w_gate': _L0_ffn_in['w_gate'], 'L0_ffn_w_down': _L0_ffn_in['w_down']}
    _x0 = _d['L0_attn_x']
    _d['L0_attn_x'] = jax.random.normal(jax.random.fold_in(jax.random.key(seed), 1), (4, 1024, 256), dtype=_x0.dtype)
    del _x0
    return _d

def reference(L0_attn_x, L0_attn_W_Q, L0_attn_W_K, L0_attn_W_V, L0_attn_W_O, L0_ffn_wg, L0_ffn_w_gate, L0_ffn_w_down):

    def _L0_attn_ref(x, W_Q, W_K, W_V, W_O):
        import jax, jax.numpy as jnp
        import numpy as np
        B, N, E = (2, 512, 256)
        H = 16
        BM = 32
        BN = 32
        BUDGET = 0.2

        def _forward(x, W_Q, W_K, W_V, W_O):
            Bx, Nx, Ex = x.shape
            D = Ex // H
            Tr, Tc = (Nx // BM, Nx // BN)
            k = max(1, int(BUDGET * Tc))

            def heads(t):
                return t.reshape(Bx, Nx, H, D).transpose(0, 2, 1, 3)
            Q = heads(x @ W_Q)
            K = heads(x @ W_K)
            V = heads(x @ W_V)
            Qp = Q.reshape(Bx, H, Tr, BM, D).mean(axis=3)
            Kp = K.reshape(Bx, H, Tc, BN, D).mean(axis=3)
            avg_sc = jnp.einsum('bhid,bhjd->bhij', Qp, Kp).mean(axis=(0, 1))
            _, idx = jax.lax.top_k(avg_sc, k)
            Kb = K.reshape(Bx, H, Tc, BN, D)
            Vb = V.reshape(Bx, H, Tc, BN, D)
            Ksel = Kb[:, :, idx]
            Vsel = Vb[:, :, idx]
            Qb = Q.reshape(Bx, H, Tr, BM, D)
            scale = 1.0 / jnp.sqrt(jnp.asarray(D, jnp.float32))
            logits = jnp.einsum('bhtqd,bhtknd->bhtqkn', Qb, Ksel).reshape(Bx, H, Tr, BM, k * BN) * scale
            P = jax.nn.softmax(logits, axis=-1)
            Ob = jnp.einsum('bhtqs,bhtsd->bhtqd', P, Vsel.reshape(Bx, H, Tr, k * BN, D))
            O = Ob.reshape(Bx, H, Nx, D).transpose(0, 2, 1, 3).reshape(Bx, Nx, Ex)
            return O @ W_O
        return _forward(x, W_Q, W_K, W_V, W_O)

    def _L0_ffn_ref(x, wg, w_gate, w_down):
        import jax, jax.numpy as jnp
        import numpy as np
        B, S, D, E, F = (4, 512, 256, 8, 1024)
        Bb, Ss, Dd = x.shape
        Ee = wg.shape[1]
        T = Bb * Ss
        C = 2 * T // Ee
        tokens = x.reshape(T, Dd)
        logits = tokens.astype(jnp.float32) @ wg.astype(jnp.float32)
        gates = jax.nn.softmax(logits, axis=-1)
        idx1 = jnp.argmax(gates, axis=-1)
        mask1 = jax.nn.one_hot(idx1, Ee, dtype=jnp.int32)
        logits_no1 = jnp.where(mask1 > 0, -jnp.inf, logits)
        idx2 = jnp.argmax(logits_no1, axis=-1)
        mask2 = jax.nn.one_hot(idx2, Ee, dtype=jnp.int32)
        g1 = jnp.take_along_axis(gates, idx1[:, None], axis=-1)[:, 0]
        g2 = jnp.take_along_axis(gates, idx2[:, None], axis=-1)[:, 0]
        denom = jnp.clip(g1 + g2, 1e-09, None)
        g1, g2 = (g1 / denom, g2 / denom)
        loc1 = jnp.cumsum(mask1, axis=0) - mask1
        loc2 = jnp.cumsum(mask2, axis=0) - mask2 + jnp.sum(mask1, axis=0, keepdims=True)
        loc1_s = jnp.sum(loc1 * mask1, axis=-1)
        loc2_s = jnp.sum(loc2 * mask2, axis=-1)
        keep1 = (loc1_s < C).astype(x.dtype)
        keep2 = (loc2_s < C).astype(x.dtype)
        f1 = idx1 * C + jnp.minimum(loc1_s, C - 1)
        f2 = idx2 * C + jnp.minimum(loc2_s, C - 1)
        disp = jnp.zeros((Ee * C, Dd), dtype=x.dtype)
        disp = disp.at[f1].add(tokens * keep1[:, None])
        disp = disp.at[f2].add(tokens * keep2[:, None])
        disp = disp.reshape(Ee, C, Dd)
        h = jax.nn.gelu(jnp.einsum('ecd,edf->ecf', disp, w_gate), approximate=False)
        eo = jnp.einsum('ecf,efd->ecd', h, w_down).reshape(Ee * C, Dd)
        out = (g1 * keep1)[:, None].astype(x.dtype) * eo[f1] + (g2 * keep2)[:, None].astype(x.dtype) * eo[f2]
        return out.reshape(Bb, Ss, Dd)
    x = L0_attn_x
    x = x + _L0_attn_ref(_layernorm(x, axis=-1), L0_attn_W_Q, L0_attn_W_K, L0_attn_W_V, L0_attn_W_O)
    x = x + _L0_ffn_ref(_layernorm(x, axis=-1), L0_ffn_wg, L0_ffn_w_gate, L0_ffn_w_down)
    return x

_drawn_inputs = setup_inputs


def setup_inputs(seed=0):
    import zlib

    import numpy as np

    out = dict(_drawn_inputs(seed))
    spreads = {}
    factors = {'L0_attn_W_Q': 6.243, 'L0_attn_W_K': 6.257, 'L0_attn_W_V': 5.616, 'L0_attn_W_O': 5.65}
    for name, (base, spread) in spreads.items():
        noise = np.random.default_rng([zlib.crc32(name.encode()), seed]).standard_normal(out[name].shape)
        drawn = base * np.exp(spread * noise) if base else spread * noise
        out[name] = jnp.asarray(drawn.astype(out[name].dtype))
    for name, factor in factors.items():
        out[name] = (out[name] * factor).astype(out[name].dtype)
    return out
```

```python
from contextlib import ExitStack

import concourse.bass as bass
from concourse import mybir

ALU = mybir.AluOpType
ACT = mybir.ActivationFunctionType
AX = mybir.AxisListType
F32 = mybir.dt.float32
I32 = mybir.dt.int32
U32 = mybir.dt.uint32

P = 128
N_CONSTS = 8
LN_EPS = 1e-5
BATCH, SEQ, DM = 4, 1024, 256
TOK = BATCH * SEQ
TILES = TOK // P
HEADS, HD = 16, 16
BLK = 32
NBLK = SEQ // BLK
TOPK = int(0.2 * NBLK)
GROUPS = SEQ // P
KEYS = TOPK * BLK
HALFK = KEYS // 2
KD = DM // P
NE, FF = 8, 1024
CAP = 2 * TOK // NE
SLOT_TILES = NE * CAP // P
FCH = FF // P
HS = 8
GHS = 4 * HS
NEG = -3.0e38


def build(nc, x_d, wq_d, wk_d, wv_d, wo_d, wg_d, up_d, down_d, out_d, scratch):
    v_rows, xn2_rows, eo_rows, sel_d = scratch
    with ExitStack() as ctx:
        def sb(name, shape, dt=F32):
            return ctx.enter_context(nc.sbuf_tensor(name, shape, dt))

        def sem(name):
            return ctx.enter_context(nc.semaphore(name))

        x_sb = sb("x_sb", [P, TILES, DM])
        kq = sb("kq", [P, 2 * 8192])
        QT = kq[:, 0:8192].rearrange("p (h b n) -> p h b n", h=2, b=BATCH)
        KT = kq[:, 8192:16384].rearrange("p (k h b n) -> p k h b n", k=NBLK, h=2, b=BATCH)
        Xg = kq[:, 0:4096].rearrange("p (r s d) -> p r s d", r=2, s=8)
        XT = kq[:, 4096:8192].rearrange("p (r k n) -> p r k n", r=2, k=KD)
        hT = kq[:, 8192:16384].rearrange("p (c f n) -> p c f n", c=2, f=FCH)
        gath = sb("gath", [P, 2 * 1536 + 2 * 2048])
        Ksel = gath[:, 0:3072].rearrange("p (r j h b n) -> p r j h b n", r=2, j=TOPK, h=2, b=BATCH)
        Vsel = gath[:, 3072:7168].rearrange("p (r c b d) -> p r c b d", r=2, c=2, b=BATCH)
        G = gath[:, 0:4096].rearrange("p (r t w d) -> p r t w d", r=2, t=4, w=2)
        work = sb("work", [P, 2 * 2048 + 2 * 384 + 2 * 512 + 1024 + 1024])
        Qbd = work[:, 0:4096].rearrange("p (r h b e n) -> p r h b e n", r=2, h=2, b=BATCH, e=8)
        Pr = work[:, 4096:4864].rearrange("p (r c n) -> p r c n", r=2, c=2)
        PT = work[:, 4864:5888].rearrange("p (r c k n) -> p r c k n", r=2, c=2, k=2)
        On = work[:, 5888:6912].rearrange("p (b d) -> p b d", b=BATCH)
        OT = work[:, 6912:7936].rearrange("p (b k n) -> p b k n", b=BATCH, k=KD)
        xn = work[:, 0:2048].rearrange("p (r j d) -> p r j d", r=2, j=4)
        xnT = work[:, 2048:4096].rearrange("p (r k n) -> p r k n", r=2, k=KD)
        vst = work[:, 4096:6144].rearrange("p (r j d) -> p r j d", r=2, j=4)
        ohlo = work[:, 0:1024].rearrange("p (r q n) -> p r q n", r=2, q=4)
        ohhi = work[:, 1024:2048].rearrange("p (r q w n) -> p r q w n", r=2, q=4, w=2)
        eos = work[:, 2048:4096].rearrange("p (r s d) -> p r s d", r=4, s=2)
        wgt = sb("wgt", [P, 4 * 2048])
        wup = wgt[:, 0:4096].rearrange("p (r k f) -> p r k f", r=2, k=KD)
        wdn = wgt[:, 4096:8192].rearrange("p (r f d) -> p r f d", r=2, f=FCH)
        wproj = sb("wproj", [P, 4, KD, DM])
        wgate = sb("wgate", [P, KD, NE])
        ident = sb("ident", [P, P])
        tri = sb("tri", [P, P])
        ones = sb("ones", [P, P])
        hmask = sb("hmask", [P, 8])[:, :]
        iot_i = gath[:, 0:P].bitcast(I32)
        iot = sb("iot", [P, P])
        pcol_i = gath[:, P:P + 1].bitcast(I32)
        pcol = sb("pcol", [P, 1])
        small = sb("small", [P, 768])
        xnp = small[:, 0:256].rearrange("p (k b n) -> p k b n", k=KD, b=BATCH)
        qkp = small[:, 256:768].rearrange("p (w h b n) -> p w h b n", w=2, h=2, b=BATCH)
        slo, shi, pk, tk = (small[:, 64 * i:64 * i + 64].rearrange("p (m t) -> p m t", m=2) for i in range(4))
        lo_i, hi_i = (small[:, 256 + 64 * i:320 + 64 * i].bitcast(U32).rearrange("p (m t) -> p m t", m=2) for i in range(2))
        gt = small[:, 384:512].rearrange("p (q t) -> p q t", q=4)
        avg = sb("avg", [NBLK, NBLK])
        top8 = sb("top8", [NBLK, 8])
        idx8 = sb("idx8", [NBLK, 8], U32)
        st = sb("st", [P, 4, 6])
        mv = sb("mv", [P, 4, 2])
        rstd = sb("rstd", [P, 4])
        mhalf = sb("mhalf", [P, 4])
        epst = sb("epst", [P, 4])
        carrier = sb("carrier", [P, 1])
        carrier_v = sb("carrier_v", [P, 1])
        negmax = sb("negmax", [P, 2, 2])
        rsum = sb("rsum", [P, 2, 2, 4])
        rinv = sb("rinv", [P, 2, 4])
        xn2 = sb("xn2", [P, 2, DM])
        xn2T = sb("xn2T", [P, 2, KD, P])
        L = sb("L", [P, TILES, NE])
        mx = sb("mx", [P, 2, TILES])
        route = gath[:, 4096:7168]
        mask, tmp, tmp2 = (route[:, 512 * i:512 * i + 512].rearrange("p (m t e) -> p m t e", m=2, t=TILES) for i in range(3))
        ex = route[:, 1536:1792].rearrange("p (t e) -> p t e", t=TILES)
        tblf = route[:, 2816:2816 + SLOT_TILES]
        seg, pref = (route[:, i:i + 512].rearrange("p (e t) -> p e t", t=TILES) for i in (1792, 2304))
        eidx = sb("eidx", [P, 2, TILES])
        loc = sb("loc", [P, 2, TILES])
        keep = sb("keep", [P, 2, TILES])
        fidx = sb("fidx", [P, 2, TILES])
        fi32 = sb("fi32", [P, 2, TILES], U32)
        gk = sb("gk", [P, 2, TILES])
        tbl = sb("tbl", [P, SLOT_TILES], U32)
        sidx = sb("sidx", [P, 2, 8], U32)
        cidx = sb("cidx", [P, 2, 2, 4], U32)

        ps = [ctx.enter_context(nc.psum_tensor(f"ps{i}", [P, 512], F32)) for i in range(8)]
        Sp = [ps[i][:, 0:2 * KEYS].rearrange("p (c n) -> p c n", c=2) for i in (0, 1)]
        PTp = [ps[i][:, :].rearrange("p (c k n) -> p c k n", c=2, k=2) for i in (2, 3)]
        Op = [ps[i][:, :].rearrange("p (b c d) -> p b c d", b=2, c=4) for i in (4, 5)]
        Mp = [ps[i] for i in (6, 7)]

        x_loaded = [sem(f"x_loaded{i}") for i in range(2)]
        w_loaded = sem("w_loaded")
        consts = sem("consts")
        pool_step = sem("pool_step")
        dve_step = sem("dve_step")
        stats_ready = sem("stats_ready")
        vareps_ready = sem("vareps_ready")
        carried = sem("carried")
        rstd_ready = sem("rstd_ready")
        dve_recip = sem("dve_recip")
        dve_ln = sem("dve_ln")
        dve_acc = sem("dve_acc")
        xn_ready = sem("xn_ready")
        xt_done = sem("xt_done")
        xnt_ready = sem("xnt_ready")
        proj_done = sem("proj_done")
        projc_act = sem("projc_act")
        projc_dve = sem("projc_dve")
        vp_done = sem("vp_done")
        vst_ready = sem("vst_ready")
        v_stored = [sem(f"v_stored{i}") for i in range(2)]
        xnp_ready = sem("xnp_ready")
        pool_mm = sem("pool_mm")
        pooled_ready = sem("pooled_ready")
        avg_done = sem("avg_done")
        sel_ready = sem("sel_ready")
        sel_stored = sem("sel_stored")
        ksel_loaded = [sem(f"ksel_loaded{i}") for i in range(2)]
        vsel_loaded = [sem(f"vsel_loaded{i}") for i in range(2)]
        qbd_ready = sem("qbd_ready")
        qk_done = sem("qk_done")
        max_done = sem("max_done")
        exp_done = sem("exp_done")
        pt_done = sem("pt_done")
        ptc_dve = sem("ptc_dve")
        ptc_act = sem("ptc_act")
        pv_done = sem("pv_done")
        o_ready = sem("o_ready")
        ot_done = sem("ot_done")
        ot_ready = sem("ot_ready")
        oproj_done = sem("oproj_done")
        xn2_ready = sem("xn2_ready")
        xn2_stored = [sem(f"xn2_stored{i}") for i in range(2)]
        xn2t_done = sem("xn2t_done")
        xn2t_ready = sem("xn2t_ready")
        lg_done = sem("lg_done")
        lg_ready = sem("lg_ready")
        ex_in = sem("ex_in")
        ex_done = sem("ex_done")
        masks_ready = sem("masks_ready")
        prefix_done = sem("prefix_done")
        oh_ready = sem("oh_ready")
        oh_used = sem("oh_used")
        sidx_ready = sem("sidx_ready")
        xg_loaded = [sem(f"xg_loaded{i}") for i in range(2)]
        xgt_done = sem("xgt_done")
        xgt_ready = sem("xgt_ready")
        we_loaded = [sem(f"we_loaded{i}") for i in range(2)]
        up_done = sem("up_done")
        h_ready = sem("h_ready")
        dn_done = sem("dn_done")
        eo_ready = sem("eo_ready")
        eo_stored = [sem(f"eo_stored{i}") for i in range(4)]
        cidx_ready = sem("cidx_ready")
        g_loaded = [sem(f"g_loaded{i}") for i in range(2)]
        y_ready = sem("y_ready")
        out_stored = sem("out_stored")

        x_v = x_d.rearrange("b (t p) d -> p (b t) d", p=P)
        out_v = out_d.rearrange("b (t p) d -> p (b t) d", p=P)
        v_v = v_rows.rearrange("(t p) b d -> p t b d", p=P)
        xn2_v = xn2_rows.rearrange("(t p) d -> p t d", p=P)
        eo_v = eo_rows.rearrange("(s p) d -> p s d", p=P)
        N_PROJ_ACT = 3

        block = ctx.enter_context(nc.Block())

        def wait_count(eng, semaphore, count):
            if not (isinstance(count, int) and count == 0):
                eng.wait_ge(semaphore, count)

        @block.sync
        def _(sp):
            for i, w in enumerate((wk_d, wq_d, wv_d, wo_d)):
                if i == 0:
                    sp.dma_start(x_sb[:, 0:4, :], x_v[:, 0:4, :]).then_inc(x_loaded[0], 16)
                slot = (1, 0, 2, 3)[i]
                sp.dma_start(wproj[:, slot], w.rearrange("(k p) n -> p k n", p=P)).then_inc(w_loaded, 16)
                if i == 0:
                    sp.dma_start(x_sb[:, 4:8, :], x_v[:, 4:8, :]).then_inc(x_loaded[1], 16)
            sp.dma_start(wgate[:], wg_d.rearrange("(k p) e -> p k e", p=P)).then_inc(w_loaded, 16)

            def load_expert(e, r):
                sp.dma_start(wup[:, r], up_d[bass.ds(e, 1)].rearrange("e (k p) f -> p (e k) f", p=P))\
                    .then_inc(we_loaded[r], 16)
                sp.dma_start(wdn[:, r], down_d[bass.ds(e, 1)].rearrange("e (f p) d -> p (e f) d", p=P))\
                    .then_inc(we_loaded[r], 16)

            def store_v(b, r):
                sp.wait_ge(vst_ready, 4 * b + 2 * r + 2)
                sp.dma_start(v_v[:, 4 * r:4 * r + 4, bass.ds(b, 1), :].rearrange("p t b d -> p t (b d)"),
                             vst[:, r]).then_inc(v_stored[r], 16)

            with sp.Fori(0, BATCH - 1) as b:
                for r in range(2):
                    sp.wait_ge(x_loaded[r], 16 * b + 16)
                    sp.dma_start(x_sb[:, bass.ds(8 * b + 8 + 4 * r, 4), :],
                                 x_v[:, bass.ds(8 * b + 8 + 4 * r, 4), :]).then_inc(x_loaded[r], 16)
                for r in range(2):
                    store_v(b, r)
            for r in range(2):
                store_v(BATCH - 1, r)
            for r in range(2):
                load_expert(r, r)

            sp.wait_ge(sel_ready, 1)
            sp.dma_start(sel_d, idx8[:]).then_inc(sel_stored, 16)
            sp.wait_ge(sel_stored, 16)
            for r in range(2):
                sp.wait_ge(v_stored[r], 16 * BATCH)

            def gather(t, r):
                _, blocks = nc.values_load_multi_w_load_instructions(
                    sel_d[bass.ds(t, 1), 0:TOPK], engines=(mybir.EngineType.SP,), min_val=0, max_val=NBLK - 1)
                if not isinstance(t, int):
                    sp.wait_ge(qk_done, HS * t - HS)
                for j, blk in enumerate(blocks):
                    sp.dma_start(Ksel[:, r, j].rearrange("p h b n -> p (h b n)"),
                                 KT[:, bass.ds(blk, 1)].rearrange("p k h b n -> p (k h b n)"))\
                        .then_inc(ksel_loaded[r], 16)
                if not isinstance(t, int):
                    sp.wait_ge(pv_done, HS * t - HS)
                for j, blk in enumerate(blocks):
                    q = 32 * (j % 3)
                    sp.dma_start(Vsel[q:q + 32, r, j // 3].rearrange("p b d -> p (b d)"),
                                 v_rows[bass.ds(blk * BLK, BLK)].rearrange("n b d -> n (b d)"))\
                        .then_inc(vsel_loaded[r], 16)

            sp.wait_ge(projc_act, N_PROJ_ACT * 2 * BATCH)
            for r in range(2):
                gather(r, r)
            with sp.Fori(1, NBLK // 2) as u:
                for r in range(2):
                    gather(2 * u + r, r)

            def store_eo(e, s):
                n = 4 * e + s
                sp.wait_ge(eo_ready, n + 1)
                sp.dma_start(eo_v[:, bass.ds(8 * e + 2 * s, 2), :], eos[:, s]).then_inc(eo_stored[s], 16)

            def expert_io(e, r, more):
                for s in range(4):
                    store_eo(e, s)
                if more:
                    load_expert(e + 2, r)

            with sp.Fori(0, NE // 2 - 1) as u:
                for r in range(2):
                    expert_io(2 * u + r, r, True)
            for r in range(2):
                expert_io(NE - 2 + r, r, False)
            with sp.Fori(0, TILES // 4) as i:
                sp.wait_ge(y_ready, i + 1)
                sp.dma_start(out_v[:, bass.ds(4 * i, 4), :], x_sb[:, bass.ds(4 * i, 4), :])\
                    .then_inc(out_stored, 16)
            sp.wait_ge(out_stored, 16 * (TILES // 4))
            for r in range(2):
                sp.wait_ge(xn2_stored[r], 16 * TILES // 2)
            for s in range(4):
                sp.wait_ge(eo_stored[s], 16 * NE)

        @block.gpsimd
        def _(pool):
            nc.gpsimd.memset(ident[:], 0.0).then_inc(pool_step, 1)
            nc.gpsimd.memset(tri[:], 1.0).then_inc(pool_step, 1)
            nc.gpsimd.memset(hmask, float(HD) ** -0.5).then_inc(pool_step, 1)
            nc.gpsimd.memset(ones[:], 1.0).then_inc(consts, 1)
            nc.gpsimd.memset(mhalf[:], -0.5).then_inc(consts, 1)
            nc.gpsimd.memset(epst[:], LN_EPS).then_inc(consts, 1)
            nc.gpsimd.memset(carrier[:], 0.0).then_inc(carried, 1)
            nc.gpsimd.iota(iot_i, pattern=[[1, P]], base=0, channel_multiplier=0).then_inc(pool_step, 1)
            nc.gpsimd.iota(pcol_i, pattern=[[0, 1]], base=0, channel_multiplier=1).then_inc(pool_step, 1)
            pool.wait_ge(pool_step, 5)
            nc.gpsimd.affine_select(out=ident[:], in_=ident[:], compare_op=ALU.not_equal, fill=1.0, base=0,
                                    pattern=[[-1, P]], channel_multiplier=1).then_inc(consts, 1)
            nc.gpsimd.affine_select(out=tri[:], in_=tri[:], compare_op=ALU.is_ge, fill=0.0, base=-1,
                                    pattern=[[1, P]], channel_multiplier=-1).then_inc(consts, 1)
            nc.gpsimd.affine_select(out=hmask, in_=hmask, compare_op=ALU.is_ge, fill=0.0, base=0,
                                    pattern=[[-HD, 8]], channel_multiplier=1).then_inc(pool_step, 1)
            pool.wait_ge(pool_step, 6)
            nc.gpsimd.affine_select(out=hmask, in_=hmask, compare_op=ALU.is_ge, fill=0.0, base=HD - 1,
                                    pattern=[[HD, 8]], channel_multiplier=-1).then_inc(consts, 1)
            nc.gpsimd.tensor_copy(iot[:], iot_i).then_inc(consts, 1)
            nc.gpsimd.tensor_copy(pcol[:], pcol_i).then_inc(consts, 1)
            pool.wait_ge(consts, N_CONSTS)

            def inv_sqrt(n, var, eps, half, out):
                nc.gpsimd.tensor_tensor(out, var, eps, ALU.add).then_inc(vareps_ready, 1)
                pool.wait_ge(vareps_ready, n + 1)
                nc.gpsimd.tensor_tensor(out, out, half, ALU.pow).then_inc(rstd_ready, 1)

            with pool.Fori(0, 2 * BATCH) as c:
                pool.wait_ge(stats_ready, c + 1)
                inv_sqrt(c, mv[:, :, 1], epst[:], mhalf[:], rstd[:])

            def spread_q(t, r):
                src = QT[:, :, :, bass.ds(t * BLK, BLK)].rearrange("p h b n -> p (h b) n")
                dst = Qbd[:, r].rearrange("p h b e n -> p (h b) e n")
                nc.gpsimd.tensor_tensor(
                    dst, src[:, :, None, :].to_broadcast([P, 8, 8, BLK]),
                    hmask[:, None, :, None].to_broadcast([P, 8, 8, BLK]), ALU.mult).then_inc(qbd_ready, 1)

            pool.wait_ge(projc_act, N_PROJ_ACT * 2 * BATCH)
            pool.wait_ge(projc_dve, 2 * BATCH)
            pool.wait_ge(vp_done, 4 * BATCH)
            pool.wait_ge(vst_ready, 4 * BATCH)
            for r in range(2):
                pool.wait_ge(v_stored[r], 16 * BATCH)
            for r in range(2):
                spread_q(r, r)

            def spread_next(t, r):
                pool.wait_ge(qk_done, HS * t - HS)
                spread_q(t, r)

            def rstd_of(n):
                pool.wait_ge(stats_ready, 2 * BATCH + n + 1)
                inv_sqrt(2 * BATCH + n, mv[:, 0, 1:2], epst[:, 0:1], mhalf[:, 0:1], rstd[:, 0:1])

            def group(g, first, last):
                for what, n in (("q", 2), ("r", 0), ("r", 1), ("q", 3), ("r", 2), ("q", 4), ("r", 3), ("q", 5)):
                    if what == "q" and not (last and n >= 4):
                        spread_next(4 * g + n, n % 2)
                    if what == "r" and not first:
                        rstd_of(4 * (g - 1) + n)

            group(0, True, False)
            group(1, False, False)
            with pool.Fori(2, GROUPS - 1) as g:
                group(g, False, False)
            group(GROUPS - 1, False, True)
            for b in range(BATCH):
                rstd_of(4 * (GROUPS - 1) + b)

            def carry_pool(n):
                pool.wait_ge(carried, n + 1)
                nc.gpsimd.tensor_tensor(carrier[0:1, :], mhalf[0:1, 0:1], epst[0:1, 0:1], ALU.add).then_inc(carried, 1)

            def gather_tokens(e, r):
                pool.wait_ge(sidx_ready, e + 1)
                carry_pool(e)
                for s in range(8):
                    nc.gpsimd.indirect_dma_start(
                        out=Xg[:, r, s, :], out_offset=None, in_=xn2_rows,
                        in_offset=bass.IndirectOffsetOnAxis(ap=sidx[:, r, s:s + 1], axis=0))\
                        .then_inc(xg_loaded[r], 16)

            for r in range(2):
                pool.wait_ge(xn2_stored[r], 16 * TILES // 2)
            with pool.Fori(0, NE // 2) as u:
                for r in range(2):
                    gather_tokens(2 * u + r, r)

            for s in range(4):
                pool.wait_ge(eo_stored[s], 16 * NE)
            with pool.Fori(0, TILES // 8) as u:
                for r in range(2):
                    pool.wait_ge(cidx_ready, 2 * u + r + 1)
                    carry_pool(NE + 2 * u + r)
                    for t in range(4):
                        for w in range(2):
                            nc.gpsimd.indirect_dma_start(
                                out=G[:, r, t, w, :], out_offset=None, in_=eo_rows,
                                in_offset=bass.IndirectOffsetOnAxis(ap=cidx[:, r, w, t:t + 1], axis=0))\
                                .then_inc(g_loaded[r], 16)

        @block.scalar
        def _(act):
            def project(b):
                for r in range(2):
                    c = 2 * b + r
                    act.wait_ge(xt_done, c + 1)
                    for k in range(KD):
                        nc.scalar.copy(xnT[:, r, k, :], ps[k][:]).then_inc(xnt_ready, 1)
                    for h in range(2):
                        act.wait_ge(proj_done, 4 * c + h + 1)
                        nc.scalar.copy(KT[:, 16 * r:16 * r + 16, h, bass.ds(b, 1), :].rearrange("p k b n -> p k (b n)"),
                                       ps[2 + h][:, :].rearrange("p (k n) -> p k n", n=BLK)).then_inc(projc_act, 1)
                    act.wait_ge(proj_done, 4 * c + 3)
                    nc.scalar.copy(QT[:, 0, bass.ds(b, 1), 512 * r:512 * r + 512].rearrange("p b n -> p (b n)"),
                                   ps[4][:]).then_inc(projc_act, 1)

            project(0)
            with act.Fori(1, BATCH) as b:
                project(b)

            def exps(hs, r, b, h, t4):
                w = (2 * t4 + b // 2) % 2
                act.wait_ge(max_done, hs + 1)
                for c in range(2):
                    a = nc.scalar.activation(Pr[:, r, c, :], Sp[r][:, c, :], ACT.Exp, bias=negmax[:, r, c:c + 1],
                                             accum_out=rsum[:, w, b % 2, 2 * h + c:2 * h + c + 1])
                a.then_inc(exp_done, 1)

            def copy_pt(hs, r):
                act.wait_ge(pt_done, hs + 1)
                nc.scalar.copy(PT[0:HALFK, r], PTp[r][0:HALFK]).then_inc(ptc_act, 1)

            def out_steps(g, k):
                if k in (4, 5):
                    i = k - 4
                    act.wait_ge(ot_done, 2 * g + i + 1)
                    nc.scalar.copy(OT[:, 2 * i:2 * i + 2].rearrange("p b k n -> p (b k n)"), Mp[i][:])\
                        .then_inc(ot_ready, 1)
                for b in range(BATCH):
                    base = 4 + 6 * b
                    if k == base + 6:
                        act.wait_ge(xn2t_done, 4 * g + b + 1)
                        nc.scalar.copy(xn2T[:, b % 2].rearrange("p k n -> p (k n)"), Mp[b % 2][:, 256:512])\
                            .then_inc(xn2t_ready, 1)
                        act.wait_ge(xn2_ready, 4 * g + b + 1)
                        act.dma_start(xn2_v[:, bass.ds(8 * b + g, 1), :].rearrange("p t d -> p (t d)"), xn2[:, b % 2, :])\
                            .then_inc(xn2_stored[b % 2], 16)

            def group(g, first, last):
                if first:
                    act.wait_ge(w_loaded, 16)
                    for k in range(2):
                        exps(k, k, 0, k, 0)
                for k in range(GHS):
                    hs = GHS * g + k
                    if k % 2:
                        copy_pt(hs, 1)
                    n = k + 2
                    if not (last and n >= GHS):
                        m = n % GHS
                        if m % 4 == 0 and not (first and n < 8):
                            act.wait_ge(o_ready, 8 * g + n // 4 - 1)
                        exps(hs + 2, m % 2, (m % HS) // 2, m % 2, m // HS)
                    if not first:
                        out_steps(g - 1, k)

            group(0, True, False)
            group(1, False, False)
            with act.Fori(2, GROUPS - 1) as g:
                group(g, False, False)
            group(GROUPS - 1, False, True)
            for k in range(GHS):
                out_steps(GROUPS - 1, k)

            act.wait_ge(ex_in, 1)
            nc.scalar.activation(ex, tmp[:, 0], ACT.Exp).then_inc(ex_done, 1)
            nc.scalar.activation(gt[:, 2, :], mx[:, 1, :], ACT.Exp).then_inc(ex_done, 1)

            with act.Fori(0, NE) as e:
                for n in range(16):
                    c, f = n // 8, n % 8
                    act.wait_ge(up_done, 16 * e + n + 1)
                    nc.scalar.activation(hT[:, c, f, :], ps[2 + n % 4][:], ACT.Gelu).then_inc(h_ready, 1)

        @block.tensor
        def _(pe):
            pe.wait_ge(consts, N_CONSTS)
            pe.wait_ge(w_loaded, 16 * 5)
            def project(b):
                for r in range(2):
                    c = 2 * b + r
                    pe.wait_ge(xn_ready, c + 1)
                    wait_count(pe, xnt_ready, 2 * c)
                    for k in range(KD):
                        for j in range(4):
                            mm = nc.tensor.transpose(ps[k][:, j * P:(j + 1) * P], xn[:, r, j, k * P:(k + 1) * P], ident[:])
                    mm.then_inc(xt_done, 1)
                    pe.wait_ge(xnt_ready, 2 * c + 2)
                    for i, (w, h) in enumerate(((1, 0), (1, 1), (0, 0), (0, 1))):
                        if i < 3:
                            wait_count(pe, projc_act, N_PROJ_ACT * c)
                        else:
                            wait_count(pe, projc_dve, c)
                        for k in range(KD):
                            mm = nc.tensor.matmul(ps[2 + i][:], wproj[:, w, k, h * P:(h + 1) * P], xnT[:, r, k, :],
                                                  start=(k == 0), stop=(k == KD - 1))
                        mm.then_inc(proj_done, 1)
                    for i in range(2):
                        wait_count(pe, vst_ready, 2 * c)
                        for jj in range(2):
                            j = 2 * i + jj
                            for k in range(KD):
                                mm = nc.tensor.matmul(ps[6 + i][:, jj * DM:(jj + 1) * DM],
                                                      xnT[:, r, k, j * P:(j + 1) * P], wproj[:, 2, k, :],
                                                      start=(k == 0), stop=(k == KD - 1))
                        mm.then_inc(vp_done, 1)

            project(0)
            with pe.Fori(1, BATCH) as b:
                project(b)

            pe.wait_ge(xnp_ready, 2 * BATCH)
            pe.wait_ge(xnt_ready, 4 * BATCH)
            for w in range(2):
                for h in range(2):
                    for k in range(KD):
                        mm = nc.tensor.matmul(ps[0][:, (2 * w + h) * P:(2 * w + h + 1) * P],
                                              wproj[:, w, k, h * P:(h + 1) * P],
                                              xnp[:, k].rearrange("p b n -> p (b n)"),
                                              start=(k == 0), stop=(k == KD - 1))
            mm.then_inc(pool_mm, 1)
            pe.wait_ge(pooled_ready, 1)
            n = 0
            for h in range(2):
                for b in range(BATCH):
                    mm = nc.tensor.matmul(ps[1][0:NBLK, 0:NBLK], qkp[:, 0, h, b, :], qkp[:, 1, h, b, :],
                                          start=(n == 0), stop=(n == 7))
                    n += 1
            mm.then_inc(avg_done, 1)

            def scores(hs, m):
                t4, b, h = m // HS, (m % HS) // 2, m % 2
                r = t4 % 2
                for c in range(2):
                    mm = nc.tensor.matmul(Sp[m % 2][:, c, :], Qbd[:, r, h, b, 4 * c:4 * c + 4, :].rearrange("p e n -> p (e n)"),
                                          Ksel[:, r, :, h, b, :], start=True, stop=True)
                mm.then_inc(qk_done, 1)

            def scores_ready(t, g, t4):
                r = t4 % 2
                pe.wait_ge(qbd_ready, t + 1)
                pe.wait_ge(ksel_loaded[r], 96 * (2 * g + t4 // 2) + 96)

            def values(hs, m):
                t4, b, h = m // HS, (m % HS) // 2, m % 2
                w = (2 * t4 + b // 2) % 2
                for c in range(2):
                    q = 2 * h + c
                    for kc in range(2):
                        mm = nc.tensor.matmul(Op[w][:, b % 2, q, :], PT[0:HALFK, m % 2, c, kc, :],
                                              Vsel[0:HALFK, t4 % 2, kc, b, q * 64:(q + 1) * 64],
                                              start=(kc == 0), stop=(kc == 1))
                mm.then_inc(pv_done, 1)

            def out_steps(g, k):
                if k in (2, 3):
                    i = k - 2
                    if i == 0:
                        pe.wait_ge(o_ready, 8 * g + 8)
                    wait_count(pe, lg_ready, 4 * g)
                    for b in (2 * i, 2 * i + 1):
                        for kk in range(KD):
                            mm = nc.tensor.transpose(Mp[i][:, ((b % 2) * 2 + kk) * P:((b % 2) * 2 + kk + 1) * P],
                                                     On[:, b, kk * P:(kk + 1) * P], ident[:])
                    mm.then_inc(ot_done, 1)
                for b in range(BATCH):
                    base = 4 + 6 * b
                    M = Mp[b % 2]
                    if k == base + 1:
                        pe.wait_ge(ot_ready, 2 * g + 2)
                        if b >= 2:
                            pe.wait_ge(lg_ready, 4 * g + b - 1)
                        for kk in range(KD):
                            mm = nc.tensor.matmul(M[:, 0:DM], OT[:, b, kk, :], wproj[:, 3, kk, :],
                                                  start=(kk == 0), stop=(kk == KD - 1))
                        mm.then_inc(oproj_done, 1)
                    if k == base + 5:
                        pe.wait_ge(xn2_ready, 4 * g + b + 1)
                        for kk in range(KD):
                            mm = nc.tensor.transpose(M[:, 256 + kk * P:256 + (kk + 1) * P], xn2[:, b % 2, kk * P:(kk + 1) * P],
                                                     ident[:])
                        mm.then_inc(xn2t_done, 1)
                    if k == base + 7:
                        pe.wait_ge(xn2t_ready, 4 * g + b + 1)
                        for kk in range(KD):
                            mm = nc.tensor.matmul(M[:, 0:NE], xn2T[:, b % 2, kk, :], wgate[:, kk, :],
                                                  start=(kk == 0), stop=(kk == KD - 1))
                        mm.then_inc(lg_done, 1)

            def group(g, first, last):
                if first:
                    scores_ready(0, 0, 0)
                    pe.wait_ge(sel_ready, 1)
                    for m in range(2):
                        scores(m, m)
                for k in range(GHS):
                    hs = GHS * g + k
                    pe.wait_ge(exp_done, hs + 1)
                    if not (first and k < 2):
                        pe.wait_ge(ptc_act if k % 2 else ptc_dve, (GHS // 2) * g + k // 2)
                    for c in range(2):
                        for kc in range(2):
                            mm = nc.tensor.transpose(PTp[k % 2][0:HALFK, c, kc, :],
                                                     Pr[:, k % 2, c, kc * HALFK:(kc + 1) * HALFK], ident[:])
                    mm.then_inc(pt_done, 1)
                    n = k + 2
                    if not (last and n >= GHS):
                        if n % HS == 0:
                            scores_ready(4 * g + n // HS, g + (1 if n >= GHS else 0), (n // HS) % 4)
                        scores(hs + 2, n % GHS)
                    if not (first and k == 0):
                        m = (k - 1) % GHS
                        if m % 4 == 0 and not (first and k - 1 < 8):
                            pe.wait_ge(o_ready, 8 * g + (k - 1) // 4 - 1)
                        if m % HS == 0:
                            pe.wait_ge(vsel_loaded[(m // HS) % 2], 96 * (2 * g + m // HS // 2) + 96)
                        pe.wait_ge(ptc_act if m % 2 else ptc_dve, (GHS // 2) * g + ((k - 1) // 2) + 1)
                        values(hs - 1, m)
                    if not first:
                        out_steps(g - 1, k)

            group(0, True, False)
            group(1, False, False)
            with pe.Fori(2, GROUPS - 1) as g:
                group(g, False, False)
            group(GROUPS - 1, False, True)
            pe.wait_ge(ptc_act, GROUPS * GHS // 2)
            values(0, GHS - 1)
            for k in range(GHS):
                out_steps(GROUPS - 1, k)

            pe.wait_ge(masks_ready, 1)
            mflat = mask.rearrange("p m t e -> p (m t e)")
            nc.tensor.matmul(ps[0][:], tri[:], mflat, start=True, stop=True)
            nc.tensor.matmul(ps[1][:], ones[:], mflat, start=True, stop=True).then_inc(prefix_done, 1)
            n = 0
            for i in range(16):
                pe.wait_ge(oh_ready, i + 1)
                for q in range(4):
                    mm = nc.tensor.matmul(ps[6][:, 0:P], ohlo[:, i % 2, q, :],
                                          ohhi[:, i % 2, q].rearrange("p w n -> p (w n)"),
                                          start=(n == 0), stop=(n == 63))
                    n += 1
                mm.then_inc(oh_used, 1)

            def turn_rows(e, r):
                pe.wait_ge(xg_loaded[r], 64 * (e - r) + 128)
                for i in range(4):
                    wait_count(pe, xgt_ready, 4 * e + max(i - 1, 0))
                    for s in range(2):
                        for k in range(KD):
                            mm = nc.tensor.transpose(ps[i % 2][:, (2 * k + s) * P:(2 * k + s + 1) * P],
                                                     Xg[:, r, 2 * i + s, k * P:(k + 1) * P], ident[:])
                    mm.then_inc(xgt_done, 1)

            def up(e, r):
                pe.wait_ge(we_loaded[r], 16 * (e - r) + 32)
                pe.wait_ge(xgt_ready, 4 * e + 4)
                for n in range(16):
                    c, f = n // 8, n % 8
                    if not (isinstance(e, int) and e == 0 and n < 4):
                        pe.wait_ge(h_ready, 16 * e + n - 3)
                    for k in range(KD):
                        mm = nc.tensor.matmul(ps[2 + n % 4][:], wup[:, r, k, f * P:(f + 1) * P],
                                              XT[:, r, k, c * 512:(c + 1) * 512], start=(k == 0), stop=(k == KD - 1))
                    mm.then_inc(up_done, 1)

            def down(e, r):
                for i in range(4):
                    if i % 2 == 0:
                        pe.wait_ge(h_ready, 16 * e + 4 * i + 8)
                    if not (isinstance(e, int) and e == 0 and i < 2):
                        pe.wait_ge(eo_ready, 4 * e + i - 1)
                    for s in range(2):
                        t = 2 * i + s
                        for f in range(FCH):
                            mm = nc.tensor.matmul(ps[6 + i % 2][:, s * DM:(s + 1) * DM],
                                                  hT[:, t // 4, f, (t % 4) * P:(t % 4 + 1) * P], wdn[:, r, f, :],
                                                  start=(f == 0), stop=(f == FCH - 1))
                    mm.then_inc(dn_done, 1)

            def expert(e, r, more):
                up(e, r)
                if more:
                    turn_rows(e + 1, 1 - r)
                down(e, r)

            pe.wait_ge(sidx_ready, 1)
            turn_rows(0, 0)
            for r in range(2):
                expert(r, r, True)
            with pe.Fori(1, NE // 2 - 1) as u:
                for r in range(2):
                    expert(2 * u + r, r, True)
            for r in range(2):
                expert(NE - 2 + r, r, r == 0)

        @block.vector
        def _(dve):
            steps = [0]

            def carry_dve():
                nc.vector.memset(carrier_v[0:1, :], 0.0)

            def step_wait(base, k):
                dve.wait_ge(dve_step, base + k)

            LN_STEPS = 4
            dve.wait_ge(consts, N_CONSTS)
            def project(b):
                for r in range(2):
                    c = 2 * b + r
                    s0 = LN_STEPS * c
                    dve.wait_ge(x_loaded[r], 16 * b + 16)
                    carry_dve()
                    for j in range(4):
                        nc.vector.bn_stats(st[:, j, :], x_sb[:, bass.ds(4 * c + j, 1), :].rearrange("p t d -> p (t d)"))\
                            .then_inc(dve_step, 1)
                    step_wait(s0, 4)
                    carry_dve()
                    for j in range(4):
                        a = nc.vector.bn_aggr(mv[:, j, :], st[:, j, :])
                    a.then_inc(stats_ready, 1)
                    dve.wait_ge(rstd_ready, c + 1)
                    for j in range(4):
                        a = nc.vector.tensor_scalar(xn[:, r, j, :], x_sb[:, bass.ds(4 * c + j, 1), :].rearrange("p t d -> p (t d)"),
                                                    mv[:, j, 0:1], rstd[:, j:j + 1], ALU.subtract, ALU.mult)
                    a.then_inc(xn_ready, 1)
                    dve.wait_ge(xnt_ready, 2 * c + 2)
                    nc.vector.tensor_reduce(
                        xnp[:, :, bass.ds(b, 1), 16 * r:16 * r + 16].rearrange("p k b n -> p k (b n)"),
                        xnT[:, r].rearrange("p k (n q) -> p k n q", q=BLK), AX.X, ALU.add).then_inc(xnp_ready, 1)
                    dve.wait_ge(proj_done, 4 * c + 4)
                    nc.vector.tensor_copy(QT[:, 1, bass.ds(b, 1), 512 * r:512 * r + 512].rearrange("p b n -> p (b n)"),
                                          ps[5][:]).then_inc(projc_dve, 1)
                    wait_count(dve, v_stored[r], 16 * b)
                    for i in range(2):
                        dve.wait_ge(vp_done, 2 * c + i + 1)
                        nc.vector.tensor_copy(vst[:, r, 2 * i:2 * i + 2, :].rearrange("p j d -> p (j d)"), ps[6 + i][:])\
                            .then_inc(vst_ready, 1)

            project(0)
            with dve.Fori(1, BATCH) as b:
                project(b)
            s0 = LN_STEPS * 2 * BATCH

            dve.wait_ge(pool_mm, 1)
            nc.vector.tensor_copy(qkp.rearrange("p w h b n -> p (w h b n)"), ps[0][:]).then_inc(pooled_ready, 1)
            dve.wait_ge(avg_done, 1)
            nc.vector.tensor_copy(avg[:], ps[1][0:NBLK, 0:NBLK]).then_inc(dve_step, 1)
            step_wait(s0, 1)
            nc.vector.max(top8[:], avg[:]).then_inc(dve_step, 1)
            step_wait(s0, 2)
            nc.vector.max_index(idx8[:], top8[:], avg[:]).then_inc(sel_ready, 1)
            s0 += 2

            def maxima(hs, r):
                dve.wait_ge(qk_done, hs + 1)
                nc.vector.tensor_reduce(negmax[:, r, :], Sp[r], AX.X, ALU.max, negate=True).then_inc(max_done, 1)

            def copy_pt(hs, r):
                dve.wait_ge(pt_done, hs + 1)
                nc.vector.tensor_copy(PT[0:HALFK, r], PTp[r][0:HALFK]).then_inc(ptc_dve, 1)

            def norm_out(g, w8):
                t4, bp = w8 // 2, w8 % 2
                dve.wait_ge(pv_done, GHS * g + 4 * w8 + 4)
                nc.vector.reciprocal(rinv[:].rearrange("p b c -> p (b c)"), rsum[:, w8 % 2].rearrange("p b c -> p (b c)"))\
                    .then_inc(dve_recip, 1)
                dve.wait_ge(dve_recip, 8 * g + w8 + 1)
                for e in range(4):
                    q = slice(32 * e, 32 * e + 32)
                    a = nc.vector.tensor_tensor(
                        On[32 * t4:32 * t4 + 32, 2 * bp:2 * bp + 2, :].rearrange("p b (c x) -> p (b c) x", c=4)[:, :, HD * e:HD * e + HD],
                        Op[w8 % 2][q].rearrange("p b c d -> p (b c) d")[:, :, HD * e:HD * e + HD],
                        rinv[q].rearrange("p b c -> p (b c)")[:, :, None].to_broadcast([32, 8, HD]), ALU.mult)
                a.then_inc(o_ready, 1)

            def out_steps(g, k):
                for b in range(BATCH):
                    base = 4 + 6 * b
                    M = Mp[b % 2]
                    xt = x_sb[:, bass.ds(8 * b + g, 1), :].rearrange("p t d -> p (t d)")
                    s = 2 * (4 * g + b)
                    if k == base + 2:
                        dve.wait_ge(oproj_done, 4 * g + b + 1)
                        nc.vector.tensor_tensor(xt, M[:, 0:DM], xt, ALU.add).then_inc(dve_ln, 1)
                        dve.wait_ge(dve_ln, s + 1)
                        carry_dve()
                        nc.vector.bn_stats(st[:, 0, :], xt).then_inc(dve_ln, 1)
                        dve.wait_ge(dve_ln, s + 2)
                        carry_dve()
                        nc.vector.bn_aggr(mv[:, 0, :], st[:, 0, :]).then_inc(stats_ready, 1)
                    if k == base + 4:
                        dve.wait_ge(rstd_ready, 2 * BATCH + 4 * g + b + 1)
                        wait_count(dve, xn2_stored[b % 2], 32 * g + 16 * (b // 2))
                        nc.vector.tensor_scalar(xn2[:, b % 2, :], xt, mv[:, 0, 0:1], rstd[:, 0:1], ALU.subtract, ALU.mult)\
                            .then_inc(xn2_ready, 1)
                    if k == base + 8:
                        dve.wait_ge(lg_done, 4 * g + b + 1)
                        nc.vector.tensor_copy(L[:, bass.ds(8 * b + g, 1), :].rearrange("p t e -> p (t e)"), M[:, 0:NE])\
                            .then_inc(lg_ready, 1)

            def group(g, first, last):
                if first:
                    for k in range(2):
                        maxima(k, k)
                for k in range(GHS):
                    hs = GHS * g + k
                    if k % 2 == 0:
                        copy_pt(hs, 0)
                    if not (last and k + 2 >= GHS):
                        maxima(hs + 2, k % 2)
                    if k % 4 == 1 and not (first and k == 1):
                        if k == 5 and not first:
                            dve.wait_ge(ot_done, 2 * g)
                        w8 = k // 4 - 1
                        if w8 >= 0:
                            norm_out(g, w8)
                        else:
                            norm_out(g - 1, 7)
                    if not first:
                        out_steps(g - 1, k)

            group(0, True, False)
            group(1, False, False)
            with dve.Fori(2, GROUPS - 1) as g:
                group(g, False, False)
            group(GROUPS - 1, False, True)
            norm_out(GROUPS - 1, 7)
            for k in range(GHS):
                out_steps(GROUPS - 1, k)

            cnt = [s0]

            def link(ins):
                cnt[0] += 1
                ins.then_inc(dve_step, 1)
                dve.wait_ge(dve_step, cnt[0])

            V = nc.vector
            dve.wait_ge(lg_ready, TILES)
            eb = iot[:, None, 0:NE].to_broadcast([P, TILES, NE])

            def per_tile(a):
                return a[:, :, None].to_broadcast([P, TILES, NE])

            for w in range(2):
                src = L[:] if w == 0 else tmp2[:, 1]
                link(V.tensor_reduce(mx[:, w, :], src, AX.X, ALU.max))
                link(V.tensor_tensor(tmp[:, w], src, per_tile(mx[:, w, :]), ALU.is_equal))
                link(V.tensor_scalar(tmp[:, w], tmp[:, w], -float(NE), float(NE), ALU.mult, ALU.add))
                link(V.tensor_tensor(tmp[:, w], tmp[:, w], eb, ALU.add))
                link(V.tensor_reduce(eidx[:, w, :], tmp[:, w], AX.X, ALU.min))
                link(V.tensor_tensor(mask[:, w], eb, per_tile(eidx[:, w, :]), ALU.is_equal))
                if w == 0:
                    link(V.scalar_tensor_tensor(tmp2[:, 1], mask[:, 0], NEG, L[:], ALU.mult, ALU.add))
            V.drain().then_inc(masks_ready, 1)
            link(V.tensor_tensor(tmp[:, 0], L[:], per_tile(mx[:, 0, :]), ALU.subtract))
            link(V.tensor_tensor(mx[:, 1, :], mx[:, 1, :], mx[:, 0, :], ALU.subtract))
            V.drain().then_inc(ex_in, 1)
            V.memset(seg, 1.0).then_inc(dve_step, 1)
            cnt[0] += 1
            dve.wait_ge(dve_step, cnt[0])
            link(V.memset(seg[:, :, 0:1], 0.0))
            dve.wait_ge(prefix_done, 1)
            tot = ps[1][:, :].rearrange("p (m t e) -> p m e t", m=2, t=TILES)
            link(V.tensor_copy(tmp2.rearrange("p m t e -> p (m t e)").rearrange("p (m e t) -> p m e t", m=2, e=NE), tot))
            totf = tmp2.rearrange("p m t e -> p (m t e)")
            link(V.tensor_tensor_scan(pref.rearrange("p e t -> p (e t)"), seg.rearrange("p e t -> p (e t)"), totf,
                                      0.0, ALU.mult, ALU.add))
            tot1 = pref[:, 0:NE, TILES - 1:TILES]
            link(V.tensor_tensor(seg.rearrange("p e t -> p (e t)"), pref.rearrange("p e t -> p (e t)"), totf, ALU.subtract))
            link(V.tensor_tensor(seg[:, NE:2 * NE, :], seg[:, NE:2 * NE, :], tot1.to_broadcast([P, NE, TILES]), ALU.add))
            link(V.tensor_tensor(tmp2, ps[0][:, :].rearrange("p (m t e) -> p m t e", m=2, t=TILES),
                                 seg.rearrange("p (m e) t -> p m t e", m=2), ALU.add))
            link(V.tensor_tensor(tmp2, tmp2, mask, ALU.mult))
            link(V.tensor_reduce(loc[:], tmp2, AX.X, ALU.add))
            link(V.tensor_scalar(keep[:], loc[:], float(CAP), None, ALU.is_lt))
            link(V.tensor_scalar(loc[:], loc[:], float(CAP - 1), None, ALU.min))
            link(V.scalar_tensor_tensor(fidx[:], eidx[:], float(CAP), loc[:], ALU.mult, ALU.add))
            link(V.tensor_copy(fi32[:], fidx[:]))
            link(V.tensor_scalar(lo_i, fi32[:], P - 1, None, ALU.bitwise_and))
            link(V.tensor_scalar(hi_i, fi32[:], 7, None, ALU.logical_shift_right))
            link(V.tensor_copy(slo, lo_i))
            link(V.tensor_copy(shi, hi_i))
            link(V.tensor_scalar(pk, keep[:], pcol[:, 0:1], None, ALU.mult))
            link(V.tensor_tensor(tk, keep[:], iot[:, None, 0:TILES].to_broadcast([P, 2, TILES]), ALU.mult))
            for i in range(16):
                m, t = i // 8, 4 * (i % 8)
                if i >= 2:
                    dve.wait_ge(oh_used, i - 1)
                link(V.tensor_tensor(ohlo[:, i % 2], iot[:, None, :].to_broadcast([P, 4, P]),
                                     slo[:, m, t:t + 4, None].to_broadcast([P, 4, P]), ALU.is_equal))
                link(V.tensor_tensor(ohhi[:, i % 2], iot[:, None, None, 0:64].to_broadcast([P, 4, 2, 64]),
                                     shi[:, m, t:t + 4, None, None].to_broadcast([P, 4, 2, 64]), ALU.is_equal))
                V.tensor_tensor(ohhi[:, i % 2, :, 0, :], ohhi[:, i % 2, :, 0, :],
                                pk[:, m, t:t + 4, None].to_broadcast([P, 4, 64]), ALU.mult).then_inc(dve_step, 1)
                cnt[0] += 1
                V.tensor_tensor(ohhi[:, i % 2, :, 1, :], ohhi[:, i % 2, :, 1, :],
                                tk[:, m, t:t + 4, None].to_broadcast([P, 4, 64]), ALU.mult).then_inc(oh_ready, 1)
            dve.wait_ge(oh_used, 16)
            dve.wait_ge(ex_done, 2)
            link(V.tensor_copy(tmp[:, 0].rearrange("p t e -> p (t e)")[:, 0:P], ps[6][:, 0:P]))
            t0 = tmp[:, 0].rearrange("p t e -> p (t e)")
            link(V.scalar_tensor_tensor(tblf, t0[:, 64:128], float(P), t0[:, 0:64], ALU.mult, ALU.add))
            link(V.tensor_copy(tbl[:], tblf))
            for r in range(2):
                V.tensor_copy(sidx[:, r, :], tbl[:, 8 * r:8 * r + 8]).then_inc(sidx_ready, 1)
            link(V.tensor_reduce(gt[:, 0, :], ex, AX.X, ALU.add))
            link(V.reciprocal(gt[:, 1, :], gt[:, 0, :]))
            link(V.tensor_tensor(gt[:, 2, :], gt[:, 2, :], gt[:, 1, :], ALU.mult))
            link(V.tensor_tensor(gt[:, 3, :], gt[:, 1, :], gt[:, 2, :], ALU.add))
            link(V.tensor_scalar(gt[:, 3, :], gt[:, 3, :], 1e-9, None, ALU.max))
            link(V.reciprocal(gt[:, 0, :], gt[:, 3, :]))
            link(V.tensor_tensor(gk[:], gt[:, 1:3, :], gt[:, 0:1, :].to_broadcast([P, 2, TILES]), ALU.mult))
            link(V.tensor_tensor(gk[:], gk[:], keep[:], ALU.mult))

            def rows_in(e, r):
                for i in range(4):
                    dve.wait_ge(xgt_done, 4 * e + i + 1)
                    V.tensor_copy(XT[:, r, :, 2 * i * P:(2 * i + 2) * P], ps[i % 2][:, :].rearrange("p (k n) -> p k n", k=KD))\
                        .then_inc(xgt_ready, 1)

            def next_idx(e, r):
                dve.wait_ge(xgt_done, 4 * e - 4)
                V.tensor_copy(sidx[:, r, :], tbl[:, bass.ds(8 * e, 8)]).then_inc(sidx_ready, 1)

            def eo_out(e, r):
                for i in range(4):
                    dve.wait_ge(dn_done, 4 * e + i + 1)
                    if not (isinstance(e, int) and e == 0):
                        dve.wait_ge(eo_stored[i], 16 * e)
                    V.tensor_copy(eos[:, i].rearrange("p s d -> p (s d)"), ps[6 + i % 2][:]).then_inc(eo_ready, 1)

            rows_in(0, 0)
            for r in range(2):
                rows_in(r + 1, 1 - r)
                next_idx(r + 2, r)
                eo_out(r, r)
            with dve.Fori(1, NE // 2 - 1) as u:
                for r in range(2):
                    e = 2 * u + r
                    rows_in(e + 1, 1 - r)
                    next_idx(e + 2, r)
                    eo_out(e, r)
            rows_in(NE - 1, 1)
            for r in range(2):
                eo_out(NE - 2 + r, r)

            def set_cidx(i, r):
                V.tensor_copy(cidx[:, r], fi32[:, :, bass.ds(4 * i, 4)]).then_inc(cidx_ready, 1)

            def combine(i, r):
                dve.wait_ge(g_loaded[r], 64 * (i - r) + 128)
                for w in range(2):
                    for t in range(4):
                        xt = x_sb[:, bass.ds(4 * i + t, 1), :].rearrange("p t d -> p (t d)")
                        a = V.scalar_tensor_tensor(xt, G[:, r, t, w, :], gk[:, w, bass.ds(4 * i + t, 1)], xt, ALU.mult, ALU.add)
                        if w == 0:
                            a.then_inc(dve_acc, 1)
                    if w == 0:
                        dve.wait_ge(dve_acc, 4 * i + 4)
                a.then_inc(y_ready, 1)

            for r in range(2):
                set_cidx(r, r)
            with dve.Fori(0, TILES // 8 - 1) as u:
                for r in range(2):
                    combine(2 * u + r, r)
                    set_cidx(2 * u + r + 2, r)
            for r in range(2):
                combine(TILES // 4 - 2 + r, r)


_INS = ["L0_attn_x", "L0_attn_W_Q", "L0_attn_W_K", "L0_attn_W_V", "L0_attn_W_O", "L0_ffn_wg", "L0_ffn_w_gate", "L0_ffn_w_down"]


def kernel(**inputs):
    import numpy as _np
    import concourse.bacc as _bacc
    from concourse import mybir as _mybir
    from concourse.bass_utils import run_bass_kernel_spmd as _run

    nc = _bacc.Bacc("TRN2", target_bir_lowering=False, num_devices=1)
    arrays, args = {}, []
    for name in _INS:
        a = _np.ascontiguousarray(inputs[name])
        arrays[f"in_{name}_dram"] = a
        args.append(nc.dram_tensor(f"in_{name}_dram", a.shape, _mybir.dt.from_np(a.dtype), kind="ExternalInput").ap())
    args.append(nc.dram_tensor("out_0_dram", (BATCH, SEQ, DM), _mybir.dt.float32, kind="ExternalOutput").ap())
    scratch = [nc.dram_tensor("v_rows", (SEQ, BATCH, DM), _mybir.dt.float32, kind="Internal").ap(),
               nc.dram_tensor("xn2_rows", (TOK, DM), _mybir.dt.float32, kind="Internal").ap(),
               nc.dram_tensor("eo_rows", (NE * CAP, DM), _mybir.dt.float32, kind="Internal").ap(),
               nc.dram_tensor("sel_d", (NBLK, 8), _mybir.dt.uint32, kind="Internal").ap()]
    build(nc, *args, scratch)
    r = _run(nc, [arrays], core_ids=[0])
    return r.results[0]["out_0_dram"]
```

```python
from contextlib import ExitStack

import concourse.bass as bass
from concourse import mybir

ALU = mybir.AluOpType
ACT = mybir.ActivationFunctionType
AX = mybir.AxisListType
F32 = mybir.dt.float32
F16 = mybir.dt.float16
I32 = mybir.dt.int32
U32 = mybir.dt.uint32

P = 128
P_SCALE = 2.0 ** 12
N_CONSTS = 8
LN_EPS = 1e-5
BATCH, SEQ, DM = 4, 1024, 256
TOK = BATCH * SEQ
TILES = TOK // P
HEADS, HD = 16, 16
BLK = 32
NBLK = SEQ // BLK
TOPK = int(0.2 * NBLK)
GROUPS = SEQ // P
KEYS = TOPK * BLK
HALFK = KEYS // 2
KD = DM // P
NE, FF = 8, 1024
CAP = 2 * TOK // NE
SLOT_TILES = NE * CAP // P
FCH = FF // P
PARTS = ((0, 0), (0, 1), (1, 0))
HS = 8
GHS = 4 * HS
NEG = -3.0e38


def build(nc, x_d, wq_d, wk_d, wv_d, wo_d, wg_d, up_d, down_d, out_d, scratch):
    v_rows, xn2_rows, y_rows, sel_d = scratch
    with ExitStack() as ctx:
        def sb(name, shape, dt=F32):
            return ctx.enter_context(nc.sbuf_tensor(name, shape, dt))

        def sem(name):
            return ctx.enter_context(nc.semaphore(name))

        x_sb = sb("x_sb", [P, TILES, DM])
        kq = sb("kq", [P, 2 * 8192])
        QT = kq[:, 0:8192].rearrange("p (h b n) -> p h b n", h=2, b=BATCH)
        KT = kq[:, 8192:16384].rearrange("p (k h b n) -> p k h b n", k=NBLK, h=2, b=BATCH)
        Xg = kq[:, 0:4096].rearrange("p (r s d) -> p r s d", r=2, s=8)
        XT = kq[:, 4096:8192].bitcast(F16).rearrange("p (r k l n) -> p r k l n", r=2, k=KD, l=2)
        hT = kq[:, 8192:16384].bitcast(F16).rearrange("p (c f l n) -> p c f l n", c=2, f=FCH, l=2)
        Y = kq[:, :].rearrange("p (w t d) -> p w t d", w=2, t=TILES)
        gath = sb("gath", [P, 2 * 1536 + 2 * 2048])
        Ksel = gath[:, 0:3072].rearrange("p (r j h b n) -> p r j h b n", r=2, j=TOPK, h=2, b=BATCH)
        Vsel = gath[:, 3072:7168].bitcast(F16).rearrange("p (r c b l d) -> p r c b l d", r=2, c=2, b=BATCH, l=2)
        work = sb("work", [P, 2 * 2048 + 2 * 384 + 2 * 512 + 1024 + 1024])
        Qbd = work[:, 0:4096].rearrange("p (r h b e n) -> p r h b e n", r=2, h=2, b=BATCH, e=8)
        Pr = work[:, 4096:4864].rearrange("p (r c n) -> p r c n", r=2, c=2)
        PT = work[:, 4864:5888].bitcast(F16).rearrange("p (r l c k n) -> p r l c k n", r=2, l=2, c=2, k=2)
        On = work[:, 5888:6912].rearrange("p (b d) -> p b d", b=BATCH)
        OT = work[:, 6912:7936].rearrange("p (b k n) -> p b k n", b=BATCH, k=KD)
        xn = work[:, 0:2048].rearrange("p (r j d) -> p r j d", r=2, j=4)
        xnT = work[:, 2048:4096].rearrange("p (r k n) -> p r k n", r=2, k=KD)
        vst = work[:, 4096:6144].bitcast(F16).rearrange("p (r j l d) -> p r j l d", r=2, j=4, l=2)
        ohlo = work[:, 0:512].bitcast(F16).rearrange("p (r q n) -> p r q n", r=2, q=4)
        ohhi = work[:, 512:768].bitcast(F16).rearrange("p (r q n) -> p r q n", r=2, q=4)
        ohtok = work[:, 768:1280].bitcast(F16).rearrange("p (r q w n) -> p r q w n", r=2, q=4, w=2)
        iot16 = work[:, 1280:1344].bitcast(F16)
        eos = work[:, 2048:4096].rearrange("p (r s d) -> p r s d", r=4, s=2)
        wgt = sb("wgt", [P, 4 * 2048])
        wup = wgt[:, 0:4096].bitcast(F16).rearrange("p (r k l f) -> p r k l f", r=2, k=KD, l=2)
        wdn = wgt[:, 4096:8192].bitcast(F16).rearrange("p (r f l d) -> p r f l d", r=2, f=FCH, l=2)
        stage = ((gath[:, 4096:6144], work[:, 0:2048]), (gath[:, 0:2048], gath[:, 2048:4096]))
        stage_first = (wgt[:, 2048:4096], wgt[:, 6144:8192])
        h32 = work[:, 4096:6144].rearrange("p (r n) -> p r n", r=4)
        wproj = sb("wproj", [P, 4, KD, DM])
        wgate = sb("wgate", [P, KD, NE])
        ident = sb("ident", [P, P])
        tri = sb("tri", [P, P])
        ones = sb("ones", [P, P])
        hmask = sb("hmask", [P, 8])[:, :]
        iot_i = gath[:, 0:P].bitcast(I32)
        iot = sb("iot", [P, P])
        pcol_i = gath[:, P:P + 1].bitcast(I32)
        pcol = sb("pcol", [P, 1])
        small = sb("small", [P, 768])
        xnp = small[:, 0:256].rearrange("p (k b n) -> p k b n", k=KD, b=BATCH)
        qkp = small[:, 256:768].rearrange("p (w h b n) -> p w h b n", w=2, h=2, b=BATCH)
        zeros = small[:, 0:256]
        slo, shi = (small[:, 64 * i:64 * i + 32].bitcast(F16).rearrange("p (m t) -> p m t", m=2) for i in range(2))
        yk = small[:, 128:192].bitcast(F16).rearrange("p (m t w) -> p m t w", m=2, w=2)
        lo_i, hi_i = (small[:, 256 + 64 * i:320 + 64 * i].bitcast(U32).rearrange("p (m t) -> p m t", m=2) for i in range(2))
        gt = small[:, 384:512].rearrange("p (q t) -> p q t", q=4)
        avg = sb("avg", [NBLK, NBLK])
        top8 = sb("top8", [NBLK, 8])
        idx8 = sb("idx8", [NBLK, 8], U32)
        st = sb("st", [P, 4, 6])
        mv = sb("mv", [P, 4, 2])
        rstd = sb("rstd", [P, 4])
        mhalf = sb("mhalf", [P, 4])
        epst = sb("epst", [P, 4])
        carrier = sb("carrier", [P, 1])
        carrier_v = sb("carrier_v", [P, 1])
        negmax = sb("negmax", [P, 2, 2])
        rsum = sb("rsum", [P, 2, 2, 4])
        rinv = sb("rinv", [P, 2, 4])
        xn2 = sb("xn2", [P, 2, DM])
        xn2T = sb("xn2T", [P, 2, KD, P])
        xn2_slot = [xn2[:, 0, :], xn2[:, 1, :], work[:, 0:256], work[:, 256:512]]
        xn2T_slot = [xn2T[:, i] for i in range(2)] + \
            [work[:, i:i + 256].rearrange("p (k n) -> p k n", k=KD) for i in (512, 768)]
        L = sb("L", [P, TILES, NE])
        mx = sb("mx", [P, 2, TILES])
        route = gath[:, 4096:7168]
        mask, tmp, tmp2 = (route[:, 512 * i:512 * i + 512].rearrange("p (m t e) -> p m t e", m=2, t=TILES) for i in range(3))
        ex = route[:, 1536:1792].rearrange("p (t e) -> p t e", t=TILES)
        tblf = route[:, 2816:2816 + SLOT_TILES]
        tblp = route[:, 2880:2880 + 2 * SLOT_TILES]
        seg, pref = (route[:, i:i + 512].rearrange("p (e t) -> p e t", t=TILES) for i in (1792, 2304))
        eidx = sb("eidx", [P, 2, TILES])
        loc = sb("loc", [P, 2, TILES])
        keep = sb("keep", [P, 2, TILES])
        fidx = sb("fidx", [P, 2, TILES])
        fi32 = sb("fi32", [P, 2, TILES], U32)
        gk = sb("gk", [P, 2, TILES])
        tbl = small[:, 512:576].bitcast(U32)
        ytbl = small[:, 576:640].bitcast(U32)
        sidx = sb("sidx", [P, 2, 8], U32)
        yidx = sb("yidx", [P, 2, 8], U32)
        wstat = sb("wstat", [P, 32])
        wmax = wstat[:, 0:8]
        wmax2 = wstat[:, 8:10]
        wpow = wstat[0:2, 10:11]
        wdiag = wstat[0:2, 12:14]
        wpow_all, wpow_inv = wstat[:, 14:16], wstat[:, 16:18]
        scl = wstat[:, 20:30].rearrange("p (r n) -> p r n", r=2)

        ps = [ctx.enter_context(nc.psum_tensor(f"ps{i}", [P, 512], F32)) for i in range(8)]
        Sp = [ps[i][:, 0:2 * KEYS].rearrange("p (c n) -> p c n", c=2) for i in (0, 1)]
        PTp = [ps[i][:, :].rearrange("p (c k n) -> p c k n", c=2, k=2) for i in (2, 3)]
        Op = [ps[i][:, :].rearrange("p (b c d) -> p b c d", b=2, c=4) for i in (4, 5)]
        Mp = [ps[i] for i in (6, 7, 0, 1)]

        x_loaded = [sem(f"x_loaded{i}") for i in range(2)]
        w_loaded = sem("w_loaded")
        consts = sem("consts")
        pool_step = sem("pool_step")
        dve_step = sem("dve_step")
        stats_ready = sem("stats_ready")
        vareps_ready = sem("vareps_ready")
        carried = sem("carried")
        rstd_ready = sem("rstd_ready")
        dve_recip = sem("dve_recip")
        dve_ln = sem("dve_ln")
        dve_acc = sem("dve_acc")
        xn_ready = sem("xn_ready")
        xt_done = sem("xt_done")
        xnt_ready = sem("xnt_ready")
        proj_done = sem("proj_done")
        projc_act = sem("projc_act")
        projc_dve = sem("projc_dve")
        vp_done = sem("vp_done")
        wv_scaled = sem("wv_scaled")
        wo_scaled = sem("wo_scaled")
        vhi_ready = sem("vhi_ready")
        vst_ready = sem("vst_ready")
        v_stored = [sem(f"v_stored{i}") for i in range(2)]
        xnp_ready = sem("xnp_ready")
        pool_mm = sem("pool_mm")
        pooled_ready = sem("pooled_ready")
        avg_done = sem("avg_done")
        sel_ready = sem("sel_ready")
        sel_stored = sem("sel_stored")
        ksel_loaded = [sem(f"ksel_loaded{i}") for i in range(2)]
        vsel_loaded = [sem(f"vsel_loaded{i}") for i in range(2)]
        qbd_ready = sem("qbd_ready")
        qk_done = sem("qk_done")
        max_done = sem("max_done")
        exp_done = sem("exp_done")
        pt_done = sem("pt_done")
        pt_high = sem("pt_high")
        pt_ready = sem("pt_ready")
        pv_done = sem("pv_done")
        o_ready = sem("o_ready")
        ot_done = sem("ot_done")
        ot_ready = sem("ot_ready")
        oproj_done = sem("oproj_done")
        xn2_ready = sem("xn2_ready")
        xn2_stored = [sem(f"xn2_stored{i}") for i in range(2)]
        xn2t_done = sem("xn2t_done")
        xn2t_ready = sem("xn2t_ready")
        lg_done = sem("lg_done")
        lg_ready = sem("lg_ready")
        ex_in = sem("ex_in")
        ex_done = sem("ex_done")
        masks_ready = sem("masks_ready")
        prefix_done = sem("prefix_done")
        ohlo_ready = sem("ohlo_ready")
        ohtok_ready = sem("ohtok_ready")
        oh_used = sem("oh_used")
        sidx_ready = sem("sidx_ready")
        xg_loaded = [[sem(f"xg_loaded{i}{j}") for j in range(2)] for i in range(2)]
        xgt_done = sem("xgt_done")
        xgt_ready = sem("xgt_ready")
        w_staged_first = sem("w_staged_first")
        w_staged = [sem(f"w_staged{i}") for i in range(2)]
        route_done = sem("route_done")
        wstat_step = sem("wstat_step")
        wmax_ready = sem("wmax_ready")
        wmax_turned = sem("wmax_turned")
        wdiag_ready = sem("wdiag_ready")
        wpow_spread = sem("wpow_spread")
        scl_ready = sem("scl_ready")
        whi_ready = sem("whi_ready")
        wlo_ready = sem("wlo_ready")
        xhi_ready = sem("xhi_ready")
        gelu_done = sem("gelu_done")
        hhi_ready = sem("hhi_ready")
        up_done = sem("up_done")
        h_ready = sem("h_ready")
        dn_done = sem("dn_done")
        eo_ready = sem("eo_ready")
        y_scattered = [sem(f"y_scattered{i}") for i in range(4)]
        yidx_ready = sem("yidx_ready")
        zeros_ready = sem("zeros_ready")
        y_zeroed = sem("y_zeroed")
        ohhi_ready = sem("ohhi_ready")
        y_loaded = [[sem(f"y_loaded{w}{i}") for i in range(TILES // 4)] for w in range(2)]
        y_ready = sem("y_ready")
        out_stored = sem("out_stored")

        x_v = x_d.rearrange("b (t p) d -> p (b t) d", p=P)
        out_v = out_d.rearrange("b (t p) d -> p (b t) d", p=P)
        v_v = v_rows.rearrange("(t p) b l d -> p t b (l d)", p=P)
        xn2_v = xn2_rows.rearrange("(t p) d -> p t d", p=P)
        y_v = y_rows.rearrange("(t p) d -> p t d", p=P)
        LN_STEPS = 4
        BASES, LAST_BASES = (6, 11, 16, 21), (6, 7, 8, 9)
        N_PROJ_ACT = 3

        block = ctx.enter_context(nc.Block())

        def wait_count(eng, semaphore, count):
            if not (isinstance(count, int) and count == 0):
                eng.wait_ge(semaphore, count)

        def load_y(eng, w):
            for s in range(4):
                eng.wait_ge(y_scattered[s], 32 * NE)
            for i in range(TILES // 4):
                t = 1 + w * TILES + 4 * i
                eng.dma_start(Y[:, w, 4 * i:4 * i + 4, :], y_v[:, t:t + 4, :]).then_inc(y_loaded[w][i], 16)

        @block.sync
        def _(sp):
            for i, w in enumerate((wk_d, wq_d, wv_d, wo_d)):
                if i == 0:
                    sp.dma_start(x_sb[:, 0:4, :], x_v[:, 0:4, :]).then_inc(x_loaded[0], 16)
                slot = (1, 0, 2, 3)[i]
                sp.dma_start(wproj[:, slot], w.rearrange("(k p) n -> p k n", p=P)).then_inc(w_loaded, 16)
                if i == 0:
                    sp.dma_start(x_sb[:, 4:8, :], x_v[:, 4:8, :]).then_inc(x_loaded[1], 16)
            sp.dma_start(wgate[:], wg_d.rearrange("(k p) e -> p k e", p=P)).then_inc(w_loaded, 16)

            def load_expert(e, halves, signal):
                up_half, down_half = halves
                sp.dma_start(up_half.rearrange("p (k f) -> p k f", k=KD),
                             up_d[bass.ds(e, 1)].rearrange("e (k p) f -> p (e k) f", p=P)).then_inc(signal, 16)
                sp.dma_start(down_half.rearrange("p (f d) -> p f d", f=FCH),
                             down_d[bass.ds(e, 1)].rearrange("e (f p) d -> p (e f) d", p=P)).then_inc(signal, 16)

            def store_v(b, r):
                sp.wait_ge(vst_ready, 4 * b + 2 * r + 2)
                sp.dma_start(v_v[:, 4 * r:4 * r + 4, bass.ds(b, 1), :].rearrange("p t b d -> p t (b d)"),
                             vst[:, r].rearrange("p j l d -> p j (l d)")).then_inc(v_stored[r], 16)

            with sp.Fori(0, BATCH - 1) as b:
                for r in range(2):
                    sp.wait_ge(x_loaded[r], 16 * b + 16)
                    sp.dma_start(x_sb[:, bass.ds(8 * b + 8 + 4 * r, 4), :],
                                 x_v[:, bass.ds(8 * b + 8 + 4 * r, 4), :]).then_inc(x_loaded[r], 16)
                for r in range(2):
                    store_v(b, r)
            for r in range(2):
                store_v(BATCH - 1, r)
            load_expert(0, stage_first, w_staged_first)

            sp.wait_ge(sel_ready, 1)
            sp.dma_start(sel_d, idx8[:]).then_inc(sel_stored, 16)
            sp.wait_ge(sel_stored, 16)
            for r in range(2):
                sp.wait_ge(v_stored[r], 16 * BATCH)

            def gather(t, r):
                _, blocks = nc.values_load_multi_w_load_instructions(
                    sel_d[bass.ds(t, 1), 0:TOPK], engines=(mybir.EngineType.SP,), min_val=0, max_val=NBLK - 1)
                if not isinstance(t, int):
                    sp.wait_ge(qk_done, HS * t - HS)
                for j, blk in enumerate(blocks):
                    sp.dma_start(Ksel[:, r, j].rearrange("p h b n -> p (h b n)"),
                                 KT[:, bass.ds(blk, 1)].rearrange("p k h b n -> p (k h b n)"))\
                        .then_inc(ksel_loaded[r], 16)
                if not isinstance(t, int):
                    sp.wait_ge(pv_done, HS * t - HS)
                for j, blk in enumerate(blocks):
                    q = 32 * (j % 3)
                    sp.dma_start(Vsel[q:q + 32, r, j // 3].rearrange("p b l d -> p (b l d)"),
                                 v_rows[bass.ds(blk * BLK, BLK)].rearrange("n b l d -> n (b l d)"))\
                        .then_inc(vsel_loaded[r], 16)

            sp.wait_ge(projc_act, N_PROJ_ACT * 2 * BATCH)
            for r in range(2):
                gather(r, r)

            def zero_y(u):
                sp.dma_start(y_v[:, bass.ds(4 * u + 1, 4), :], zeros[:, None, :].to_broadcast([P, 4, DM])).then_inc(y_zeroed, 16)

            sp.wait_ge(zeros_ready, 1)
            zero_y(0)
            with sp.Fori(1, NBLK // 2) as u:
                for r in range(2):
                    gather(2 * u + r, r)
                zero_y(u)

            sp.wait_ge(pv_done, HS * NBLK)
            load_expert(1, stage[1], w_staged[1])
            sp.wait_ge(route_done, 1)
            load_expert(2, stage[0], w_staged[0])
            sp.wait_ge(wlo_ready, 4)
            load_expert(3, stage[1], w_staged[1])
            with sp.Fori(2, NE // 2) as u:
                for r in range(2):
                    sp.wait_ge(wlo_ready, 4 * u + 2 * r - 2)
                    load_expert(2 * u + r, stage[r], w_staged[r])
            load_y(sp, 0)
            sp.wait_ge(out_stored, 16 * (TILES // 4))
            for r in range(2):
                sp.wait_ge(xn2_stored[r], 16 * TILES // 2)

        @block.gpsimd
        def _(pool):
            nc.gpsimd.memset(ident[:], 0.0).then_inc(pool_step, 1)
            nc.gpsimd.memset(tri[:], 1.0).then_inc(pool_step, 1)
            nc.gpsimd.memset(hmask, float(HD) ** -0.5).then_inc(pool_step, 1)
            nc.gpsimd.memset(ones[:], 1.0).then_inc(consts, 1)
            nc.gpsimd.memset(mhalf[:], -0.5).then_inc(consts, 1)
            nc.gpsimd.memset(epst[:], LN_EPS).then_inc(consts, 1)
            nc.gpsimd.memset(carrier[:], 0.0).then_inc(carried, 1)
            nc.gpsimd.iota(iot_i, pattern=[[1, P]], base=0, channel_multiplier=0).then_inc(pool_step, 1)
            nc.gpsimd.iota(pcol_i, pattern=[[0, 1]], base=0, channel_multiplier=1).then_inc(pool_step, 1)
            pool.wait_ge(pool_step, 5)
            nc.gpsimd.affine_select(out=ident[:], in_=ident[:], compare_op=ALU.not_equal, fill=1.0, base=0,
                                    pattern=[[-1, P]], channel_multiplier=1).then_inc(consts, 1)
            nc.gpsimd.affine_select(out=tri[:], in_=tri[:], compare_op=ALU.is_ge, fill=0.0, base=-1,
                                    pattern=[[1, P]], channel_multiplier=-1).then_inc(consts, 1)
            nc.gpsimd.affine_select(out=hmask, in_=hmask, compare_op=ALU.is_ge, fill=0.0, base=0,
                                    pattern=[[-HD, 8]], channel_multiplier=1).then_inc(pool_step, 1)
            pool.wait_ge(pool_step, 6)
            nc.gpsimd.affine_select(out=hmask, in_=hmask, compare_op=ALU.is_ge, fill=0.0, base=HD - 1,
                                    pattern=[[HD, 8]], channel_multiplier=-1).then_inc(consts, 1)
            nc.gpsimd.tensor_copy(iot[:], iot_i).then_inc(consts, 1)
            nc.gpsimd.tensor_copy(pcol[:], pcol_i).then_inc(consts, 1)
            pool.wait_ge(consts, N_CONSTS)

            def inv_sqrt(n, var, eps, half, out):
                nc.gpsimd.tensor_tensor(out, var, eps, ALU.add).then_inc(vareps_ready, 1)
                pool.wait_ge(vareps_ready, n + 1)
                nc.gpsimd.tensor_tensor(out, out, half, ALU.pow).then_inc(rstd_ready, 1)

            with pool.Fori(0, 2 * BATCH) as c:
                pool.wait_ge(stats_ready, c + 1)
                inv_sqrt(c, mv[:, :, 1], epst[:], mhalf[:], rstd[:])

            def spread_q(t, r):
                src = QT[:, :, :, bass.ds(t * BLK, BLK)].rearrange("p h b n -> p (h b) n")
                dst = Qbd[:, r].rearrange("p h b e n -> p (h b) e n")
                nc.gpsimd.tensor_tensor(
                    dst, src[:, :, None, :].to_broadcast([P, 8, 8, BLK]),
                    hmask[:, None, :, None].to_broadcast([P, 8, 8, BLK]), ALU.mult).then_inc(qbd_ready, 1)

            pool.wait_ge(pool_mm, 1)
            nc.gpsimd.memset(zeros, 0.0).then_inc(zeros_ready, 1)
            pool.wait_ge(projc_act, N_PROJ_ACT * 2 * BATCH)
            pool.wait_ge(projc_dve, 2 * BATCH)
            pool.wait_ge(vp_done, 4 * BATCH)
            pool.wait_ge(vst_ready, 4 * BATCH)
            for r in range(2):
                pool.wait_ge(v_stored[r], 16 * BATCH)
            for r in range(2):
                spread_q(r, r)

            def spread_next(t, r):
                pool.wait_ge(qk_done, HS * t - HS)
                spread_q(t, r)

            def rstd_of(n, b):
                pool.wait_ge(stats_ready, 2 * BATCH + n + 1)
                inv_sqrt(2 * BATCH + n, mv[:, b, 1:2], epst[:, 0:1], mhalf[:, 0:1], rstd[:, b:b + 1])

            def group(g, first, last):
                for what, n in (("q", 2), ("r", 0), ("r", 1), ("q", 3), ("r", 2), ("q", 4), ("r", 3), ("q", 5)):
                    if what == "q" and not (last and n >= 4):
                        spread_next(4 * g + n, n % 2)
                    if what == "r" and not first:
                        rstd_of(4 * (g - 1) + n, n)

            group(0, True, False)
            group(1, False, False)
            with pool.Fori(2, GROUPS - 1) as g:
                group(g, False, False)
            group(GROUPS - 1, False, True)
            for b in range(BATCH):
                rstd_of(4 * (GROUPS - 1) + b, b)

            def carry_pool(n):
                pool.wait_ge(carried, n + 1)
                nc.gpsimd.tensor_tensor(carrier[0:1, :], mhalf[0:1, 0:1], epst[0:1, 0:1], ALU.add).then_inc(carried, 1)

            for i in range(16):
                m, t = i // 8, 4 * (i % 8)
                pool.wait_ge(ohhi_ready, i + 1)
                if i >= 2:
                    pool.wait_ge(oh_used, i - 1)
                nc.gpsimd.tensor_tensor(ohtok[:, i % 2], ohhi[:, i % 2, :, None, :].to_broadcast([P, 4, 2, 64]),
                                        yk[:, m, t:t + 4, :, None].to_broadcast([P, 4, 2, 64]),
                                        ALU.mult).then_inc(ohtok_ready, 1)

            def gather_tokens(e, r, n):
                pool.wait_ge(sidx_ready, e + 1)
                carry_pool(n)
                for s in range(8):
                    nc.gpsimd.indirect_dma_start(
                        out=Xg[:, r, s, :], out_offset=None, in_=xn2_rows,
                        in_offset=bass.IndirectOffsetOnAxis(ap=sidx[:, r, s:s + 1], axis=0))\
                        .then_inc(xg_loaded[r][s // 4], 16)

            def scatter_rows(e, r, n):
                pool.wait_ge(yidx_ready, e + 1)
                for i in range(4):
                    pool.wait_ge(eo_ready, 4 * e + i + 1)
                    carry_pool(n + i)
                    for s in range(2):
                        nc.gpsimd.indirect_dma_start(
                            out=y_rows, out_offset=bass.IndirectOffsetOnAxis(ap=yidx[:, r, 2 * i + s:2 * i + s + 1], axis=0),
                            in_=eos[:, i, s, :], in_offset=None).then_inc(y_scattered[i], 16)

            for r in range(2):
                pool.wait_ge(xn2_stored[r], 16 * TILES // 2)
            for r in range(2):
                gather_tokens(r, r, r)
            pool.wait_ge(y_zeroed, 16 * (NBLK // 2))
            with pool.Fori(0, NE // 2 - 1) as u:
                for r in range(2):
                    scatter_rows(2 * u + r, r, 10 * u + 5 * r + 2)
                    gather_tokens(2 * u + r + 2, r, 10 * u + 5 * r + 6)
            for r in range(2):
                scatter_rows(NE - 2 + r, r, 5 * (NE - 2) + 4 * r + 2)

        @block.scalar
        def _(act):
            def rows_turned(c, r):
                act.wait_ge(xt_done, c + 1)
                for k in range(KD):
                    nc.scalar.copy(xnT[:, r, k, :], ps[k][:]).then_inc(xnt_ready, 1)

            def project(b, last):
                for r in range(2):
                    c = 2 * b + r
                    for h in range(2):
                        act.wait_ge(proj_done, 4 * c + h + 1)
                        nc.scalar.copy(KT[:, 16 * r:16 * r + 16, h, bass.ds(b, 1), :].rearrange("p k b n -> p k (b n)"),
                                       ps[2 + h][:, :].rearrange("p (k n) -> p k n", n=BLK)).then_inc(projc_act, 1)
                    act.wait_ge(proj_done, 4 * c + 3)
                    nc.scalar.copy(QT[:, 0, bass.ds(b, 1), 512 * r:512 * r + 512].rearrange("p b n -> p (b n)"),
                                   ps[4][:]).then_inc(projc_act, 1)
                    if not (last and r == 1):
                        rows_turned(c + 1, 1 - r)
                    wait_count(act, v_stored[r], 16 * b)
                    for i in range(2):
                        act.wait_ge(vp_done, 2 * c + i + 1)
                        nc.scalar.copy(vst[:, r, 2 * i:2 * i + 2, 0, :], ps[6 + i][:, :].rearrange("p (j d) -> p j d", j=2))\
                            .then_inc(vhi_ready, 1)

            rows_turned(0, 0)
            project(0, False)
            with act.Fori(1, BATCH - 1) as b:
                project(b, False)
            project(BATCH - 1, True)

            def split_high(e, r, halves):
                act.wait_ge(scl_ready, 4 * e + 4)
                nc.scalar.mul(wup[:, r, :, 0, :], halves[0].rearrange("p (k f) -> p k f", k=KD), scl[:, r, 0:1])\
                    .then_inc(whi_ready, 1)
                nc.scalar.mul(wdn[:, r, :, 0, :], halves[1].rearrange("p (f d) -> p f d", f=FCH), scl[:, r, 1:2])\
                    .then_inc(whi_ready, 1)

            split_high(0, 0, stage_first)

            def exps(hs, r, b, h, t4):
                w = (2 * t4 + b // 2) % 2
                act.wait_ge(max_done, hs + 1)
                for c in range(2):
                    a = nc.scalar.activation(Pr[:, r, c, :], Sp[r][:, c, :], ACT.Exp, bias=negmax[:, r, c:c + 1],
                                             accum_out=rsum[:, w, b % 2, 2 * h + c:2 * h + c + 1])
                a.then_inc(exp_done, 1)

            def turned_high(hs, r):
                act.wait_ge(pt_done, hs + 1)
                nc.scalar.mul(PT[0:HALFK, r, 0], PTp[r][0:HALFK], P_SCALE).then_inc(pt_high, 1)

            def out_steps(g, k, tail=False):
                if k in (5, 6):
                    i = k - 5
                    act.wait_ge(ot_done, 2 * g + i + 1)
                    nc.scalar.copy(OT[:, 2 * i:2 * i + 2].rearrange("p b k n -> p (b k n)"), Mp[i][:])\
                        .then_inc(ot_ready, 1)
                for b in range(BATCH):
                    base, slot = (LAST_BASES[b], b) if tail else (BASES[b], b % 2)
                    if k == base + 6:
                        act.wait_ge(xn2t_done, 4 * g + b + 1)
                        nc.scalar.copy(xn2T_slot[slot].rearrange("p k n -> p (k n)"), Mp[slot][:, 256:512])\
                            .then_inc(xn2t_ready, 1)
                        act.wait_ge(xn2_ready, 4 * g + b + 1)
                        act.dma_start(xn2_v[:, bass.ds(8 * b + g, 1), :].rearrange("p t d -> p (t d)"), xn2_slot[slot])\
                            .then_inc(xn2_stored[b % 2], 16)

            def group(g, first, last):
                if first:
                    act.wait_ge(w_loaded, 16)
                    for k in range(2):
                        exps(k, k, 0, k, 0)
                for k in range(GHS):
                    hs = GHS * g + k
                    turned_high(hs, k % 2)
                    n = k + 2
                    if not (last and n >= GHS):
                        m = n % GHS
                        if m % 4 == 0 and not (first and n < 8):
                            act.wait_ge(dve_recip, 8 * g + n // 4 - 1)
                        exps(hs + 2, m % 2, (m % HS) // 2, m % 2, m // HS)
                    if not first:
                        out_steps(g - 1, k)

            group(0, True, False)
            group(1, False, False)
            with act.Fori(2, GROUPS - 1) as g:
                group(g, False, False)
            group(GROUPS - 1, False, True)
            for k in range(GHS):
                out_steps(GROUPS - 1, k, tail=True)

            act.wait_ge(ex_in, 1)
            nc.scalar.activation(ex, tmp[:, 0], ACT.Exp).then_inc(ex_done, 1)
            nc.scalar.activation(gt[:, 2, :], mx[:, 1, :], ACT.Exp).then_inc(ex_done, 1)

            def hidden_high(e, r, n):
                act.wait_ge(gelu_done, 16 * e + n + 1)
                nc.scalar.mul(hT[:, n // 8, n % 8, 0, :], h32[:, n % 4, :], scl[:, r, 2:3]).then_inc(hhi_ready, 1)

            def hidden(e, r):
                for n in range(16):
                    act.wait_ge(up_done, 16 * e + n + 1)
                    if not (isinstance(e, int) and e == 0 and n < 4):
                        act.wait_ge(h_ready, 16 * e + n - 3)
                    nc.scalar.activation(h32[:, n % 4, :], ps[2 + n % 4][:], ACT.Gelu, scale=scl[:, r, 3:4]).then_inc(gelu_done, 1)
                    if n:
                        hidden_high(e, r, n - 1)
                hidden_high(e, r, 15)

            hidden(0, 0)
            split_high(1, 1, stage[1])
            with act.Fori(0, NE // 2 - 1) as u:
                for r in range(2):
                    hidden(2 * u + r + 1, 1 - r)
                    split_high(2 * u + r + 2, r, stage[r])
            hidden(NE - 1, 1)

            load_y(act, 1)
            with act.Fori(0, TILES // 4) as i:
                act.wait_ge(y_ready, i + 1)
                act.dma_start(out_v[:, bass.ds(4 * i, 4), :], x_sb[:, bass.ds(4 * i, 4), :])\
                    .then_inc(out_stored, 16)

        @block.tensor
        def _(pe):
            pe.wait_ge(consts, N_CONSTS)
            pe.wait_ge(w_loaded, 16 * 5)
            def turn_maxima(n, bank):
                pe.wait_ge(wmax_ready, n + 1)
                nc.tensor.transpose(bank[0:2, 0:P], wmax2, ident[:]).then_inc(wmax_turned, 1)

            def spread_powers(n, bank):
                pe.wait_ge(wdiag_ready, n + 1)
                nc.tensor.matmul(bank[:, 0:2], ones[0:2, :], wdiag, start=True, stop=True).then_inc(wpow_spread, 1)

            def turn_chunk(c, r):
                pe.wait_ge(xn_ready, c + 1)
                wait_count(pe, xnt_ready, 2 * c)
                for k in range(KD):
                    for j in range(4):
                        mm = nc.tensor.transpose(ps[k][:, j * P:(j + 1) * P], xn[:, r, j, k * P:(k + 1) * P], ident[:])
                mm.then_inc(xt_done, 1)

            def keys_queries(c, r):
                pe.wait_ge(xnt_ready, 2 * c + 2)
                for i, (w, h) in enumerate(((1, 0), (1, 1), (0, 0), (0, 1))):
                    if i < 3:
                        wait_count(pe, projc_act, N_PROJ_ACT * c)
                    else:
                        wait_count(pe, projc_dve, c)
                    for k in range(KD):
                        mm = nc.tensor.matmul(ps[2 + i][:], wproj[:, w, k, h * P:(h + 1) * P], xnT[:, r, k, :],
                                              start=(k == 0), stop=(k == KD - 1))
                    mm.then_inc(proj_done, 1)

            def value_rows(c, r, i):
                wait_count(pe, vst_ready, 2 * c)
                for jj in range(2):
                    j = 2 * i + jj
                    for k in range(KD):
                        mm = nc.tensor.matmul(ps[6 + i][:, jj * DM:(jj + 1) * DM],
                                              xnT[:, r, k, j * P:(j + 1) * P], wproj[:, 2, k, :],
                                              start=(k == 0), stop=(k == KD - 1))
                mm.then_inc(vp_done, 1)

            def pooled():
                pe.wait_ge(xnp_ready, 2 * BATCH)
                for w in range(2):
                    for h in range(2):
                        for k in range(KD):
                            mm = nc.tensor.matmul(ps[0][:, (2 * w + h) * P:(2 * w + h + 1) * P],
                                                  wproj[:, w, k, h * P:(h + 1) * P],
                                                  xnp[:, k].rearrange("p b n -> p (b n)"),
                                                  start=(k == 0), stop=(k == KD - 1))
                mm.then_inc(pool_mm, 1)

            def block_scores():
                pe.wait_ge(pooled_ready, 1)
                n = 0
                for h in range(2):
                    for b in range(BATCH):
                        mm = nc.tensor.matmul(ps[1][0:NBLK, 0:NBLK], qkp[:, 0, h, b, :], qkp[:, 1, h, b, :],
                                              start=(n == 0), stop=(n == 7))
                        n += 1
                mm.then_inc(avg_done, 1)

            def project(b, first, last):
                for r in range(2):
                    c = 2 * b + r
                    keys_queries(c, r)
                    if not (last and r == 1):
                        turn_chunk(c + 1, 1 - r)
                    if first and r == 0:
                        turn_maxima(0, ps[6])
                        spread_powers(0, ps[7])
                        pe.wait_ge(wv_scaled, 1)
                    if last and r == 1:
                        pooled()
                    value_rows(c, r, 0)
                    if last and r == 1:
                        block_scores()
                    value_rows(c, r, 1)

            turn_chunk(0, 0)
            project(0, True, False)
            with pe.Fori(1, BATCH - 1) as b:
                project(b, False, False)
            project(BATCH - 1, False, True)

            pe.wait_ge(dve_step, LN_STEPS * 2 * BATCH + 1)
            turn_maxima(1, ps[0])
            spread_powers(1, ps[1])
            pe.wait_ge(scl_ready, 4)

            def scores(hs, m):
                t4, b, h = m // HS, (m % HS) // 2, m % 2
                r = t4 % 2
                for c in range(2):
                    mm = nc.tensor.matmul(Sp[m % 2][:, c, :], Qbd[:, r, h, b, 4 * c:4 * c + 4, :].rearrange("p e n -> p (e n)"),
                                          Ksel[:, r, :, h, b, :], start=True, stop=True)
                mm.then_inc(qk_done, 1)

            def scores_ready(t, g, t4):
                r = t4 % 2
                pe.wait_ge(qbd_ready, t + 1)
                pe.wait_ge(ksel_loaded[r], 96 * (2 * g + t4 // 2) + 96)

            def values(hs, m):
                t4, b, h = m // HS, (m % HS) // 2, m % 2
                w = (2 * t4 + b // 2) % 2
                for c in range(2):
                    q = 2 * h + c
                    for kc in range(2):
                        for pl, vl in PARTS:
                            mm = nc.tensor.matmul(Op[w][:, b % 2, q, :], PT[0:HALFK, m % 2, pl, c, kc, :],
                                                  Vsel[0:HALFK, t4 % 2, kc, b, vl, q * 64:(q + 1) * 64],
                                                  start=(kc == 0 and pl + vl == 0), stop=(kc == 1 and pl == 1))
                mm.then_inc(pv_done, 1)

            def out_steps(g, k, tail=False):
                if k in (4, 5):
                    i = k - 4
                    if i == 0:
                        pe.wait_ge(o_ready, 8 * g + 8)
                    wait_count(pe, lg_ready, 4 * g)
                    for b in (2 * i, 2 * i + 1):
                        for kk in range(KD):
                            mm = nc.tensor.transpose(Mp[i][:, ((b % 2) * 2 + kk) * P:((b % 2) * 2 + kk + 1) * P],
                                                     On[:, b, kk * P:(kk + 1) * P], ident[:])
                    mm.then_inc(ot_done, 1)
                for b in range(BATCH):
                    base, slot = (LAST_BASES[b], b) if tail else (BASES[b], b % 2)
                    M = Mp[slot]
                    if k == base + 1:
                        if isinstance(g, int) and g == 0:
                            pe.wait_ge(wo_scaled, 1)
                        pe.wait_ge(ot_ready, 2 * g + 2)
                        if b >= 2 and not tail:
                            pe.wait_ge(lg_ready, 4 * g + b - 1)
                        for kk in range(KD):
                            mm = nc.tensor.matmul(M[:, 0:DM], OT[:, b, kk, :], wproj[:, 3, kk, :],
                                                  start=(kk == 0), stop=(kk == KD - 1))
                        mm.then_inc(oproj_done, 1)
                    if k == base + 5:
                        pe.wait_ge(xn2_ready, 4 * g + b + 1)
                        for kk in range(KD):
                            mm = nc.tensor.transpose(M[:, 256 + kk * P:256 + (kk + 1) * P], xn2_slot[slot][:, kk * P:(kk + 1) * P],
                                                     ident[:])
                        mm.then_inc(xn2t_done, 1)
                    if k == base + 7:
                        pe.wait_ge(xn2t_ready, 4 * g + b + 1)
                        for kk in range(KD):
                            mm = nc.tensor.matmul(M[:, 0:NE], xn2T_slot[slot][:, kk, :], wgate[:, kk, :],
                                                  start=(kk == 0), stop=(kk == KD - 1))
                        mm.then_inc(lg_done, 1)

            def group(g, first, last):
                if first:
                    scores_ready(0, 0, 0)
                    pe.wait_ge(sel_ready, 1)
                    for m in range(2):
                        scores(m, m)
                for k in range(GHS):
                    hs = GHS * g + k
                    pe.wait_ge(exp_done, hs + 1)
                    if not (first and k < 2):
                        pe.wait_ge(pt_ready, hs - 1)
                    for c in range(2):
                        for kc in range(2):
                            mm = nc.tensor.transpose(PTp[k % 2][0:HALFK, c, kc, :],
                                                     Pr[:, k % 2, c, kc * HALFK:(kc + 1) * HALFK], ident[:])
                    mm.then_inc(pt_done, 1)
                    n = k + 2
                    if not (last and n >= GHS):
                        if n % HS == 0:
                            scores_ready(4 * g + n // HS, g + (1 if n >= GHS else 0), (n // HS) % 4)
                        scores(hs + 2, n % GHS)
                    if not (first and k == 0):
                        m = (k - 1) % GHS
                        if m % 4 == 0 and not (first and k - 1 < 8):
                            pe.wait_ge(o_ready, 8 * g + (k - 1) // 4 - 1)
                        if m % HS == 0:
                            pe.wait_ge(vsel_loaded[(m // HS) % 2], 96 * (2 * g + m // HS // 2) + 96)
                        pe.wait_ge(pt_ready, hs)
                        values(hs - 1, m)
                    if not first:
                        out_steps(g - 1, k)

            group(0, True, False)
            group(1, False, False)
            with pe.Fori(2, GROUPS - 1) as g:
                group(g, False, False)
            group(GROUPS - 1, False, True)
            pe.wait_ge(pt_ready, GROUPS * GHS)
            values(0, GHS - 1)
            for k in range(GHS):
                out_steps(GROUPS - 1, k, tail=True)

            pe.wait_ge(masks_ready, 1)
            mflat = mask.rearrange("p m t e -> p (m t e)")
            nc.tensor.matmul(ps[0][:], tri[:], mflat, start=True, stop=True)
            nc.tensor.matmul(ps[1][:], ones[:], mflat, start=True, stop=True).then_inc(prefix_done, 1)
            n = 0
            for i in range(16):
                pe.wait_ge(ohlo_ready, i + 1)
                pe.wait_ge(ohtok_ready, i + 1)
                for q in range(4):
                    mm = nc.tensor.matmul(ps[6][:, 0:2 * SLOT_TILES], ohlo[:, i % 2, q, :],
                                          ohtok[:, i % 2, q].rearrange("p w n -> p (w n)"),
                                          start=(n == 0), stop=(n == 63))
                    n += 1
                mm.then_inc(oh_used, 1)

            def turn_rows(e, r, half):
                pe.wait_ge(scl_ready, 4 * e + 4)
                for i in (2 * half, 2 * half + 1):
                    if i % 2 == 0:
                        pe.wait_ge(xg_loaded[r][i // 2], 32 * (e - r) + 64)
                    wait_count(pe, xgt_ready, 4 * e + max(i - 1, 0))
                    for s in range(2):
                        for k in range(KD):
                            mm = nc.tensor.transpose(ps[i % 2][:, (2 * k + s) * P:(2 * k + s + 1) * P],
                                                     Xg[:, r, 2 * i + s, k * P:(k + 1) * P], ident[:])
                    mm.then_inc(xgt_done, 1)

            def up(e, r, more):
                pe.wait_ge(wlo_ready, 2 * e + 1)
                pe.wait_ge(xgt_ready, 4 * e + 4)
                for n in range(16):
                    c, f = n // 8, n % 8
                    if not (isinstance(e, int) and e == 0 and n < 4):
                        pe.wait_ge(gelu_done, 16 * e + n - 3)
                    i = 0
                    for k in range(KD):
                        for wl, xl in PARTS:
                            mm = nc.tensor.matmul(ps[2 + n % 4][:], wup[:, r, k, wl, f * P:(f + 1) * P],
                                                  XT[:, r, k, xl, c * 512:(c + 1) * 512],
                                                  start=(i == 0), stop=(i == 3 * KD - 1))
                            i += 1
                    mm.then_inc(up_done, 1)
                    if more and n == 13:
                        turn_maxima(e + 2, ps[0])

            def down(e, r, more):
                pe.wait_ge(wlo_ready, 2 * e + 2)
                for i in range(4):
                    if more and i == 1:
                        spread_powers(e + 2, ps[1])
                    if more and i >= 2:
                        turn_rows(e + 1, 1 - r, i - 2)
                    if i % 2 == 0:
                        pe.wait_ge(h_ready, 16 * e + 4 * i + 8)
                    if not (isinstance(e, int) and e == 0 and i < 2):
                        pe.wait_ge(eo_ready, 4 * e + i - 1)
                    for s in range(2):
                        t = 2 * i + s
                        for f in range(FCH):
                            for hl, wl in PARTS:
                                mm = nc.tensor.matmul(ps[6 + i % 2][:, s * DM:(s + 1) * DM],
                                                      hT[:, t // 4, f, hl, (t % 4) * P:(t % 4 + 1) * P],
                                                      wdn[:, r, f, wl, :],
                                                      start=(f == 0 and hl + wl == 0), stop=(f == FCH - 1 and hl == 1))
                    mm.then_inc(dn_done, 1)

            def expert(e, r, more):
                up(e, r, more)
                down(e, r, more)

            pe.wait_ge(sidx_ready, 1)
            for half in range(2):
                turn_rows(0, 0, half)
            for r in range(2):
                expert(r, r, True)
            with pe.Fori(1, NE // 2 - 1) as u:
                for r in range(2):
                    expert(2 * u + r, r, True)
            for r in range(2):
                expert(NE - 2 + r, r, r == 0)

        @block.vector
        def _(dve):
            steps = [0]

            def carry_dve():
                nc.vector.memset(carrier_v[0:1, :], 0.0)

            def step_wait(base, k):
                dve.wait_ge(dve_step, base + k)

            dve.wait_ge(consts, N_CONSTS)
            WSTAT_STEPS = 13

            def weight_piece(halves, q, size):
                i = size * (q % 4)
                nc.vector.tensor_reduce(wmax[:, q:q + 1], halves[q // 4][:, i:i + size], AX.X, ALU.max,
                                        apply_absolute_value=True).then_inc(wstat_step, 1)

            def weight_maxima(n):
                dve.wait_ge(wstat_step, WSTAT_STEPS * n + 8)
                nc.vector.tensor_reduce(wmax2, wmax.rearrange("p (w q) -> p w q", w=2), AX.X, ALU.max).then_inc(wmax_ready, 1)

            def weight_powers(n, bank):
                dve.wait_ge(wmax_turned, n + 1)
                n = WSTAT_STEPS * n + 8
                nc.vector.tensor_reduce(wpow, bank[0:2, 0:P], AX.X, ALU.max).then_inc(wstat_step, 1)
                dve.wait_ge(wstat_step, n + 1)
                nc.vector.tensor_scalar(wpow, wpow, 1e-18, None, ALU.max).then_inc(wstat_step, 1)
                dve.wait_ge(wstat_step, n + 2)
                bits = wpow.bitcast(U32)
                nc.vector.tensor_scalar(bits, bits, 23, 23, ALU.logical_shift_right, ALU.logical_shift_left)\
                    .then_inc(wstat_step, 1)
                dve.wait_ge(wstat_step, n + 3)
                nc.vector.tensor_scalar(wdiag, ident[0:2, 0:2], wpow, None, ALU.mult).then_inc(wdiag_ready, 1)

            def powers_everywhere(n, bank):
                dve.wait_ge(wpow_spread, n + 1)
                n = WSTAT_STEPS * n + 11
                nc.vector.tensor_copy(wpow_all, bank[:, 0:2]).then_inc(wstat_step, 1)
                dve.wait_ge(wstat_step, n + 1)
                nc.vector.reciprocal(wpow_inv, wpow_all).then_inc(wstat_step, 1)
                dve.wait_ge(wstat_step, n + 2)

            def weight_scales(e, r):
                powers_everywhere(e + 1, ps[1])
                nc.vector.tensor_scalar(scl[:, r, 0:2], wpow_inv, 2.0 ** 7, None, ALU.mult).then_inc(scl_ready, 1)
                nc.vector.tensor_scalar(scl[:, r, 2:3], wpow_inv[:, 0:1], 2.0 ** 6, None, ALU.mult).then_inc(scl_ready, 1)
                nc.vector.tensor_scalar(scl[:, r, 3:4], wpow_all[:, 0:1], 2.0 ** -7, None, ALU.mult).then_inc(scl_ready, 1)
                nc.vector.tensor_scalar(scl[:, r, 4:5], wpow_all[:, 0:1], wpow_all[:, 1:2], 2.0 ** -13, ALU.mult, ALU.mult)\
                    .then_inc(scl_ready, 1)

            def split_low(e, r, halves, w):
                dve.wait_ge(whi_ready, 2 * e + w + 1)
                dve.wait_ge(scl_ready, 4 * e + 4)
                src, dst = (halves[0].rearrange("p (k f) -> p k f", k=KD), wup) if w == 0 else \
                    (halves[1].rearrange("p (f d) -> p f d", f=FCH), wdn)
                nc.vector.scalar_tensor_tensor(dst[:, r, :, 1, :], src, scl[:, r, w:w + 1], dst[:, r, :, 0, :],
                                               ALU.mult, ALU.subtract).then_inc(wlo_ready, 1)

            def scale_wv():
                wv = wproj[:, 2].rearrange("p k n -> p (k n)")
                wo = wproj[:, 3].rearrange("p k n -> p (k n)")
                dve.wait_ge(w_loaded, 16 * 5)
                for q in range(8):
                    weight_piece((wv, wv), q, 128)
                weight_maxima(0)
                weight_powers(0, ps[6])
                powers_everywhere(0, ps[7])
                nc.vector.tensor_scalar(wv, wv, wpow_inv[:, 0:1], 2.0 ** 6, ALU.mult, ALU.mult).then_inc(wv_scaled, 1)
                nc.vector.tensor_scalar(wo, wo, wpow_all[:, 0:1], 2.0 ** -6 / P_SCALE, ALU.mult, ALU.mult).then_inc(wo_scaled, 1)

            def normed(b, r):
                c = 2 * b + r
                dve.wait_ge(x_loaded[r], 16 * b + 16)
                carry_dve()
                for j in range(4):
                    nc.vector.bn_stats(st[:, j, :], x_sb[:, bass.ds(4 * c + j, 1), :].rearrange("p t d -> p (t d)"))\
                        .then_inc(dve_step, 1)
                step_wait(LN_STEPS * c, 4)
                carry_dve()
                for j in range(4):
                    a = nc.vector.bn_aggr(mv[:, j, :], st[:, j, :])
                a.then_inc(stats_ready, 1)
                dve.wait_ge(rstd_ready, c + 1)
                for j in range(4):
                    a = nc.vector.tensor_scalar(xn[:, r, j, :], x_sb[:, bass.ds(4 * c + j, 1), :].rearrange("p t d -> p (t d)"),
                                                mv[:, j, 0:1], rstd[:, j:j + 1], ALU.subtract, ALU.mult)
                a.then_inc(xn_ready, 1)

            def project(b, first, last):
                for r in range(2):
                    c = 2 * b + r
                    if not (last and r == 1):
                        normed(b + r, 1 - r)
                    if first and r == 0:
                        scale_wv()
                    dve.wait_ge(xnt_ready, 2 * c + 2)
                    nc.vector.tensor_reduce(
                        xnp[:, :, bass.ds(b, 1), 16 * r:16 * r + 16].rearrange("p k b n -> p k (b n)"),
                        xnT[:, r].rearrange("p k (n q) -> p k n q", q=BLK), AX.X, ALU.add).then_inc(xnp_ready, 1)
                    dve.wait_ge(proj_done, 4 * c + 4)
                    nc.vector.tensor_copy(QT[:, 1, bass.ds(b, 1), 512 * r:512 * r + 512].rearrange("p b n -> p (b n)"),
                                          ps[5][:]).then_inc(projc_dve, 1)
                    if last and r == 1:
                        dve.wait_ge(pool_mm, 1)
                        nc.vector.tensor_copy(qkp.rearrange("p w h b n -> p (w h b n)"), ps[0][:]).then_inc(pooled_ready, 1)
                    for i in range(2):
                        if last and r == 1 and i == 1:
                            choose_blocks()
                        dve.wait_ge(vhi_ready, 2 * c + i + 1)
                        hi, lo = (vst[:, r, 2 * i:2 * i + 2, l, :] for l in range(2))
                        nc.vector.tensor_tensor(lo, ps[6 + i][:, :].rearrange("p (j d) -> p j d", j=2), hi, ALU.subtract)\
                            .then_inc(vst_ready, 1)

            def choose_blocks():
                s0 = LN_STEPS * 2 * BATCH
                dve.wait_ge(avg_done, 1)
                nc.vector.tensor_copy(avg[:], ps[1][0:NBLK, 0:NBLK]).then_inc(dve_step, 1)
                step_wait(s0, 1)
                nc.vector.max(top8[:], avg[:]).then_inc(dve_step, 1)
                step_wait(s0, 2)
                nc.vector.max_index(idx8[:], top8[:], avg[:]).then_inc(sel_ready, 1)

            normed(0, 0)
            project(0, True, False)
            with dve.Fori(1, BATCH - 1) as b:
                project(b, False, False)
            project(BATCH - 1, False, True)
            s0 = LN_STEPS * 2 * BATCH + 2

            dve.wait_ge(w_staged_first, 32)
            for q in range(8):
                weight_piece(stage_first, q, 512)
            weight_maxima(1)
            weight_powers(1, ps[0])
            weight_scales(0, 0)
            for w in range(2):
                split_low(0, 0, stage_first, w)

            def maxima(hs, r):
                dve.wait_ge(qk_done, hs + 1)
                nc.vector.tensor_reduce(negmax[:, r, :], Sp[r], AX.X, ALU.max, negate=True).then_inc(max_done, 1)

            def turned_low(hs, r):
                dve.wait_ge(pt_high, hs + 1)
                nc.vector.scalar_tensor_tensor(PT[0:HALFK, r, 1], PTp[r][0:HALFK], P_SCALE, PT[0:HALFK, r, 0],
                                               ALU.mult, ALU.subtract).then_inc(pt_ready, 1)

            def norm_out(g, w8, step):
                t4, bp = w8 // 2, w8 % 2
                if step == 0:
                    wait_count(dve, o_ready, 8 * g + w8)
                    nc.vector.reciprocal(rinv[:].rearrange("p b c -> p (b c)"), rsum[:, w8 % 2].rearrange("p b c -> p (b c)"))\
                        .then_inc(dve_recip, 1)
                    dve.wait_ge(dve_recip, 8 * g + w8 + 1)
                    dve.wait_ge(pv_done, GHS * g + 4 * w8 + 4)
                for e in ((0,), (1,), (2, 3))[step]:
                    q = slice(32 * e, 32 * e + 32)
                    a = nc.vector.tensor_tensor(
                        On[32 * t4:32 * t4 + 32, 2 * bp:2 * bp + 2, :].rearrange("p b (c x) -> p (b c) x", c=4)[:, :, HD * e:HD * e + HD],
                        Op[w8 % 2][q].rearrange("p b c d -> p (b c) d")[:, :, HD * e:HD * e + HD],
                        rinv[q].rearrange("p b c -> p (b c)")[:, :, None].to_broadcast([32, 8, HD]), ALU.mult)
                if step == 2:
                    a.then_inc(o_ready, 1)

            def out_steps(g, k, tail=False):
                for b in range(BATCH):
                    base, slot = (LAST_BASES[b], b) if tail else (BASES[b], b % 2)
                    M = Mp[slot]
                    xt = x_sb[:, bass.ds(8 * b + g, 1), :].rearrange("p t d -> p (t d)")
                    s = 2 * (4 * g + b)
                    if k == base + 2:
                        dve.wait_ge(oproj_done, 4 * g + b + 1)
                        nc.vector.tensor_tensor(xt, M[:, 0:DM], xt, ALU.add).then_inc(dve_ln, 1)
                        dve.wait_ge(dve_ln, s + 1)
                        carry_dve()
                        nc.vector.bn_stats(st[:, b, :], xt).then_inc(dve_ln, 1)
                        dve.wait_ge(dve_ln, s + 2)
                        carry_dve()
                        nc.vector.bn_aggr(mv[:, b, :], st[:, b, :]).then_inc(stats_ready, 1)
                    if k == base + 4:
                        dve.wait_ge(rstd_ready, 2 * BATCH + 4 * g + b + 1)
                        if slot < 2:
                            wait_count(dve, xn2_stored[slot], 32 * g + 16 * (b // 2))
                        nc.vector.tensor_scalar(xn2_slot[slot], xt, mv[:, b, 0:1], rstd[:, b:b + 1], ALU.subtract, ALU.mult)\
                            .then_inc(xn2_ready, 1)
                    if k == base + 8:
                        dve.wait_ge(lg_done, 4 * g + b + 1)
                        nc.vector.tensor_copy(L[:, bass.ds(8 * b + g, 1), :].rearrange("p t e -> p (t e)"), M[:, 0:NE])\
                            .then_inc(lg_ready, 1)

            def group(g, first, last):
                if first:
                    for k in range(2):
                        maxima(k, k)
                for k in range(GHS):
                    hs = GHS * g + k
                    if not (last and k + 2 >= GHS):
                        maxima(hs + 2, k % 2)
                    turned_low(hs, k % 2)
                    if k % 4 and not (first and k < 4):
                        if k == 5 and not first:
                            dve.wait_ge(ot_done, 2 * g - 1)
                        if k == 9 and not first:
                            dve.wait_ge(ot_done, 2 * g)
                        w8 = k // 4 - 1
                        if w8 >= 0:
                            norm_out(g, w8, k % 4 - 1)
                        else:
                            norm_out(g - 1, 7, k % 4 - 1)
                    if not first:
                        out_steps(g - 1, k)

            group(0, True, False)
            group(1, False, False)
            with dve.Fori(2, GROUPS - 1) as g:
                group(g, False, False)
            group(GROUPS - 1, False, True)
            for step in range(3):
                norm_out(GROUPS - 1, 7, step)
            for k in range(GHS):
                out_steps(GROUPS - 1, k, tail=True)

            cnt = [s0]

            def link(ins):
                cnt[0] += 1
                ins.then_inc(dve_step, 1)
                dve.wait_ge(dve_step, cnt[0])

            V = nc.vector
            dve.wait_ge(lg_ready, TILES)
            eb = iot[:, None, 0:NE].to_broadcast([P, TILES, NE])

            def per_tile(a):
                return a[:, :, None].to_broadcast([P, TILES, NE])

            dve.wait_ge(y_zeroed, 16 * (NBLK // 2))
            for w in range(2):
                src = L[:] if w == 0 else tmp2[:, 1]
                link(V.tensor_reduce(mx[:, w, :], src, AX.X, ALU.max))
                link(V.tensor_tensor(tmp[:, w], src, per_tile(mx[:, w, :]), ALU.is_equal))
                link(V.tensor_scalar(tmp[:, w], tmp[:, w], -float(NE), float(NE), ALU.mult, ALU.add))
                link(V.tensor_tensor(tmp[:, w], tmp[:, w], eb, ALU.add))
                link(V.tensor_reduce(eidx[:, w, :], tmp[:, w], AX.X, ALU.min))
                link(V.tensor_tensor(mask[:, w], eb, per_tile(eidx[:, w, :]), ALU.is_equal))
                if w == 0:
                    link(V.scalar_tensor_tensor(tmp2[:, 1], mask[:, 0], NEG, L[:], ALU.mult, ALU.add))
            V.drain().then_inc(masks_ready, 1)
            link(V.tensor_tensor(tmp[:, 0], L[:], per_tile(mx[:, 0, :]), ALU.subtract))
            link(V.tensor_tensor(mx[:, 1, :], mx[:, 1, :], mx[:, 0, :], ALU.subtract))
            V.drain().then_inc(ex_in, 1)
            V.memset(seg, 1.0).then_inc(dve_step, 1)
            cnt[0] += 1
            dve.wait_ge(dve_step, cnt[0])
            link(V.memset(seg[:, :, 0:1], 0.0))
            dve.wait_ge(prefix_done, 1)
            tot = ps[1][:, :].rearrange("p (m t e) -> p m e t", m=2, t=TILES)
            link(V.tensor_copy(tmp2.rearrange("p m t e -> p (m t e)").rearrange("p (m e t) -> p m e t", m=2, e=NE), tot))
            totf = tmp2.rearrange("p m t e -> p (m t e)")
            link(V.tensor_tensor_scan(pref.rearrange("p e t -> p (e t)"), seg.rearrange("p e t -> p (e t)"), totf,
                                      0.0, ALU.mult, ALU.add))
            tot1 = pref[:, 0:NE, TILES - 1:TILES]
            link(V.tensor_tensor(seg.rearrange("p e t -> p (e t)"), pref.rearrange("p e t -> p (e t)"), totf, ALU.subtract))
            link(V.tensor_tensor(seg[:, NE:2 * NE, :], seg[:, NE:2 * NE, :], tot1.to_broadcast([P, NE, TILES]), ALU.add))
            link(V.tensor_tensor(tmp2, ps[0][:, :].rearrange("p (m t e) -> p m t e", m=2, t=TILES),
                                 seg.rearrange("p (m e) t -> p m t e", m=2), ALU.add))
            link(V.tensor_tensor(tmp2, tmp2, mask, ALU.mult))
            link(V.tensor_reduce(loc[:], tmp2, AX.X, ALU.add))
            link(V.tensor_scalar(keep[:], loc[:], float(CAP), None, ALU.is_lt))
            link(V.tensor_scalar(loc[:], loc[:], float(CAP - 1), None, ALU.min))
            link(V.scalar_tensor_tensor(fidx[:], eidx[:], float(CAP), loc[:], ALU.mult, ALU.add))
            link(V.tensor_copy(fi32[:], fidx[:]))
            link(V.tensor_scalar(lo_i, fi32[:], P - 1, None, ALU.bitwise_and))
            link(V.tensor_scalar(hi_i, fi32[:], 7, None, ALU.logical_shift_right))
            link(V.tensor_copy(slo, lo_i))
            link(V.tensor_copy(shi, hi_i))
            link(V.tensor_scalar(yk[:, :, :, 0], keep[:], pcol[:, 0:1], None, ALU.mult))
            link(V.tensor_tensor(yk[:, :, :, 1], keep[:], iot[:, 1:1 + 2 * TILES].rearrange("p (m t) -> p m t", m=2), ALU.mult))
            for r in range(2):
                dve.wait_ge(xn2_stored[r], 16 * TILES // 2)
            link(V.tensor_copy(iot16, iot[:]))
            for i in range(16):
                m, t = i // 8, 4 * (i % 8)
                if i >= 2:
                    dve.wait_ge(ohtok_ready, i - 1)
                V.tensor_tensor(ohhi[:, i % 2], iot16[:, None, 0:SLOT_TILES].to_broadcast([P, 4, SLOT_TILES]),
                                shi[:, m, t:t + 4, None].to_broadcast([P, 4, SLOT_TILES]), ALU.is_equal).then_inc(ohhi_ready, 1)
                if i >= 2:
                    dve.wait_ge(oh_used, i - 1)
                V.tensor_tensor(ohlo[:, i % 2], iot16[:, None, :].to_broadcast([P, 4, P]),
                                slo[:, m, t:t + 4, None].to_broadcast([P, 4, P]), ALU.is_equal).then_inc(ohlo_ready, 1)
            dve.wait_ge(oh_used, 16)
            link(V.tensor_copy(tblp, ps[6][:, 0:2 * SLOT_TILES]))
            link(V.scalar_tensor_tensor(tblf, tblp[:, SLOT_TILES:2 * SLOT_TILES], float(P), tblp[:, 0:SLOT_TILES], ALU.mult, ALU.add))
            link(V.tensor_scalar(tblp[:, 0:SLOT_TILES], tblf, float(P + TOK), -float(TOK), ALU.is_ge, ALU.mult))
            link(V.tensor_tensor(tblp[:, 0:SLOT_TILES], tblp[:, 0:SLOT_TILES], tblf, ALU.add))
            link(V.tensor_scalar(tbl[:], tblp[:, 0:SLOT_TILES], -float(P), 0.0, ALU.add, ALU.max))
            for r in range(2):
                V.tensor_copy(sidx[:, r, :], tbl[:, 8 * r:8 * r + 8]).then_inc(sidx_ready, 1)
            link(V.tensor_copy(ytbl[:], tblf))
            for r in range(2):
                V.tensor_copy(yidx[:, r, :], ytbl[:, 8 * r:8 * r + 8]).then_inc(yidx_ready, 1)
            dve.wait_ge(ex_done, 2)
            link(V.tensor_reduce(gt[:, 0, :], ex, AX.X, ALU.add))
            link(V.reciprocal(gt[:, 1, :], gt[:, 0, :]))
            link(V.tensor_tensor(gt[:, 2, :], gt[:, 2, :], gt[:, 1, :], ALU.mult))
            link(V.tensor_tensor(gt[:, 3, :], gt[:, 1, :], gt[:, 2, :], ALU.add))
            link(V.tensor_scalar(gt[:, 3, :], gt[:, 3, :], 1e-9, None, ALU.max))
            link(V.reciprocal(gt[:, 0, :], gt[:, 3, :]))
            link(V.tensor_tensor(gk[:], gt[:, 1:3, :], gt[:, 0:1, :].to_broadcast([P, 2, TILES]), ALU.mult))
            link(V.tensor_tensor(gk[:], gk[:], keep[:], ALU.mult))

            V.drain().then_inc(route_done, 1)

            def rows_in(e, r, half):
                for i in (2 * half, 2 * half + 1):
                    def dst(l):
                        return XT[:, r, :, l, 2 * i * P:(2 * i + 2) * P]
                    src = ps[i % 2][:, :].rearrange("p (k n) -> p k n", k=KD)
                    dve.wait_ge(xgt_done, 4 * e + i + 1)
                    V.tensor_copy(dst(0), src).then_inc(xhi_ready, 1)
                    dve.wait_ge(xhi_ready, 4 * e + i + 1)
                    V.tensor_tensor(dst(1), src, dst(0), ALU.subtract).then_inc(xgt_ready, 1)

            def hidden_low(e, r, more):
                for n in range(16):
                    if more and 2 <= n < 10:
                        if n == 2:
                            dve.wait_ge(w_staged[1 - r], 16 * (e + 1) + 16 * (1 - r))
                        weight_piece(stage[1 - r], n - 2, 512)
                    if more and n == 10:
                        weight_maxima(e + 2)
                    if more and n == 13:
                        weight_powers(e + 2, ps[0])
                    dve.wait_ge(hhi_ready, 16 * e + n + 1)
                    V.scalar_tensor_tensor(hT[:, n // 8, n % 8, 1, :], h32[:, n % 4, :], scl[:, r, 2:3],
                                           hT[:, n // 8, n % 8, 0, :], ALU.mult, ALU.subtract).then_inc(h_ready, 1)

            def next_idx(e, r):
                dve.wait_ge(xgt_done, 4 * e - 4)
                V.tensor_copy(sidx[:, r, :], tbl[:, bass.ds(8 * e, 8)]).then_inc(sidx_ready, 1)

            def eo_out(e, r, i):
                dve.wait_ge(dn_done, 4 * e + i + 1)
                if not (isinstance(e, int) and e == 0):
                    dve.wait_ge(y_scattered[i], 32 * e)
                V.tensor_scalar(eos[:, i].rearrange("p s d -> p (s d)"), ps[6 + i % 2][:], scl[:, r, 4:5], None, ALU.mult)\
                    .then_inc(eo_ready, 1)

            def expert(e, r, more, more2):
                hidden_low(e, r, more)
                if more2:
                    next_idx(e + 2, r)
                if not (isinstance(e, int) and e < 2):
                    for i in range(4):
                        dve.wait_ge(y_scattered[i], 32 * e - 32)
                    V.tensor_copy(yidx[:, r, :], ytbl[:, bass.ds(8 * e, 8)]).then_inc(yidx_ready, 1)
                for i in range(4):
                    eo_out(e, r, i)
                    if more and i == 0:
                        weight_scales(e + 1, 1 - r)
                        for w in range(2):
                            split_low(e + 1, 1 - r, stage[1 - r], w)
                    if more and i in (1, 2):
                        rows_in(e + 1, 1 - r, i - 1)

            for half in range(2):
                rows_in(0, 0, half)
            for r in range(2):
                expert(r, r, True, True)
            with dve.Fori(1, NE // 2 - 1) as u:
                for r in range(2):
                    expert(2 * u + r, r, True, True)
            expert(NE - 2, 0, True, False)
            expert(NE - 1, 1, False, False)

            for i in range(TILES // 4):
                for w in range(2):
                    dve.wait_ge(y_loaded[w][i], 16)
                    for t in range(4 * i, 4 * i + 4):
                        a = V.scalar_tensor_tensor(x_sb[:, t, :], Y[:, w, t, :], gk[:, w, t:t + 1], x_sb[:, t, :],
                                                   ALU.mult, ALU.add)
                        if w == 0:
                            a.then_inc(dve_acc, 1)
                    if w == 0:
                        dve.wait_ge(dve_acc, 4 * i + 4)
                a.then_inc(y_ready, 1)


_INS = ["L0_attn_x", "L0_attn_W_Q", "L0_attn_W_K", "L0_attn_W_V", "L0_attn_W_O", "L0_ffn_wg", "L0_ffn_w_gate", "L0_ffn_w_down"]


def kernel(**inputs):
    import numpy as _np
    import concourse.bacc as _bacc
    from concourse import mybir as _mybir
    from concourse.bass_utils import run_bass_kernel_spmd as _run

    nc = _bacc.Bacc("TRN2", target_bir_lowering=False, num_devices=1)
    arrays, args = {}, []
    for name in _INS:
        a = _np.ascontiguousarray(inputs[name])
        arrays[f"in_{name}_dram"] = a
        args.append(nc.dram_tensor(f"in_{name}_dram", a.shape, _mybir.dt.from_np(a.dtype), kind="ExternalInput").ap())
    args.append(nc.dram_tensor("out_0_dram", (BATCH, SEQ, DM), _mybir.dt.float32, kind="ExternalOutput").ap())
    scratch = [nc.dram_tensor("v_rows", (SEQ, BATCH, 2, DM), _mybir.dt.float16, kind="Internal").ap(),
               nc.dram_tensor("xn2_rows", (TOK, DM), _mybir.dt.float32, kind="Internal").ap(),
               nc.dram_tensor("y_rows", (P + 2 * TOK, DM), _mybir.dt.float32, kind="Internal").ap(),
               nc.dram_tensor("sel_d", (NBLK, 8), _mybir.dt.uint32, kind="Internal").ap()]
    build(nc, *args, scratch)
    r = _run(nc, [arrays], core_ids=[0])
    return r.results[0]["out_0_dram"]
```

```python
from contextlib import ExitStack

import concourse.bass as bass
from concourse import mybir

ALU = mybir.AluOpType
ACT = mybir.ActivationFunctionType
AX = mybir.AxisListType
F32 = mybir.dt.float32
F16 = mybir.dt.float16
I32 = mybir.dt.int32
U32 = mybir.dt.uint32

P = 128
P_SCALE = 2.0 ** 12
N_CONSTS = 8
LN_EPS = 1e-5
BATCH, SEQ, DM = 4, 1024, 256
TOK = BATCH * SEQ
TILES = TOK // P
HEADS, HD = 16, 16
BLK = 32
NBLK = SEQ // BLK
TOPK = int(0.2 * NBLK)
GROUPS = SEQ // P
KEYS = TOPK * BLK
KCH = 2 * KEYS // P
KD = DM // P
NE, FF = 8, 1024
CAP = 2 * TOK // NE
SLOT_TILES = NE * CAP // P
FCH = FF // P
PARTS = ((0, 0), (0, 1), (1, 0))
HS = 8
GHS = 4 * HS
NEG = -3.0e38
Y_RING = 6
Y_LOADS = 2 * TILES // 4


def build(nc, x_d, wq_d, wk_d, wv_d, wo_d, wg_d, up_d, down_d, out_d, scratch):
    v_rows, xn2_rows, y_rows, sel_d = scratch
    with ExitStack() as ctx:
        def sb(name, shape, dt=F32):
            return ctx.enter_context(nc.sbuf_tensor(name, shape, dt))

        def sem(name):
            return ctx.enter_context(nc.semaphore(name))

        x_sb = sb("x_sb", [P, TILES, DM])
        kq = sb("kq", [P, 2 * 8192])
        QT = kq[:, 0:8192].rearrange("p (h b n) -> p h b n", h=2, b=BATCH)
        KT = kq[:, 8192:16384].rearrange("p (k h b n) -> p k h b n", k=NBLK, h=2, b=BATCH)
        Xg = kq[:, 0:4096].rearrange("p (r s d) -> p r s d", r=2, s=8)
        XT = kq[:, 4096:8192].bitcast(F16).rearrange("p (r k l n) -> p r k l n", r=2, k=KD, l=2)
        hT = kq[:, 8192:16384].bitcast(F16).rearrange("p (c f l n) -> p c f l n", c=2, f=FCH, l=2)
        YL = kq[:, 0:8192].rearrange("p (t d) -> p t d", t=TILES)
        gath = sb("gath", [P, 2 * 1536 + 2 * 2048])
        Ksel = gath[:, 0:3072].rearrange("p (r j h b n) -> p r j h b n", r=2, j=TOPK, h=2, b=BATCH)
        Vsel = gath[:, 3072:7168].bitcast(F16).rearrange("p (r i b l y) -> p r i b l y", r=2, i=KCH + 1, b=BATCH, l=2)
        work = sb("work", [P, 2 * 2048 + 2 * 384 + 2 * 512 + 1024 + 1024])
        Qbd = work[:, 0:4096].rearrange("p (r h b e n) -> p r h b e n", r=2, h=2, b=BATCH, e=8)
        Pr = work[:, 4096:4864].rearrange("p (r c n) -> p r c n", r=2, c=2)
        PT = work[:, 4864:5632].bitcast(F16).rearrange("p (r l i n) -> p r l i n", r=2, l=2, i=KCH)
        On = work[:, 5888:6912].rearrange("p (b d) -> p b d", b=BATCH)
        OT = work[:, 6912:7936].rearrange("p (b k n) -> p b k n", b=BATCH, k=KD)
        Y = gath[:, 0:Y_RING * 1024].rearrange("p (r t d) -> p r t d", r=Y_RING, t=4)
        xn = work[:, 0:2048].rearrange("p (r j d) -> p r j d", r=2, j=4)
        xnT = work[:, 2048:4096].bitcast(F16).rearrange("p (r k l n) -> p r k l n", r=2, k=KD, l=2)
        wparts = work[:, 6144:7680].bitcast(F16).rearrange("p (w k l n) -> p w k l n", w=3, k=KD, l=2)
        vst = work[:, 4096:6144].bitcast(F16).rearrange("p (r j c l y) -> p r j c l y", r=2, j=4, c=2, l=2)
        ohlo = work[:, 0:512].bitcast(F16).rearrange("p (r q n) -> p r q n", r=2, q=4)
        ohhi = work[:, 512:768].bitcast(F16).rearrange("p (r q n) -> p r q n", r=2, q=4)
        ohtok = work[:, 768:1280].bitcast(F16).rearrange("p (r q w n) -> p r q w n", r=2, q=4, w=2)
        eos = work[:, 2048:4096].rearrange("p (r s d) -> p r s d", r=4, s=2)
        wgt = sb("wgt", [P, 4 * 2048])
        wup = wgt[:, 0:4096].bitcast(F16).rearrange("p (r k l f) -> p r k l f", r=2, k=KD, l=2)
        wdn = wgt[:, 4096:8192].bitcast(F16).rearrange("p (r f l d) -> p r f l d", r=2, f=FCH, l=2)
        stage = ((gath[:, 4096:6144], work[:, 0:2048]), (gath[:, 0:2048], gath[:, 2048:4096]))
        stage_first = (wgt[:, 2048:4096], wgt[:, 6144:8192])
        h32 = work[:, 4096:6144].rearrange("p (r n) -> p r n", r=4)
        wproj = sb("wproj", [P, 4, KD, DM])
        wgate = sb("wgate", [P, KD, NE])
        ident = sb("ident", [P, P])
        tri = sb("tri", [P, P])
        ones = sb("ones", [P, P])
        hmask = sb("hmask", [P, 8])[:, :]
        iot_i = gath[:, 0:P].bitcast(I32)
        iot = sb("iot", [P, P])
        pcol_i = gath[:, P:P + 1].bitcast(I32)
        pcol = sb("pcol", [P, 1])
        small = sb("small", [P, 768])
        xnp = small[:, 0:256].rearrange("p (k b n) -> p k b n", k=KD, b=BATCH)
        qkp = small[:, 256:768].rearrange("p (w h b n) -> p w h b n", w=2, h=2, b=BATCH)
        zeros = small[:, 0:256]
        slo, shi = (small[:, 64 * i:64 * i + 32].bitcast(F16).rearrange("p (m t) -> p m t", m=2) for i in range(2))
        yk = small[:, 128:192].bitcast(F16).rearrange("p (m t w) -> p m t w", m=2, w=2)
        lo_i, hi_i = (small[:, 256 + 64 * i:320 + 64 * i].bitcast(U32).rearrange("p (m t) -> p m t", m=2) for i in range(2))
        gt = small[:, 384:512].rearrange("p (q t) -> p q t", q=4)
        avg = sb("avg", [NBLK, NBLK])
        top8 = sb("top8", [NBLK, 8])
        idx8 = sb("idx8", [NBLK, 8], U32)
        st = sb("st", [P, 4, 6])
        mv = sb("mv", [P, 4, 2])
        rstd = sb("rstd", [P, 4])
        mhalf = sb("mhalf", [P, 4])
        epst = sb("epst", [P, 4])
        carrier = sb("carrier", [P, 1])
        carrier_v = sb("carrier_v", [P, 1])
        negmax = sb("negmax", [P, 2, 2])
        qk_unscale = sb("qk_unscale", [P, 1])
        rsum = sb("rsum", [P, 2, 2, 4])
        rinv = sb("rinv", [P, 2, 4])
        xn2 = sb("xn2", [P, 2, DM])
        xn2T = sb("xn2T", [P, 2, KD, P])
        xn2_slot = [xn2[:, 0, :], xn2[:, 1, :], work[:, 0:256], work[:, 256:512]]
        xn2T_slot = [xn2T[:, i] for i in range(2)] + \
            [work[:, i:i + 256].rearrange("p (k n) -> p k n", k=KD) for i in (512, 768)]
        L = sb("L", [P, TILES, NE])
        mx = sb("mx", [P, 2, TILES])
        route = gath[:, 4096:7168]
        iot16, tri16, ones16 = (route[:, i:i + 64].bitcast(F16) for i in (264, 328, 392))
        mask = route[:, 0:264].bitcast(F16)[:, 0:NE * (1 + 2 * TILES)].rearrange("p (e n) -> p e n", e=NE)
        tmp, tmp2 = (route[:, 512 * i:512 * i + 512].rearrange("p (m t e) -> p m t e", m=2, t=TILES) for i in (1, 2))
        ex = route[:, 1536:1792].rearrange("p (t e) -> p t e", t=TILES)
        tblf = route[:, 2816:2816 + SLOT_TILES]
        tblp = route[:, 2880:2880 + 2 * SLOT_TILES]
        seg, pref = (route[:, i:i + 512].rearrange("p (e n) -> p e n", e=NE) for i in (1792, 2304))
        eidx = sb("eidx", [P, 2, TILES])
        loc = sb("loc", [P, 2, TILES])
        keep = sb("keep", [P, 2, TILES])
        fidx = sb("fidx", [P, 2, TILES])
        fi32 = sb("fi32", [P, 2, TILES], U32)
        gk = sb("gk", [P, 2, TILES])
        tbl = small[:, 512:576].bitcast(U32)
        ytbl = small[:, 576:640].bitcast(U32)
        glast = small[:, 640:640 + TILES]
        sidx = sb("sidx", [P, 2, 8], U32)
        yidx = sb("yidx", [P, 2, 8], U32)
        wstat = sb("wstat", [P, 32])
        wmax = wstat[:, 0:8]
        wmax2 = wstat[:, 8:10]
        wpow = wstat[0:2, 10:11]
        wdiag = wstat[0:2, 12:14]
        wpow_all, wpow_inv = wstat[:, 14:16], wstat[:, 16:18]
        scl = wstat[:, 20:30].rearrange("p (r n) -> p r n", r=2)

        ps = [ctx.enter_context(nc.psum_tensor(f"ps{i}", [P, 512], F32)) for i in range(8)]
        Sp = [ps[i][:, 0:2 * KEYS].rearrange("p (c n) -> p c n", c=2) for i in (0, 1)]
        PTp = [ps[i][:, 0:KCH * P].rearrange("p (i n) -> p i n", i=KCH) for i in (2, 3)]
        Op = [ps[i][:, :].rearrange("p (b c d) -> p b c d", b=2, c=4) for i in (4, 5)]
        Mp = [ps[i] for i in (6, 7, 0, 1)]

        x_loaded = [sem(f"x_loaded{i}") for i in range(2)]
        w_loaded = sem("w_loaded")
        consts = sem("consts")
        pool_step = sem("pool_step")
        dve_step = sem("dve_step")
        stats_ready = sem("stats_ready")
        vareps_ready = sem("vareps_ready")
        carried = sem("carried")
        rstd_ready = sem("rstd_ready")
        dve_recip = sem("dve_recip")
        dve_ln = sem("dve_ln")
        dve_acc = sem("dve_acc")
        xn_ready = sem("xn_ready")
        xt_done = sem("xt_done")
        xnt_ready = sem("xnt_ready")
        proj_done = sem("proj_done")
        projc_act = sem("projc_act")
        projc_dve = sem("projc_dve")
        vp_done = sem("vp_done")
        w_scaled = sem("w_scaled")
        w_high = sem("w_high")
        w_low = sem("w_low")
        xt_high = sem("xt_high")
        vhi_ready = sem("vhi_ready")
        vst_ready = sem("vst_ready")
        v_stored = [sem(f"v_stored{i}") for i in range(2)]
        xnp_ready = sem("xnp_ready")
        pool_mm = sem("pool_mm")
        pooled_ready = sem("pooled_ready")
        avg_done = sem("avg_done")
        sel_ready = sem("sel_ready")
        sel_stored = sem("sel_stored")
        ksel_loaded = [sem(f"ksel_loaded{i}") for i in range(2)]
        vsel_loaded = [sem(f"vsel_loaded{i}") for i in range(2)]
        qbd_ready = sem("qbd_ready")
        qk_done = sem("qk_done")
        max_done = sem("max_done")
        exp_done = sem("exp_done")
        pt_done = sem("pt_done")
        pt_high = sem("pt_high")
        pt_ready = sem("pt_ready")
        pv_done = sem("pv_done")
        o_ready = sem("o_ready")
        ot_done = sem("ot_done")
        ot_ready = sem("ot_ready")
        oproj_done = sem("oproj_done")
        xn2_ready = sem("xn2_ready")
        xn2_stored = [sem(f"xn2_stored{i}") for i in range(2)]
        xn2t_done = sem("xn2t_done")
        xn2t_ready = sem("xn2t_ready")
        lg_done = sem("lg_done")
        lg_ready = sem("lg_ready")
        ex_in = sem("ex_in")
        ex_done = sem("ex_done")
        masks_ready = sem("masks_ready")
        prefix_done = sem("prefix_done")
        ohlo_ready = sem("ohlo_ready")
        ohtok_ready = sem("ohtok_ready")
        oh_used = sem("oh_used")
        sidx_ready = sem("sidx_ready")
        xg_loaded = [[sem(f"xg_loaded{i}{j}") for j in range(2)] for i in range(2)]
        xgt_done = sem("xgt_done")
        xgt_ready = sem("xgt_ready")
        w_staged_first = sem("w_staged_first")
        w_staged = [sem(f"w_staged{i}") for i in range(2)]
        route_done = sem("route_done")
        wstat_step = sem("wstat_step")
        wmax_ready = sem("wmax_ready")
        wmax_turned = sem("wmax_turned")
        wdiag_ready = sem("wdiag_ready")
        wpow_spread = sem("wpow_spread")
        scl_ready = sem("scl_ready")
        whi_ready = sem("whi_ready")
        wlo_ready = sem("wlo_ready")
        xhi_ready = sem("xhi_ready")
        gelu_done = sem("gelu_done")
        hhi_ready = sem("hhi_ready")
        up_done = sem("up_done")
        h_ready = sem("h_ready")
        dn_done = sem("dn_done")
        eo_ready = sem("eo_ready")
        y_scattered = [sem(f"y_scattered{i}") for i in range(4)]
        yidx_ready = sem("yidx_ready")
        zeros_ready = sem("zeros_ready")
        y_zeroed = sem("y_zeroed")
        ohhi_ready = sem("ohhi_ready")
        y_loaded = [sem(f"y_loaded{i}") for i in range(Y_LOADS)]
        yl_loaded = [sem(f"yl_loaded{i}") for i in range(TILES // 4)]
        y_ready = sem("y_ready")
        out_stored = sem("out_stored")

        x_v = x_d.rearrange("b (t p) d -> p (b t) d", p=P)
        out_v = out_d.rearrange("b (t p) d -> p (b t) d", p=P)
        v_v = v_rows.rearrange("(t p) c b l y -> p t c b (l y)", p=P)
        xn2_v = xn2_rows.rearrange("(t p) d -> p t d", p=P)
        y_v = y_rows.rearrange("(t p) d -> p t d", p=P)
        LN_STEPS = 4
        BASES, LAST_BASES = (6, 11, 16, 21), (6, 7, 8, 9)
        N_PROJ_ACT = 3

        block = ctx.enter_context(nc.Block())

        def wait_count(eng, semaphore, count):
            if not (isinstance(count, int) and count == 0):
                eng.wait_ge(semaphore, count)

        def store_v(eng, b, r):
            eng.wait_ge(vst_ready, 4 * b + 2 * r + 2)
            for c in range(2):
                eng.dma_start(v_v[:, 4 * r:4 * r + 4, c, bass.ds(b, 1), :].rearrange("p t b d -> p t (b d)"),
                             vst[:, r, :, c].rearrange("p j l y -> p j (l y)")).then_inc(v_stored[r], 16)

        @block.sync
        def _(sp):
            for i, w in enumerate((wk_d, wq_d, wv_d, wo_d)):
                if i == 0:
                    sp.dma_start(x_sb[:, 0:4, :], x_v[:, 0:4, :]).then_inc(x_loaded[0], 16)
                slot = (1, 0, 2, 3)[i]
                sp.dma_start(wproj[:, slot], w.rearrange("(k p) n -> p k n", p=P)).then_inc(w_loaded, 16)
                if i == 0:
                    sp.dma_start(x_sb[:, 4:8, :], x_v[:, 4:8, :]).then_inc(x_loaded[1], 16)
            sp.dma_start(wgate[:], wg_d.rearrange("(k p) e -> p k e", p=P)).then_inc(w_loaded, 16)

            def load_expert(e, halves, signal):
                up_half, down_half = halves
                sp.dma_start(up_half.rearrange("p (k f) -> p k f", k=KD),
                             up_d[bass.ds(e, 1)].rearrange("e (k p) f -> p (e k) f", p=P)).then_inc(signal, 16)
                sp.dma_start(down_half.rearrange("p (f d) -> p f d", f=FCH),
                             down_d[bass.ds(e, 1)].rearrange("e (f p) d -> p (e f) d", p=P)).then_inc(signal, 16)

            with sp.Fori(0, BATCH - 1) as b:
                for r in range(2):
                    sp.wait_ge(x_loaded[r], 16 * b + 16)
                    sp.dma_start(x_sb[:, bass.ds(8 * b + 8 + 4 * r, 4), :],
                                 x_v[:, bass.ds(8 * b + 8 + 4 * r, 4), :]).then_inc(x_loaded[r], 16)
                for r in range(2):
                    store_v(sp, b, r)
            load_expert(0, stage_first, w_staged_first)
            store_v(sp, BATCH - 1, 0)
            sp.wait_ge(sel_ready, 1)
            sp.dma_start(sel_d, idx8[:]).then_inc(sel_stored, 16)
            sp.wait_ge(sel_stored, 16)

            def load_chosen(u):
                _, blocks = nc.values_load_multi_w_load_instructions(
                    sel_d.rearrange("(u r) j -> u (r j)", r=2)[bass.ds(u, 1), 0:8 + TOPK],
                    engines=(mybir.EngineType.SP,), min_val=0, max_val=NBLK - 1)
                return blocks[0:TOPK], blocks[8:8 + TOPK]

            def gather(t, r, blocks):
                if not isinstance(t, int):
                    sp.wait_ge(qk_done, HS * t - HS)
                for j, blk in enumerate(blocks):
                    sp.dma_start(Ksel[:, r, j].rearrange("p h b n -> p (h b n)"),
                                 KT[:, bass.ds(blk, 1)].rearrange("p k h b n -> p (k h b n)"))\
                        .then_inc(ksel_loaded[r], 16)
                if isinstance(t, int):
                    for i in range(2):
                        sp.wait_ge(v_stored[i], 32 * BATCH)
                else:
                    sp.wait_ge(pv_done, HS * t - HS)
                for j, blk in enumerate(blocks):
                    for c in range(2):
                        row = c * KEYS + j * BLK
                        sp.dma_start(Vsel[row % P:row % P + BLK, r, row // P + c].rearrange("p b l y -> p (b l y)"),
                                     v_rows[bass.ds(blk * BLK, BLK), c].rearrange("n b l y -> n (b l y)"))\
                            .then_inc(vsel_loaded[r], 16)

            sp.wait_ge(projc_act, N_PROJ_ACT * 2 * BATCH)
            chosen = load_chosen(0)
            for r in range(2):
                gather(r, r, chosen[r])

            with sp.Fori(1, NBLK // 2) as u:
                chosen = load_chosen(u)
                for r in range(2):
                    gather(2 * u + r, r, chosen[r])

            sp.wait_ge(pv_done, HS * NBLK)
            load_expert(1, stage[1], w_staged[1])
            sp.wait_ge(route_done, 1)
            load_expert(2, stage[0], w_staged[0])
            sp.wait_ge(wlo_ready, 4)
            load_expert(3, stage[1], w_staged[1])
            with sp.Fori(2, NE // 2) as u:
                for r in range(2):
                    sp.wait_ge(wlo_ready, 4 * u + 2 * r - 2)
                    load_expert(2 * u + r, stage[r], w_staged[r])
            for s in range(4):
                sp.wait_ge(y_scattered[s], 32 * (NE - 1))
            sp.wait_ge(wlo_ready, 2 * NE)
            for j in range(Y_LOADS):
                if j >= Y_RING:
                    sp.wait_ge(dve_acc, 4 * (j - Y_RING) + 4)
                t = 1 + (j % 2) * TILES + 4 * (j // 2)
                sp.dma_start(Y[:, j % Y_RING], y_v[:, t:t + 4, :]).then_inc(y_loaded[j], 16)
            for s in range(4):
                sp.wait_ge(y_scattered[s], 32 * NE)
            sp.wait_ge(up_done, 16 * NE)
            for i in range(TILES // 4):
                t = 1 + 2 * TILES + 4 * i
                sp.dma_start(YL[:, 4 * i:4 * i + 4, :], y_v[:, t:t + 4, :]).then_inc(yl_loaded[i], 16)
            sp.wait_ge(out_stored, 16 * (TILES // 4))
            for r in range(2):
                sp.wait_ge(xn2_stored[r], 16 * TILES // 2)

        @block.gpsimd
        def _(pool):
            nc.gpsimd.memset(ident[:], 0.0).then_inc(pool_step, 1)
            nc.gpsimd.memset(tri[:], 1.0).then_inc(pool_step, 1)
            nc.gpsimd.memset(hmask, float(HD) ** -0.5).then_inc(pool_step, 1)
            nc.gpsimd.memset(ones[:], 1.0).then_inc(consts, 1)
            nc.gpsimd.memset(mhalf[:], -0.5).then_inc(consts, 1)
            nc.gpsimd.memset(epst[:], LN_EPS).then_inc(consts, 1)
            nc.gpsimd.memset(carrier[:], 0.0).then_inc(carried, 1)
            nc.gpsimd.iota(iot_i, pattern=[[1, P]], base=0, channel_multiplier=0).then_inc(pool_step, 1)
            nc.gpsimd.iota(pcol_i, pattern=[[0, 1]], base=0, channel_multiplier=1).then_inc(pool_step, 1)
            pool.wait_ge(pool_step, 5)
            nc.gpsimd.affine_select(out=ident[:], in_=ident[:], compare_op=ALU.not_equal, fill=1.0, base=0,
                                    pattern=[[-1, P]], channel_multiplier=1).then_inc(consts, 1)
            nc.gpsimd.affine_select(out=tri[:], in_=tri[:], compare_op=ALU.is_ge, fill=0.0, base=-1,
                                    pattern=[[1, P]], channel_multiplier=-1).then_inc(consts, 1)
            nc.gpsimd.affine_select(out=hmask, in_=hmask, compare_op=ALU.is_ge, fill=0.0, base=0,
                                    pattern=[[-HD, 8]], channel_multiplier=1).then_inc(pool_step, 1)
            pool.wait_ge(pool_step, 6)
            nc.gpsimd.affine_select(out=hmask, in_=hmask, compare_op=ALU.is_ge, fill=0.0, base=HD - 1,
                                    pattern=[[HD, 8]], channel_multiplier=-1).then_inc(consts, 1)
            nc.gpsimd.tensor_copy(iot[:], iot_i).then_inc(consts, 1)
            nc.gpsimd.tensor_copy(pcol[:], pcol_i).then_inc(consts, 1)
            pool.wait_ge(consts, N_CONSTS)

            def inv_sqrt(n, var, eps, half, out):
                nc.gpsimd.tensor_tensor(out, var, eps, ALU.add).then_inc(vareps_ready, 1)
                pool.wait_ge(vareps_ready, n + 1)
                nc.gpsimd.tensor_tensor(out, out, half, ALU.pow).then_inc(rstd_ready, 1)

            with pool.Fori(0, 2 * BATCH) as c:
                pool.wait_ge(stats_ready, c + 1)
                inv_sqrt(c, mv[:, :, 1], epst[:], mhalf[:], rstd[:])

            def spread_q(t, r):
                src = QT[:, :, :, bass.ds(t * BLK, BLK)].rearrange("p h b n -> p (h b) n")
                dst = Qbd[:, r].rearrange("p h b e n -> p (h b) e n")
                nc.gpsimd.tensor_tensor(
                    dst, src[:, :, None, :].to_broadcast([P, 8, 8, BLK]),
                    hmask[:, None, :, None].to_broadcast([P, 8, 8, BLK]), ALU.mult).then_inc(qbd_ready, 1)

            pool.wait_ge(pool_mm, 1)
            nc.gpsimd.memset(zeros, 0.0).then_inc(zeros_ready, 1)
            pool.wait_ge(projc_act, N_PROJ_ACT * 2 * BATCH)
            pool.wait_ge(projc_dve, 2 * BATCH)
            pool.wait_ge(vp_done, 4 * BATCH)
            for r in range(2):
                spread_q(r, r)

            def spread_next(t, r):
                pool.wait_ge(qk_done, HS * t - HS)
                spread_q(t, r)

            def rstd_of(n, b):
                pool.wait_ge(stats_ready, 2 * BATCH + n + 1)
                inv_sqrt(2 * BATCH + n, mv[:, b, 1:2], epst[:, 0:1], mhalf[:, 0:1], rstd[:, b:b + 1])

            def group(g, first, last):
                for what, n in (("q", 2), ("r", 0), ("r", 1), ("q", 3), ("r", 2), ("q", 4), ("r", 3), ("q", 5)):
                    if what == "q" and not (last and n >= 4):
                        spread_next(4 * g + n, n % 2)
                    if what == "r" and not first:
                        rstd_of(4 * (g - 1) + n, n)

            group(0, True, False)
            group(1, False, False)
            with pool.Fori(2, GROUPS - 1) as g:
                group(g, False, False)
            group(GROUPS - 1, False, True)
            for b in range(BATCH):
                rstd_of(4 * (GROUPS - 1) + b, b)

            def carry_pool(n):
                pool.wait_ge(carried, n + 1)
                nc.gpsimd.tensor_tensor(carrier[0:1, :], mhalf[0:1, 0:1], epst[0:1, 0:1], ALU.add).then_inc(carried, 1)

            for i in range(16):
                m, t = i // 8, 4 * (i % 8)
                pool.wait_ge(ohhi_ready, i + 1)
                if i >= 2:
                    pool.wait_ge(oh_used, i - 1)
                nc.gpsimd.tensor_tensor(ohtok[:, i % 2], ohhi[:, i % 2, :, None, :].to_broadcast([P, 4, 2, 64]),
                                        yk[:, m, t:t + 4, :, None].to_broadcast([P, 4, 2, 64]),
                                        ALU.mult).then_inc(ohtok_ready, 1)

            def gather_tokens(e, r, n):
                pool.wait_ge(sidx_ready, e + 1)
                carry_pool(n)
                for s in range(8):
                    nc.gpsimd.indirect_dma_start(
                        out=Xg[:, r, s, :], out_offset=None, in_=xn2_rows,
                        in_offset=bass.IndirectOffsetOnAxis(ap=sidx[:, r, s:s + 1], axis=0))\
                        .then_inc(xg_loaded[r][s // 4], 16)

            def scatter_rows(e, r, n):
                pool.wait_ge(yidx_ready, e + 1)
                for i in range(4):
                    pool.wait_ge(eo_ready, 4 * e + i + 1)
                    carry_pool(n + i)
                    for s in range(2):
                        nc.gpsimd.indirect_dma_start(
                            out=y_rows, out_offset=bass.IndirectOffsetOnAxis(ap=yidx[:, r, 2 * i + s:2 * i + s + 1], axis=0),
                            in_=eos[:, i, s, :], in_offset=None).then_inc(y_scattered[i], 16)

            for r in range(2):
                pool.wait_ge(xn2_stored[r], 16 * TILES // 2)
            for r in range(2):
                gather_tokens(r, r, r)
            pool.wait_ge(y_zeroed, 16 * (NBLK // 2))
            with pool.Fori(0, NE // 2 - 1) as u:
                for r in range(2):
                    scatter_rows(2 * u + r, r, 10 * u + 5 * r + 2)
                    gather_tokens(2 * u + r + 2, r, 10 * u + 5 * r + 6)
            for r in range(2):
                scatter_rows(NE - 2 + r, r, 5 * (NE - 2) + 4 * r + 2)

        @block.scalar
        def _(act):
            def rows_turned(c, r):
                act.wait_ge(xt_done, c + 1)
                for k in range(KD):
                    nc.scalar.copy(xnT[:, r, k, 0, :], ps[k][:]).then_inc(xt_high, 1)

            def project(b, last):
                for r in range(2):
                    c = 2 * b + r
                    for h in range(2):
                        act.wait_ge(proj_done, 4 * c + h + 1)
                        nc.scalar.mul(KT[:, 16 * r:16 * r + 16, h, bass.ds(b, 1), :].rearrange("p k b n -> p k (b n)"),
                                      ps[2 + h][:, :].rearrange("p (k n) -> p k n", n=BLK), qk_unscale[:]).then_inc(projc_act, 1)
                    act.wait_ge(proj_done, 4 * c + 3)
                    nc.scalar.mul(QT[:, 0, bass.ds(b, 1), 512 * r:512 * r + 512].rearrange("p b n -> p (b n)"),
                                  ps[4][:], qk_unscale[:]).then_inc(projc_act, 1)
                    if not (last and r == 1):
                        rows_turned(c + 1, 1 - r)
                    wait_count(act, v_stored[r], 32 * b)
                    for i in range(2):
                        act.wait_ge(vp_done, 2 * c + i + 1)
                        nc.scalar.copy(vst[:, r, 2 * i:2 * i + 2, :, 0, :], ps[6 + i][:, :].rearrange("p (j c y) -> p j c y", j=2, c=2))\
                            .then_inc(vhi_ready, 1)

            rows_turned(0, 0)
            for w in range(3):
                act.wait_ge(w_scaled, 1 if w < 2 else 2)
                nc.scalar.copy(wparts[:, w, :, 0, :], wproj[:, w]).then_inc(w_high, 1)
            act.wait_ge(w_scaled, 4)
            project(0, False)
            with act.Fori(1, BATCH - 1) as b:
                project(b, False)
            project(BATCH - 1, True)

            def split_high(e, r, halves):
                act.wait_ge(scl_ready, 4 * e + 4)
                nc.scalar.mul(wup[:, r, :, 0, :], halves[0].rearrange("p (k f) -> p k f", k=KD), scl[:, r, 0:1])\
                    .then_inc(whi_ready, 1)
                nc.scalar.mul(wdn[:, r, :, 0, :], halves[1].rearrange("p (f d) -> p f d", f=FCH), scl[:, r, 1:2])\
                    .then_inc(whi_ready, 1)

            store_v(act, BATCH - 1, 1)
            split_high(0, 0, stage_first)

            def exps(hs, r, b, h, t4):
                w = (2 * t4 + b // 2) % 2
                act.wait_ge(max_done, hs + 1)
                for c in range(2):
                    a = nc.scalar.activation(Pr[:, r, c, :], Sp[r][:, c, :], ACT.Exp, bias=negmax[:, r, c:c + 1],
                                             accum_out=rsum[:, w, b % 2, 2 * h + c:2 * h + c + 1])
                a.then_inc(exp_done, 1)

            def turned_high(hs, r):
                act.wait_ge(pt_done, hs + 1)
                nc.scalar.mul(PT[:, r, 0], PTp[r], P_SCALE).then_inc(pt_high, 1)

            def out_steps(g, k, tail=False):
                if k in (5, 6):
                    i = k - 5
                    act.wait_ge(ot_done, 2 * g + i + 1)
                    nc.scalar.copy(OT[:, 2 * i:2 * i + 2].rearrange("p b k n -> p (b k n)"), Mp[i][:])\
                        .then_inc(ot_ready, 1)
                for b in range(BATCH):
                    base, slot = (LAST_BASES[b], b) if tail else (BASES[b], b % 2)
                    if k == base + 6:
                        act.wait_ge(xn2t_done, 4 * g + b + 1)
                        nc.scalar.copy(xn2T_slot[slot].rearrange("p k n -> p (k n)"), Mp[slot][:, 256:512])\
                            .then_inc(xn2t_ready, 1)
                        act.wait_ge(xn2_ready, 4 * g + b + 1)
                        act.dma_start(xn2_v[:, bass.ds(8 * b + g, 1), :].rearrange("p t d -> p (t d)"), xn2_slot[slot])\
                            .then_inc(xn2_stored[b % 2], 16)

            def group(g, first, last):
                if first:
                    act.wait_ge(w_loaded, 16)
                    for k in range(2):
                        exps(k, k, 0, k, 0)
                for k in range(GHS):
                    hs = GHS * g + k
                    turned_high(hs, k % 2)
                    n = k + 2
                    if not (last and n >= GHS):
                        m = n % GHS
                        if m % 4 == 0 and not (first and n < 8):
                            act.wait_ge(dve_recip, 8 * g + n // 4 - 1)
                        exps(hs + 2, m % 2, (m % HS) // 2, m % 2, m // HS)
                    if not first:
                        out_steps(g - 1, k)
                    if k in ZERO_AT:
                        u = 2 * g + ZERO_AT.index(k)
                        act.dma_start(y_v[:, bass.ds(6 * u + 1, 6), :], zeros[:, None, :].to_broadcast([P, 6, DM]))\
                            .then_inc(y_zeroed, 16)

            ZERO_AT = (7, 23)
            act.wait_ge(zeros_ready, 1)
            for r in range(2):
                act.wait_ge(v_stored[r], 32 * BATCH)
            group(0, True, False)
            group(1, False, False)
            with act.Fori(2, GROUPS - 1) as g:
                group(g, False, False)
            group(GROUPS - 1, False, True)
            for k in range(GHS):
                out_steps(GROUPS - 1, k, tail=True)

            act.wait_ge(ex_in, 1)
            nc.scalar.activation(ex, tmp[:, 0], ACT.Exp).then_inc(ex_done, 1)
            nc.scalar.activation(gt[:, 2, :], mx[:, 1, :], ACT.Exp).then_inc(ex_done, 1)

            def hidden_high(e, r, n):
                act.wait_ge(gelu_done, 16 * e + n + 1)
                nc.scalar.mul(hT[:, n // 8, n % 8, 0, :], h32[:, n % 4, :], scl[:, r, 2:3]).then_inc(hhi_ready, 1)

            def hidden(e, r):
                for n in range(16):
                    act.wait_ge(up_done, 16 * e + n + 1)
                    if not (isinstance(e, int) and e == 0 and n < 4):
                        act.wait_ge(h_ready, 16 * e + n - 3)
                    nc.scalar.activation(h32[:, n % 4, :], ps[2 + n % 4][:], ACT.Gelu, scale=scl[:, r, 3:4]).then_inc(gelu_done, 1)
                    if n:
                        hidden_high(e, r, n - 1)
                hidden_high(e, r, 15)

            hidden(0, 0)
            split_high(1, 1, stage[1])
            with act.Fori(0, NE // 2 - 1) as u:
                for r in range(2):
                    hidden(2 * u + r + 1, 1 - r)
                    split_high(2 * u + r + 2, r, stage[r])
            hidden(NE - 1, 1)

            with act.Fori(0, TILES // 4) as i:
                act.wait_ge(y_ready, i + 1)
                act.dma_start(out_v[:, bass.ds(4 * i, 4), :], x_sb[:, bass.ds(4 * i, 4), :])\
                    .then_inc(out_stored, 16)

        @block.tensor
        def _(pe):
            pe.wait_ge(consts, N_CONSTS)
            pe.wait_ge(w_loaded, 16 * 5)
            def turn_maxima(n, bank):
                pe.wait_ge(wmax_ready, n + 1)
                nc.tensor.transpose(bank[0:2, 0:P], wmax2, ident[:]).then_inc(wmax_turned, 1)

            def spread_powers(n, bank):
                pe.wait_ge(wdiag_ready, n + 1)
                nc.tensor.matmul(bank[:, 0:2], ones[0:2, :], wdiag, start=True, stop=True).then_inc(wpow_spread, 1)

            def turn_chunk(c, r):
                pe.wait_ge(xn_ready, c + 1)
                wait_count(pe, xnp_ready, 2 * c)
                for k in range(KD):
                    for j in range(4):
                        mm = nc.tensor.transpose(ps[k][:, j * P:(j + 1) * P], xn[:, r, j, k * P:(k + 1) * P], ident[:])
                mm.then_inc(xt_done, 1)

            def keys_queries(c, r, steps):
                if 0 in steps:
                    pe.wait_ge(xnt_ready, 2 * c + 2)
                for i in steps:
                    w, h = ((1, 0), (1, 1), (0, 0), (0, 1))[i]
                    if i < 3:
                        wait_count(pe, projc_act, N_PROJ_ACT * c)
                    else:
                        wait_count(pe, projc_dve, c)
                    for k in range(KD):
                        for wl, xl in PARTS:
                            mm = nc.tensor.matmul(ps[2 + i][:], wparts[:, w, k, wl, h * P:(h + 1) * P], xnT[:, r, k, xl, :],
                                                  start=(k == 0 and wl + xl == 0), stop=(k == KD - 1 and wl == 1))
                    mm.then_inc(proj_done, 1)

            def value_rows(c, r, i):
                wait_count(pe, vst_ready, 2 * c)
                for jj in range(2):
                    j = 2 * i + jj
                    for k in range(KD):
                        for xl, wl in PARTS:
                            mm = nc.tensor.matmul(ps[6 + i][:, jj * DM:(jj + 1) * DM],
                                                  xnT[:, r, k, xl, j * P:(j + 1) * P],
                                                  wparts[:, 2, k, wl, :].rearrange("p (h c x) -> p c h x", h=2, c=2),
                                                  start=(k == 0 and xl + wl == 0), stop=(k == KD - 1 and xl == 1))
                mm.then_inc(vp_done, 1)

            def pooled():
                pe.wait_ge(xnp_ready, 4 * BATCH)
                for w in range(2):
                    for h in range(2):
                        for k in range(KD):
                            mm = nc.tensor.matmul(ps[0][:, (2 * w + h) * P:(2 * w + h + 1) * P],
                                                  wproj[:, w, k, h * P:(h + 1) * P],
                                                  xnp[:, k].rearrange("p b n -> p (b n)"),
                                                  start=(k == 0), stop=(k == KD - 1))
                mm.then_inc(pool_mm, 1)

            def block_scores():
                pe.wait_ge(pooled_ready, 1)
                n = 0
                for h in range(2):
                    for b in range(BATCH):
                        mm = nc.tensor.matmul(ps[1][0:NBLK, 0:NBLK], qkp[:, 0, h, b, :], qkp[:, 1, h, b, :],
                                              start=(n == 0), stop=(n == 7))
                        n += 1
                mm.then_inc(avg_done, 1)

            def project(b, first, last):
                for r in range(2):
                    c = 2 * b + r
                    keys_queries(c, r, (0, 1, 2))
                    if not (last and r == 1):
                        turn_chunk(c + 1, 1 - r)
                    else:
                        pooled()
                    keys_queries(c, r, (3,))
                    if first and r == 0:
                        pe.wait_ge(w_low, 3)
                    if last and r == 1:
                        block_scores()
                    value_rows(c, r, 0)
                    value_rows(c, r, 1)

            turn_chunk(0, 0)
            turn_maxima(0, ps[6])
            spread_powers(0, ps[7])
            pe.wait_ge(w_low, 2)
            project(0, True, False)
            with pe.Fori(1, BATCH - 1) as b:
                project(b, False, False)
            project(BATCH - 1, False, True)

            pe.wait_ge(vst_ready, 4 * BATCH)
            turn_maxima(1, ps[6])
            spread_powers(1, ps[7])

            def scores(hs, m):
                t4, b, h = m // HS, (m % HS) // 2, m % 2
                r = t4 % 2
                for c in range(2):
                    mm = nc.tensor.matmul(Sp[m % 2][:, c, :], Qbd[:, r, h, b, 4 * c:4 * c + 4, :].rearrange("p e n -> p (e n)"),
                                          Ksel[:, r, :, h, b, :], start=True, stop=True)
                mm.then_inc(qk_done, 1)

            def scores_ready(t, g, t4):
                r = t4 % 2
                pe.wait_ge(qbd_ready, t + 1)
                pe.wait_ge(ksel_loaded[r], 96 * (2 * g + t4 // 2) + 96)

            def values(hs, m):
                t4, b, h = m // HS, (m % HS) // 2, m % 2
                w = (2 * t4 + b // 2) % 2
                for c in range(2):
                    for i in (c, c + 1):
                        for pl, vl in PARTS:
                            mm = nc.tensor.matmul(Op[w][:, b % 2, 2 * h + c, :], PT[:, m % 2, pl, i, :],
                                                  Vsel[:, t4 % 2, i + c, b, vl, h * 64:(h + 1) * 64],
                                                  start=(i == c and pl + vl == 0), stop=(i == c + 1 and pl == 1))
                mm.then_inc(pv_done, 1)

            def out_steps(g, k, tail=False):
                if k in (4, 5):
                    i = k - 4
                    if i == 0:
                        pe.wait_ge(o_ready, 8 * g + 8)
                    wait_count(pe, lg_ready, 4 * g)
                    for b in (2 * i, 2 * i + 1):
                        for kk in range(KD):
                            mm = nc.tensor.transpose(Mp[i][:, ((b % 2) * 2 + kk) * P:((b % 2) * 2 + kk + 1) * P],
                                                     On[:, b, kk * P:(kk + 1) * P], ident[:])
                    mm.then_inc(ot_done, 1)
                for b in range(BATCH):
                    base, slot = (LAST_BASES[b], b) if tail else (BASES[b], b % 2)
                    M = Mp[slot]
                    if k == base + 1:
                        if isinstance(g, int) and g == 0:
                            pe.wait_ge(w_scaled, 4)
                        pe.wait_ge(ot_ready, 2 * g + 2)
                        if b >= 2 and not tail:
                            pe.wait_ge(lg_ready, 4 * g + b - 1)
                        for kk in range(KD):
                            mm = nc.tensor.matmul(M[:, 0:DM], OT[:, b, kk, :], wproj[:, 3, kk, :],
                                                  start=(kk == 0), stop=(kk == KD - 1))
                        mm.then_inc(oproj_done, 1)
                    if k == base + 5:
                        pe.wait_ge(xn2_ready, 4 * g + b + 1)
                        for kk in range(KD):
                            mm = nc.tensor.transpose(M[:, 256 + kk * P:256 + (kk + 1) * P], xn2_slot[slot][:, kk * P:(kk + 1) * P],
                                                     ident[:])
                        mm.then_inc(xn2t_done, 1)
                    if k == base + 7:
                        pe.wait_ge(xn2t_ready, 4 * g + b + 1)
                        for kk in range(KD):
                            mm = nc.tensor.matmul(M[:, 0:NE], xn2T_slot[slot][:, kk, :], wgate[:, kk, :],
                                                  start=(kk == 0), stop=(kk == KD - 1))
                        mm.then_inc(lg_done, 1)

            def group(g, first, last):
                if first:
                    scores_ready(0, 0, 0)
                    pe.wait_ge(sel_ready, 1)
                    for m in range(2):
                        scores(m, m)
                for k in range(GHS):
                    hs = GHS * g + k
                    pe.wait_ge(exp_done, hs + 1)
                    if not (first and k < 2):
                        pe.wait_ge(pt_ready, hs - 1)
                    probs = Pr[:, k % 2].rearrange("p c n -> p (c n)")
                    for i in range(KCH):
                        mm = nc.tensor.transpose(PTp[k % 2][:, i, :], probs[:, i * P:(i + 1) * P], ident[:])
                    mm.then_inc(pt_done, 1)
                    n = k + 2
                    if not (last and n >= GHS):
                        if n % HS == 0:
                            scores_ready(4 * g + n // HS, g + (1 if n >= GHS else 0), (n // HS) % 4)
                        scores(hs + 2, n % GHS)
                    if not (first and k == 0):
                        m = (k - 1) % GHS
                        if m % 4 == 0 and not (first and k - 1 < 8):
                            pe.wait_ge(o_ready, 8 * g + (k - 1) // 4 - 1)
                        if m % HS == 0:
                            pe.wait_ge(vsel_loaded[(m // HS) % 2], 192 * (2 * g + m // HS // 2) + 192)
                        pe.wait_ge(pt_ready, hs)
                        values(hs - 1, m)
                    if not first:
                        out_steps(g - 1, k)

            group(0, True, False)
            group(1, False, False)
            with pe.Fori(2, GROUPS - 1) as g:
                group(g, False, False)
            group(GROUPS - 1, False, True)
            pe.wait_ge(pt_ready, GROUPS * GHS)
            values(0, GHS - 1)
            for k in range(GHS):
                out_steps(GROUPS - 1, k, tail=True)

            pe.wait_ge(masks_ready, 1)
            nc.tensor.matmul(ps[1][:], ones16, mask[:, :, 0:2 * TILES], start=True, stop=True).then_inc(prefix_done, 1)
            nc.tensor.matmul(ps[0][:], tri16, mask[:, :, 1:1 + 2 * TILES], start=True, stop=True).then_inc(prefix_done, 1)
            n = 0
            for i in range(16):
                pe.wait_ge(ohlo_ready, i + 1)
                pe.wait_ge(ohtok_ready, i + 1)
                for q in range(4):
                    mm = nc.tensor.matmul(ps[6][:, 0:2 * SLOT_TILES], ohlo[:, i % 2, q, :],
                                          ohtok[:, i % 2, q].rearrange("p w n -> p (w n)"),
                                          start=(n == 0), stop=(n == 63))
                    n += 1
                mm.then_inc(oh_used, 1)

            def turn_rows(e, r, half):
                pe.wait_ge(scl_ready, 4 * e + 4)
                for i in (2 * half, 2 * half + 1):
                    if i % 2 == 0:
                        pe.wait_ge(xg_loaded[r][i // 2], 32 * (e - r) + 64)
                    wait_count(pe, xgt_ready, 4 * e + max(i - 1, 0))
                    for s in range(2):
                        for k in range(KD):
                            mm = nc.tensor.transpose(ps[i % 2][:, (2 * k + s) * P:(2 * k + s + 1) * P],
                                                     Xg[:, r, 2 * i + s, k * P:(k + 1) * P], ident[:])
                    mm.then_inc(xgt_done, 1)

            def up(e, r, more):
                pe.wait_ge(wlo_ready, 2 * e + 1)
                for n in range(16):
                    c, f = n // 8, n % 8
                    if f == 0:
                        pe.wait_ge(xgt_ready, 4 * e + 2 * c + 2)
                    if not (isinstance(e, int) and e == 0 and n < 4):
                        pe.wait_ge(gelu_done, 16 * e + n - 3)
                    i = 0
                    for k in range(KD):
                        for wl, xl in PARTS:
                            mm = nc.tensor.matmul(ps[2 + n % 4][:], wup[:, r, k, wl, f * P:(f + 1) * P],
                                                  XT[:, r, k, xl, c * 512:(c + 1) * 512],
                                                  start=(i == 0), stop=(i == 3 * KD - 1))
                            i += 1
                    mm.then_inc(up_done, 1)
                    if n == 6 and isinstance(e, int) and e == 0:
                        turn_rows(0, 0, 1)
                    if more and n == 13:
                        turn_maxima(e + 2, ps[0])

            def down(e, r, more):
                pe.wait_ge(wlo_ready, 2 * e + 2)
                for i in range(4):
                    if more and i == 1:
                        spread_powers(e + 2, ps[1])
                    if more and i >= 2:
                        turn_rows(e + 1, 1 - r, i - 2)
                    if i % 2 == 0:
                        pe.wait_ge(h_ready, 16 * e + 4 * i + 8)
                    if not (isinstance(e, int) and e == 0 and i < 2):
                        pe.wait_ge(eo_ready, 4 * e + i - 1)
                    for s in range(2):
                        t = 2 * i + s
                        for f in range(FCH):
                            for hl, wl in PARTS:
                                mm = nc.tensor.matmul(ps[6 + i % 2][:, s * DM:(s + 1) * DM],
                                                      hT[:, t // 4, f, hl, (t % 4) * P:(t % 4 + 1) * P],
                                                      wdn[:, r, f, wl, :],
                                                      start=(f == 0 and hl + wl == 0), stop=(f == FCH - 1 and hl == 1))
                    mm.then_inc(dn_done, 1)

            def expert(e, r, more):
                up(e, r, more)
                down(e, r, more)

            pe.wait_ge(sidx_ready, 1)
            turn_rows(0, 0, 0)
            for r in range(2):
                expert(r, r, True)
            with pe.Fori(1, NE // 2 - 1) as u:
                for r in range(2):
                    expert(2 * u + r, r, True)
            for r in range(2):
                expert(NE - 2 + r, r, r == 0)

        @block.vector
        def _(dve):
            steps = [0]

            def carry_dve():
                nc.vector.memset(carrier_v[0:1, :], 0.0)

            def step_wait(base, k):
                dve.wait_ge(dve_step, base + k)

            for r in range(2):
                nc.vector.memset(Vsel[P // 2:P, r, 1], 0.0)
                nc.vector.memset(Vsel[0:P // 2, r, 2], 0.0)
            dve.wait_ge(consts, N_CONSTS)
            WSTAT_STEPS = 13

            def weight_piece(halves, q, size):
                i = size * (q % 4)
                nc.vector.tensor_reduce(wmax[:, q:q + 1], halves[q // 4][:, i:i + size], AX.X, ALU.max,
                                        apply_absolute_value=True).then_inc(wstat_step, 1)

            def weight_maxima(n):
                dve.wait_ge(wstat_step, WSTAT_STEPS * n + 8)
                nc.vector.tensor_reduce(wmax2, wmax.rearrange("p (w q) -> p w q", w=2), AX.X, ALU.max).then_inc(wmax_ready, 1)

            def weight_powers(n, bank):
                dve.wait_ge(wmax_turned, n + 1)
                n = WSTAT_STEPS * n + 8
                nc.vector.tensor_reduce(wpow, bank[0:2, 0:P], AX.X, ALU.max).then_inc(wstat_step, 1)
                dve.wait_ge(wstat_step, n + 1)
                nc.vector.tensor_scalar(wpow, wpow, 1e-18, None, ALU.max).then_inc(wstat_step, 1)
                dve.wait_ge(wstat_step, n + 2)
                bits = wpow.bitcast(U32)
                nc.vector.tensor_scalar(bits, bits, 23, 23, ALU.logical_shift_right, ALU.logical_shift_left)\
                    .then_inc(wstat_step, 1)
                dve.wait_ge(wstat_step, n + 3)
                nc.vector.tensor_scalar(wdiag, ident[0:2, 0:2], wpow, None, ALU.mult).then_inc(wdiag_ready, 1)

            def powers_everywhere(n, bank):
                dve.wait_ge(wpow_spread, n + 1)
                n = WSTAT_STEPS * n + 11
                nc.vector.tensor_copy(wpow_all, bank[:, 0:2]).then_inc(wstat_step, 1)
                dve.wait_ge(wstat_step, n + 1)
                nc.vector.reciprocal(wpow_inv, wpow_all).then_inc(wstat_step, 1)
                dve.wait_ge(wstat_step, n + 2)

            def weight_scales(e, r, bank=ps[1]):
                powers_everywhere(e + 1, bank)
                nc.vector.tensor_scalar(scl[:, r, 0:2], wpow_inv, 2.0 ** 7, None, ALU.mult).then_inc(scl_ready, 1)
                nc.vector.tensor_scalar(scl[:, r, 2:3], wpow_inv[:, 0:1], 2.0 ** 6, None, ALU.mult).then_inc(scl_ready, 1)
                nc.vector.tensor_scalar(scl[:, r, 3:4], wpow_all[:, 0:1], 2.0 ** -7, None, ALU.mult).then_inc(scl_ready, 1)
                nc.vector.tensor_scalar(scl[:, r, 4:5], wpow_all[:, 0:1], wpow_all[:, 1:2], 2.0 ** -13, ALU.mult, ALU.mult)\
                    .then_inc(scl_ready, 1)

            def split_low(e, r, halves, w):
                dve.wait_ge(whi_ready, 2 * e + w + 1)
                dve.wait_ge(scl_ready, 4 * e + 4)
                src, dst = (halves[0].rearrange("p (k f) -> p k f", k=KD), wup) if w == 0 else \
                    (halves[1].rearrange("p (f d) -> p f d", f=FCH), wdn)
                nc.vector.scalar_tensor_tensor(dst[:, r, :, 1, :], src, scl[:, r, w:w + 1], dst[:, r, :, 0, :],
                                               ALU.mult, ALU.subtract).then_inc(wlo_ready, 1)

            def scale_projections():
                wqk, wv, wo = (wproj[:, a:b].rearrange("p w k n -> p (w k n)") for a, b in ((0, 2), (2, 3), (3, 4)))
                dve.wait_ge(w_loaded, 16 * 5)
                for q in range(8):
                    weight_piece((wqk, wv), q, 256 if q < 4 else 128)
                weight_maxima(0)
                weight_powers(0, ps[6])
                powers_everywhere(0, ps[7])
                nc.vector.tensor_scalar(wqk, wqk, wpow_inv[:, 0:1], 2.0 ** 6, ALU.mult, ALU.mult).then_inc(w_scaled, 1)
                nc.vector.tensor_scalar(wv, wv, wpow_inv[:, 1:2], 2.0 ** 6, ALU.mult, ALU.mult).then_inc(w_scaled, 1)
                nc.vector.tensor_scalar(wo, wo, wpow_all[:, 1:2], 2.0 ** -6 / P_SCALE, ALU.mult, ALU.mult).then_inc(w_scaled, 1)
                nc.vector.tensor_scalar(qk_unscale[:], wpow_all[:, 0:1], 2.0 ** -6, None, ALU.mult).then_inc(w_scaled, 1)
                dve.wait_ge(w_scaled, 4)
                for w in range(3):
                    dve.wait_ge(w_high, w + 1)
                    nc.vector.tensor_tensor(wparts[:, w, :, 1, :], wproj[:, w], wparts[:, w, :, 0, :], ALU.subtract)\
                        .then_inc(w_low, 1)

            def rows_low(b, r):
                c = 2 * b + r
                for k in range(KD):
                    dve.wait_ge(xt_high, 2 * c + k + 1)
                    nc.vector.tensor_tensor(xnT[:, r, k, 1, :], ps[k][:], xnT[:, r, k, 0, :], ALU.subtract).then_inc(xnt_ready, 1)
                for k in range(KD):
                    nc.vector.tensor_reduce(xnp[:, k, bass.ds(b, 1), 16 * r:16 * r + 16].rearrange("p b n -> p (b n)"),
                                            ps[k][:, :].rearrange("p (n q) -> p n q", q=BLK), AX.X, ALU.add).then_inc(xnp_ready, 1)

            def row_stats(b, r):
                c = 2 * b + r
                dve.wait_ge(x_loaded[r], 16 * b + 16)
                carry_dve()
                for j in range(4):
                    nc.vector.bn_stats(st[:, j, :], x_sb[:, bass.ds(4 * c + j, 1), :].rearrange("p t d -> p (t d)"))\
                        .then_inc(dve_step, 1)
                step_wait(LN_STEPS * c, 4)
                carry_dve()
                for j in range(4):
                    a = nc.vector.bn_aggr(mv[:, j, :], st[:, j, :])
                a.then_inc(stats_ready, 1)

            def norm_rows(b, r):
                c = 2 * b + r
                dve.wait_ge(rstd_ready, c + 1)
                for j in range(4):
                    a = nc.vector.tensor_scalar(xn[:, r, j, :], x_sb[:, bass.ds(4 * c + j, 1), :].rearrange("p t d -> p (t d)"),
                                                mv[:, j, 0:1], rstd[:, j:j + 1], ALU.subtract, ALU.mult)
                a.then_inc(xn_ready, 1)

            def project(b, first, last):
                for r in range(2):
                    c = 2 * b + r
                    if not (last and r == 1):
                        norm_rows(b + r, 1 - r)
                    if not (last and r == 1):
                        rows_low(b + r, 1 - r)
                    if not last:
                        row_stats(b + 1, r)
                    elif r == 1:
                        dve.wait_ge(pool_mm, 1)
                        nc.vector.tensor_copy(qkp.rearrange("p w h b n -> p (w h b n)"), ps[0][:]).then_inc(pooled_ready, 1)
                    dve.wait_ge(proj_done, 4 * c + 4)
                    nc.vector.tensor_scalar(QT[:, 1, bass.ds(b, 1), 512 * r:512 * r + 512].rearrange("p b n -> p (b n)"),
                                            ps[5][:], qk_unscale[:], None, ALU.mult).then_inc(projc_dve, 1)
                    if last and r == 1:
                        choose_blocks()
                        dve.wait_ge(w_staged_first, 32)
                    for i in range(2):
                        if last and r == 1 and i == 0:
                            for q in range(4):
                                weight_piece(stage_first, q, 512)
                        dve.wait_ge(vhi_ready, 2 * c + i + 1)
                        hi, lo = (vst[:, r, 2 * i:2 * i + 2, :, l, :] for l in range(2))
                        nc.vector.tensor_tensor(lo, ps[6 + i][:, :].rearrange("p (j c y) -> p j c y", j=2, c=2), hi, ALU.subtract)\
                            .then_inc(vst_ready, 1)

            def choose_blocks():
                s0 = LN_STEPS * 2 * BATCH
                dve.wait_ge(avg_done, 1)
                nc.vector.tensor_copy(avg[:], ps[1][0:NBLK, 0:NBLK]).then_inc(dve_step, 1)
                step_wait(s0, 1)
                nc.vector.max(top8[:], avg[:]).then_inc(dve_step, 1)
                step_wait(s0, 2)
                nc.vector.max_index(idx8[:], top8[:], avg[:]).then_inc(sel_ready, 1)

            row_stats(0, 0)
            norm_rows(0, 0)
            row_stats(0, 1)
            scale_projections()
            rows_low(0, 0)
            project(0, True, False)
            with dve.Fori(1, BATCH - 1) as b:
                project(b, False, False)
            project(BATCH - 1, False, True)
            for q in range(4, 8):
                weight_piece(stage_first, q, 512)
            weight_maxima(1)
            weight_powers(1, ps[6])
            weight_scales(0, 0, ps[7])
            s0 = LN_STEPS * 2 * BATCH + 2

            for w in range(2):
                split_low(0, 0, stage_first, w)

            def maxima(hs, r):
                dve.wait_ge(qk_done, hs + 1)
                nc.vector.tensor_reduce(negmax[:, r, :], Sp[r], AX.X, ALU.max, negate=True).then_inc(max_done, 1)

            def turned_low(hs, r):
                dve.wait_ge(pt_high, hs + 1)
                nc.vector.scalar_tensor_tensor(PT[:, r, 1], PTp[r], P_SCALE, PT[:, r, 0],
                                               ALU.mult, ALU.subtract).then_inc(pt_ready, 1)

            def norm_out(g, w8, step):
                t4, bp = w8 // 2, w8 % 2
                if step == 0:
                    wait_count(dve, o_ready, 8 * g + w8)
                    nc.vector.reciprocal(rinv[:].rearrange("p b c -> p (b c)"), rsum[:, w8 % 2].rearrange("p b c -> p (b c)"))\
                        .then_inc(dve_recip, 1)
                    dve.wait_ge(dve_recip, 8 * g + w8 + 1)
                    dve.wait_ge(pv_done, GHS * g + 4 * w8 + 4)
                for e in ((0,), (1,), (2, 3))[step]:
                    q = slice(32 * e, 32 * e + 32)
                    a = nc.vector.tensor_tensor(
                        On[32 * t4:32 * t4 + 32, 2 * bp:2 * bp + 2, :].rearrange("p b (c x) -> p (b c) x", c=4)[:, :, HD * e:HD * e + HD],
                        Op[w8 % 2][q].rearrange("p b c d -> p (b c) d")[:, :, HD * e:HD * e + HD],
                        rinv[q].rearrange("p b c -> p (b c)")[:, :, None].to_broadcast([32, 8, HD]), ALU.mult)
                if step == 2:
                    a.then_inc(o_ready, 1)

            def out_steps(g, k, tail=False):
                for b in range(BATCH):
                    base, slot = (LAST_BASES[b], b) if tail else (BASES[b], b % 2)
                    M = Mp[slot]
                    xt = x_sb[:, bass.ds(8 * b + g, 1), :].rearrange("p t d -> p (t d)")
                    s = 2 * (4 * g + b)
                    if k == base + 2:
                        dve.wait_ge(oproj_done, 4 * g + b + 1)
                        nc.vector.tensor_tensor(xt, M[:, 0:DM], xt, ALU.add).then_inc(dve_ln, 1)
                        dve.wait_ge(dve_ln, s + 1)
                        carry_dve()
                        nc.vector.bn_stats(st[:, b, :], xt).then_inc(dve_ln, 1)
                        dve.wait_ge(dve_ln, s + 2)
                        carry_dve()
                        nc.vector.bn_aggr(mv[:, b, :], st[:, b, :]).then_inc(stats_ready, 1)
                    if k == base + 4:
                        dve.wait_ge(rstd_ready, 2 * BATCH + 4 * g + b + 1)
                        if slot < 2:
                            wait_count(dve, xn2_stored[slot], 32 * g + 16 * (b // 2))
                        nc.vector.tensor_scalar(xn2_slot[slot], xt, mv[:, b, 0:1], rstd[:, b:b + 1], ALU.subtract, ALU.mult)\
                            .then_inc(xn2_ready, 1)
                    if k == base + 8:
                        dve.wait_ge(lg_done, 4 * g + b + 1)
                        nc.vector.tensor_copy(L[:, bass.ds(8 * b + g, 1), :].rearrange("p t e -> p (t e)"), M[:, 0:NE])\
                            .then_inc(lg_ready, 1)

            def group(g, first, last):
                if first:
                    for k in range(2):
                        maxima(k, k)
                for k in range(GHS):
                    hs = GHS * g + k
                    if not (last and k + 2 >= GHS):
                        maxima(hs + 2, k % 2)
                    turned_low(hs, k % 2)
                    if k % 4 and not (first and k < 4):
                        if k == 5 and not first:
                            dve.wait_ge(ot_done, 2 * g - 1)
                        if k == 9 and not first:
                            dve.wait_ge(ot_done, 2 * g)
                        w8 = k // 4 - 1
                        if w8 >= 0:
                            norm_out(g, w8, k % 4 - 1)
                        else:
                            norm_out(g - 1, 7, k % 4 - 1)
                    if not first:
                        out_steps(g - 1, k)

            group(0, True, False)
            group(1, False, False)
            with dve.Fori(2, GROUPS - 1) as g:
                group(g, False, False)
            group(GROUPS - 1, False, True)
            for step in range(3):
                norm_out(GROUPS - 1, 7, step)
            V = nc.vector
            V.memset(seg, 1.0).then_inc(dve_step, 1)
            V.memset(mask, 0.0)
            V.tensor_copy(tri16, tri[:])
            V.tensor_copy(ones16, ones[:])
            V.tensor_copy(iot16, iot[:])
            dve.wait_ge(dve_step, s0 + 1)
            V.memset(seg[:, :, 0:1], 0.0).then_inc(dve_step, 1)
            dve.wait_ge(dve_step, s0 + 2)
            s0 += 2
            for k in range(GHS):
                out_steps(GROUPS - 1, k, tail=True)

            cnt = [s0]

            def link(ins):
                cnt[0] += 1
                ins.then_inc(dve_step, 1)
                dve.wait_ge(dve_step, cnt[0])

            dve.wait_ge(lg_ready, TILES)
            eb = iot[:, None, 0:NE].to_broadcast([P, TILES, NE])
            eb_far = iot[:, None, NE:2 * NE].to_broadcast([P, TILES, NE])

            def per_tile(a):
                return a[:, :, None].to_broadcast([P, TILES, NE])

            dve.wait_ge(y_zeroed, 16 * (NBLK // 2))
            for w in range(2):
                src = L[:] if w == 0 else tmp2[:, 1]
                chosen = mask[:, :, 1 + w * TILES:1 + (w + 1) * TILES].rearrange("p e t -> p t e")
                link(V.tensor_reduce(mx[:, w, :], src, AX.X, ALU.max))
                link(V.tensor_tensor(tmp[:, w], src, per_tile(mx[:, w, :]), ALU.is_equal))
                link(V.scalar_tensor_tensor(tmp[:, w], tmp[:, w], -float(NE), eb_far, ALU.mult, ALU.add))
                link(V.tensor_reduce(eidx[:, w, :], tmp[:, w], AX.X, ALU.min))
                link(V.tensor_tensor(chosen, eb, per_tile(eidx[:, w, :]), ALU.is_equal))
                if w == 0:
                    link(V.scalar_tensor_tensor(tmp2[:, 1], chosen, NEG, L[:], ALU.mult, ALU.add))
            V.drain().then_inc(masks_ready, 1)
            link(V.tensor_tensor(tmp[:, 0], L[:], per_tile(mx[:, 0, :]), ALU.subtract))
            link(V.tensor_tensor(mx[:, 1, :], mx[:, 1, :], mx[:, 0, :], ALU.subtract))
            V.drain().then_inc(ex_in, 1)
            dve.wait_ge(prefix_done, 1)
            link(V.tensor_tensor_scan(pref.rearrange("p e n -> p (e n)"), seg.rearrange("p e n -> p (e n)"), ps[1][:],
                                      0.0, ALU.mult, ALU.add))
            dve.wait_ge(prefix_done, 2)
            link(V.tensor_tensor(pref, ps[0][:, :].rearrange("p (e n) -> p e n", e=NE), pref, ALU.add))
            link(V.tensor_tensor(pref, pref, mask[:, :, 1:1 + 2 * TILES], ALU.mult))
            link(V.tensor_reduce(loc[:].rearrange("p m t -> p (m t)"), pref.rearrange("p e n -> p n e"), AX.X, ALU.add))
            link(V.tensor_scalar(keep[:], loc[:], float(CAP), None, ALU.is_lt))
            link(V.tensor_scalar(loc[:], loc[:], float(CAP - 1), None, ALU.min))
            link(V.scalar_tensor_tensor(fidx[:], eidx[:], float(CAP), loc[:], ALU.mult, ALU.add))
            link(V.tensor_copy(fi32[:], fidx[:]))
            link(V.tensor_scalar(lo_i, fi32[:], P - 1, None, ALU.bitwise_and))
            link(V.tensor_scalar(hi_i, fi32[:], 7, None, ALU.logical_shift_right))
            link(V.tensor_copy(slo, lo_i))
            link(V.tensor_copy(shi, hi_i))
            link(V.tensor_scalar(yk[:, :, :, 0], keep[:], pcol[:, 0:1], None, ALU.mult))
            link(V.tensor_tensor(yk[:, :, :, 1], keep[:], iot[:, 1:1 + 2 * TILES].rearrange("p (m t) -> p m t", m=2), ALU.mult))
            for r in range(2):
                dve.wait_ge(xn2_stored[r], 16 * TILES // 2)
            for i in range(16):
                m, t = i // 8, 4 * (i % 8)
                if i >= 2:
                    dve.wait_ge(ohtok_ready, i - 1)
                V.tensor_tensor(ohhi[:, i % 2], iot16[:, None, 0:SLOT_TILES].to_broadcast([P, 4, SLOT_TILES]),
                                shi[:, m, t:t + 4, None].to_broadcast([P, 4, SLOT_TILES]), ALU.is_equal).then_inc(ohhi_ready, 1)
                if i >= 2:
                    dve.wait_ge(oh_used, i - 1)
                V.tensor_tensor(ohlo[:, i % 2], iot16[:, None, :].to_broadcast([P, 4, P]),
                                slo[:, m, t:t + 4, None].to_broadcast([P, 4, P]), ALU.is_equal).then_inc(ohlo_ready, 1)
            dve.wait_ge(oh_used, 16)
            link(V.tensor_copy(tblp, ps[6][:, 0:2 * SLOT_TILES]))
            link(V.scalar_tensor_tensor(tblf, tblp[:, SLOT_TILES:2 * SLOT_TILES], float(P), tblp[:, 0:SLOT_TILES], ALU.mult, ALU.add))
            link(V.tensor_scalar(tblp[:, 0:SLOT_TILES], tblf, float(P + TOK), -float(TOK), ALU.is_ge, ALU.mult))
            link(V.tensor_tensor(tblp[:, 0:SLOT_TILES], tblp[:, 0:SLOT_TILES], tblf, ALU.add))
            link(V.tensor_scalar(tbl[:], tblp[:, 0:SLOT_TILES], -float(P), 0.0, ALU.add, ALU.max))
            for r in range(2):
                V.tensor_copy(sidx[:, r, :], tbl[:, 8 * r:8 * r + 8]).then_inc(sidx_ready, 1)
            last = slice(SLOT_TILES - 8, SLOT_TILES)
            link(V.tensor_scalar(tblp[:, 64:72], tblf[:, last], 0.5, float(P + 2 * TOK), ALU.is_ge, ALU.mult))
            link(V.tensor_scalar(tblp[:, 72:80], tblp[:, last], -float(P), 0.0, ALU.add, ALU.max))
            link(V.tensor_copy(ytbl[:, 0:SLOT_TILES - 8], tblf[:, 0:SLOT_TILES - 8]))
            link(V.tensor_tensor(ytbl[:, last], tblp[:, 64:72], tblp[:, 72:80], ALU.add))
            for r in range(2):
                V.tensor_copy(yidx[:, r, :], ytbl[:, 8 * r:8 * r + 8]).then_inc(yidx_ready, 1)
            dve.wait_ge(ex_done, 2)
            link(V.tensor_reduce(gt[:, 0, :], ex, AX.X, ALU.add))
            link(V.reciprocal(gt[:, 1, :], gt[:, 0, :]))
            link(V.tensor_tensor(gt[:, 2, :], gt[:, 2, :], gt[:, 1, :], ALU.mult))
            link(V.tensor_tensor(gt[:, 3, :], gt[:, 1, :], gt[:, 2, :], ALU.add))
            link(V.tensor_scalar(gt[:, 3, :], gt[:, 3, :], 1e-9, None, ALU.max))
            link(V.reciprocal(gt[:, 0, :], gt[:, 3, :]))
            link(V.tensor_tensor(gk[:], gt[:, 1:3, :], gt[:, 0:1, :].to_broadcast([P, 2, TILES]), ALU.mult))
            link(V.tensor_tensor(gk[:], gk[:], keep[:], ALU.mult))
            link(V.tensor_scalar(keep[:], eidx[:], float(NE - 1), None, ALU.is_equal))
            link(V.tensor_tensor(keep[:], keep[:], gk[:], ALU.mult))
            link(V.tensor_tensor(glast, keep[:, 0, :], keep[:, 1, :], ALU.add))

            V.drain().then_inc(route_done, 1)

            def rows_in(e, r, half):
                for i in (2 * half, 2 * half + 1):
                    def dst(l):
                        return XT[:, r, :, l, 2 * i * P:(2 * i + 2) * P]
                    src = ps[i % 2][:, :].rearrange("p (k n) -> p k n", k=KD)
                    dve.wait_ge(xgt_done, 4 * e + i + 1)
                    V.tensor_copy(dst(0), src).then_inc(xhi_ready, 1)
                    dve.wait_ge(xhi_ready, 4 * e + i + 1)
                    V.tensor_tensor(dst(1), src, dst(0), ALU.subtract).then_inc(xgt_ready, 1)

            def add_rows(q):
                j = q // 4
                w, t = j % 2, 4 * (j // 2) + q % 4
                if q % 4 == 0:
                    dve.wait_ge(y_loaded[j], 16)
                if w == 1:
                    dve.wait_ge(dve_acc, q - 3)
                V.scalar_tensor_tensor(x_sb[:, t, :], Y[:, j % Y_RING, q % 4, :], gk[:, w, t:t + 1], x_sb[:, t, :],
                                       ALU.mult, ALU.add).then_inc(dve_acc, 1)

            def hidden_low(e, r, more):
                for n in range(16):
                    if not more and n >= ADD_FROM:
                        for q in range(2):
                            add_rows(2 * (n - ADD_FROM) + q)
                    if n == 5 and isinstance(e, int) and e == 0:
                        rows_in(0, 0, 1)
                    if more and 2 <= n < 10:
                        if n == 2:
                            dve.wait_ge(w_staged[1 - r], 16 * (e + 1) + 16 * (1 - r))
                        weight_piece(stage[1 - r], n - 2, 512)
                    if more and n == 10:
                        weight_maxima(e + 2)
                    if more and n == 13:
                        weight_powers(e + 2, ps[0])
                    dve.wait_ge(hhi_ready, 16 * e + n + 1)
                    V.scalar_tensor_tensor(hT[:, n // 8, n % 8, 1, :], h32[:, n % 4, :], scl[:, r, 2:3],
                                           hT[:, n // 8, n % 8, 0, :], ALU.mult, ALU.subtract).then_inc(h_ready, 1)

            def next_idx(e, r):
                dve.wait_ge(xgt_done, 4 * e - 4)
                V.tensor_copy(sidx[:, r, :], tbl[:, bass.ds(8 * e, 8)]).then_inc(sidx_ready, 1)

            def eo_out(e, r, i):
                dve.wait_ge(dn_done, 4 * e + i + 1)
                if not (isinstance(e, int) and e == 0):
                    dve.wait_ge(y_scattered[i], 32 * e)
                V.tensor_scalar(eos[:, i].rearrange("p s d -> p (s d)"), ps[6 + i % 2][:], scl[:, r, 4:5], None, ALU.mult)\
                    .then_inc(eo_ready, 1)

            ADD_FROM = 6

            def expert(e, r, more, more2):
                hidden_low(e, r, more)
                if more2:
                    next_idx(e + 2, r)
                if not (isinstance(e, int) and e < 2):
                    for i in range(4):
                        dve.wait_ge(y_scattered[i], 32 * e - 32)
                    V.tensor_copy(yidx[:, r, :], ytbl[:, bass.ds(8 * e, 8)]).then_inc(yidx_ready, 1)
                for i in range(4):
                    if not more:
                        q0 = 2 * (16 - ADD_FROM)
                        for q in range(q0 + (2 * TILES - q0) * i // 4, q0 + (2 * TILES - q0) * (i + 1) // 4):
                            add_rows(q)
                    eo_out(e, r, i)
                    if more and i == 0:
                        weight_scales(e + 1, 1 - r)
                        for w in range(2):
                            split_low(e + 1, 1 - r, stage[1 - r], w)
                    if more and i in (1, 2):
                        rows_in(e + 1, 1 - r, i - 1)

            rows_in(0, 0, 0)
            for r in range(2):
                expert(r, r, True, True)
            with dve.Fori(1, NE // 2 - 1) as u:
                for r in range(2):
                    expert(2 * u + r, r, True, True)
            expert(NE - 2, 0, True, False)
            expert(NE - 1, 1, False, False)

            for i in range(TILES // 4):
                dve.wait_ge(yl_loaded[i], 16)
                dve.wait_ge(dve_acc, 2 * TILES)
                for t in range(4 * i, 4 * i + 4):
                    a = V.scalar_tensor_tensor(x_sb[:, t, :], YL[:, t, :], glast[:, t:t + 1], x_sb[:, t, :],
                                               ALU.mult, ALU.add)
                a.then_inc(y_ready, 1)


_INS = ["L0_attn_x", "L0_attn_W_Q", "L0_attn_W_K", "L0_attn_W_V", "L0_attn_W_O", "L0_ffn_wg", "L0_ffn_w_gate", "L0_ffn_w_down"]


def kernel(**inputs):
    import numpy as _np
    import concourse.bacc as _bacc
    from concourse import mybir as _mybir
    from concourse.bass_utils import run_bass_kernel_spmd as _run

    nc = _bacc.Bacc("TRN2", target_bir_lowering=False, num_devices=1)
    arrays, args = {}, []
    for name in _INS:
        a = _np.ascontiguousarray(inputs[name])
        arrays[f"in_{name}_dram"] = a
        args.append(nc.dram_tensor(f"in_{name}_dram", a.shape, _mybir.dt.from_np(a.dtype), kind="ExternalInput").ap())
    args.append(nc.dram_tensor("out_0_dram", (BATCH, SEQ, DM), _mybir.dt.float32, kind="ExternalOutput").ap())
    scratch = [nc.dram_tensor("v_rows", (SEQ, 2, BATCH, 2, DM // 2), _mybir.dt.float16, kind="Internal").ap(),
               nc.dram_tensor("xn2_rows", (TOK, DM), _mybir.dt.float32, kind="Internal").ap(),
               nc.dram_tensor("y_rows", (P + 3 * TOK, DM), _mybir.dt.float32, kind="Internal").ap(),
               nc.dram_tensor("sel_d", (NBLK, 8), _mybir.dt.uint32, kind="Internal").ap()]
    build(nc, *args, scratch)
    r = _run(nc, [arrays], core_ids=[0])
    return r.results[0]["out_0_dram"]
```
